# Optimizing a Trainium2 kernel written in Bass

```python
import numpy as np
import jax
import jax.numpy as jnp

def _softmax(x, axis=-1):
    return jax.nn.softmax(x, axis=axis)

def _gelu(x):
    return jax.nn.gelu(x, approximate=True)

def _silu(x):
    return jax.nn.silu(x)

def _sigmoid(x):
    return jax.nn.sigmoid(x)

def _layernorm(x, axis=-1, eps=1e-05):
    m = jnp.mean(x, axis=axis, keepdims=True)
    v = jnp.var(x, axis=axis, keepdims=True)
    return (x - m) / jnp.sqrt(v + eps)

def _scatter_add(tgt, idx, src, axis=0):
    return tgt.at[idx].add(src)

def _segment_sum(src, seg, n):
    return jax.ops.segment_sum(src, seg, n)
kernel_name = 'mk_adaln_ffn_d2_seqx_r4_a9613f'

def setup_inputs(seed: int=0):
    np.random.seed(seed)
    _w = jnp.asarray

    def _rec_inputs():
        import jax
        import jax.numpy as jnp
        _rk = jax.random.key(seed)
        x = 0.5 + 0.2887 * jax.random.normal(jax.random.fold_in(_rk, 1), (8, 512, 256), jnp.float32)
        _lenS = 512 - jax.random.randint(jax.random.fold_in(_rk, 7), (8,), 0, max(1, 512 // 4) + 1, jnp.int32)
        _lenS2 = 512 - jax.random.randint(jax.random.fold_in(_rk, 8), (8,), 0, max(1, 512 // 4) + 1, jnp.int32)
        condB_zX = jax.random.uniform(jax.random.fold_in(_rk, 11), (8,), jnp.float32, 0.0, 0.983423)
        condB_zY = jax.random.uniform(jax.random.fold_in(_rk, 12), (8,), jnp.float32, 0.0, 0.979075)
        condB_zR = jax.random.uniform(jax.random.fold_in(_rk, 13), (8,), jnp.float32, 0.0, 0.9968)
        itok_B_0_2 = jax.random.randint(jax.random.fold_in(_rk, 14), (8,), 0, 3, jnp.int32)
        return (x, condB_zX, condB_zY, condB_zR, itok_B_0_2)
    x, condB_zX, condB_zY, condB_zR, itok_B_0_2 = _rec_inputs()

    def _L0_cond_setup():
        import jax, jax.numpy as jnp
        import numpy as np
        key = jax.random.key(seed)
        k1, k2, k3, k4 = jax.random.split(key, 4)
        B, H, W = (64, 256, 256)
        return {'y': jax.random.uniform(k1, (B, H, W), dtype=jnp.float32), 'zX': jax.random.uniform(k2, (B, 1), dtype=jnp.float32), 'zY': jax.random.uniform(k3, (B, 1), dtype=jnp.float32), 'zR': jax.random.uniform(k4, (B, 1), dtype=jnp.float32), 'dx': 1, 'dy': 1}
    _L0_cond_all = _L0_cond_setup()
    _L0_cond_in = {k: v for k, v in _L0_cond_all.items() if k in ()}
    del _L0_cond_all

    def _L0_ffn_setup():
        import jax, jax.numpy as jnp
        import numpy as np
        B, S, H, E, I, K = (2, 512, 256, 8, 256, 2)
        ALPHA, LIMIT = (1.702, 7.0)
        key = jax.random.key(seed)
        ks = jax.random.split(key, 5)
        sc = 0.02
        return {'hidden_states': jax.random.normal(ks[0], (B, S, H), jnp.float32), 'router_weight': jax.random.normal(ks[1], (H, E), jnp.float32) * sc, 'gate_up_proj': jax.random.normal(ks[2], (E, H, 2 * I), jnp.float32) * sc, 'gate_up_proj_bias': jnp.zeros((E, 2 * I), jnp.float32), 'down_proj': jax.random.normal(ks[3], (E, I, H), jnp.float32) * sc, 'down_proj_bias': jnp.zeros((E, H), jnp.float32)}
    _L0_ffn_all = _L0_ffn_setup()
    _L0_ffn_in = {k: v for k, v in _L0_ffn_all.items() if k in ('router_weight', 'gate_up_proj', 'gate_up_proj_bias', 'down_proj', 'down_proj_bias')}
    del _L0_ffn_all

    def _L1_cond_setup():
        import jax, jax.numpy as jnp
        import numpy as np
        NEG_INF = -1e+30
        key = jax.random.key(seed)
        k1, k2, k3, k4, k5 = jax.random.split(key, 5)
        B, S, D, A = (16, 256, 256, 64)
        hidden = jax.random.normal(k1, (B, S, D), dtype=jnp.float32)
        W1 = jax.random.normal(k2, (D, A), dtype=jnp.float32) / np.sqrt(D)
        b1 = jax.random.normal(k3, (A,), dtype=jnp.float32) * 0.01
        v = jax.random.normal(k4, (A,), dtype=jnp.float32) / np.sqrt(A)
        prompt_type_ids = jax.random.randint(k5, (B,), 0, 3, dtype=jnp.int32)
        return {'hidden': hidden, 'W1': W1, 'b1': b1, 'v': v, 'prompt_type_ids': prompt_type_ids}
    _L1_cond_all = _L1_cond_setup()
    _L1_cond_in = {k: v for k, v in _L1_cond_all.items() if k in ('W1', 'b1', 'v')}
    del _L1_cond_all

    def _L1_ffn_setup():
        import jax, jax.numpy as jnp
        import numpy as np
        FEATURES = 256
        D_IN = 256

        def fp8_gemm_optimized(x, input_scale, kernel, kernel_scale):
            s_in = input_scale[0]
            s_k = kernel_scale[0]
            x_q = (x.astype(jnp.float32) / s_in).astype(jnp.float8_e4m3fn)
            k_q = (kernel.astype(jnp.float32) / s_k).astype(jnp.float8_e4m3fn)
            y = jnp.dot(x_q.astype(jnp.float32), k_q.astype(jnp.float32), preferred_element_type=jnp.float32)
            return y * (s_in * s_k)
        key = jax.random.key(seed)
        kx, kk, kb = jax.random.split(key, 3)
        x = jax.random.normal(kx, (4, 2048, D_IN), dtype=jnp.float32)
        limit = np.sqrt(6.0 / (D_IN + FEATURES)).astype(np.float32)
        kernel = jax.random.uniform(kk, (D_IN, FEATURES), dtype=jnp.float32, minval=-limit, maxval=limit).astype(jnp.bfloat16)
        input_scale = jnp.ones((1,), dtype=jnp.float32)
        kernel_scale = jnp.ones((1,), dtype=jnp.float32)
        bias = jnp.zeros((FEATURES,), dtype=jnp.bfloat16)
        return {'x': x, 'kernel': kernel, 'input_scale': input_scale, 'kernel_scale': kernel_scale, 'bias': bias}
    _L1_ffn_all = _L1_ffn_setup()
    _L1_ffn_in = {k: v for k, v in _L1_ffn_all.items() if k in ('kernel', 'input_scale', 'kernel_scale', 'bias')}
    del _L1_ffn_all
    return {'x': x, 'condB_zX': condB_zX, 'condB_zY': condB_zY, 'condB_zR': condB_zR, 'itok_B_0_2': itok_B_0_2, 'L0_ffn_router_weight': _L0_ffn_in['router_weight'], 'L0_ffn_gate_up_proj': _L0_ffn_in['gate_up_proj'], 'L0_ffn_gate_up_proj_bias': _L0_ffn_in['gate_up_proj_bias'], 'L0_ffn_down_proj': _L0_ffn_in['down_proj'], 'L0_ffn_down_proj_bias': _L0_ffn_in['down_proj_bias'], 'L1_cond_W1': _L1_cond_in['W1'], 'L1_cond_b1': _L1_cond_in['b1'], 'L1_cond_v': _L1_cond_in['v'], 'L1_ffn_kernel': _L1_ffn_in['kernel'], 'L1_ffn_input_scale': _L1_ffn_in['input_scale'], 'L1_ffn_kernel_scale': _L1_ffn_in['kernel_scale'], 'L1_ffn_bias': _L1_ffn_in['bias']}

def reference(x, condB_zX, condB_zY, condB_zR, itok_B_0_2, L0_ffn_router_weight, L0_ffn_gate_up_proj, L0_ffn_gate_up_proj_bias, L0_ffn_down_proj, L0_ffn_down_proj_bias, L1_cond_W1, L1_cond_b1, L1_cond_v, L1_ffn_kernel, L1_ffn_input_scale, L1_ffn_kernel_scale, L1_ffn_bias):
    import jax
    import jax.numpy as jnp

    def _L0_cond_ref(y, zX, zY, zR, dx, dy):
        import jax, jax.numpy as jnp
        import numpy as np
        yp_x = jnp.pad(y, ((0, 0), (0, 0), (1, 1)), mode='reflect')
        lap_x = (yp_x[:, :, :-2] - 2.0 * y + yp_x[:, :, 2:]) / (dx * dx)
        yp_y = jnp.pad(y, ((0, 0), (1, 1), (0, 0)), mode='reflect')
        lap_y = (yp_y[:, :-2, :] - 2.0 * y + yp_y[:, 2:, :]) / (dy * dy)
        du_dt = zX[:, :, None] * lap_x + zY[:, :, None] * lap_y + zR[:, :, None] * y * (1.0 - y)
        return du_dt

    def _L0_ffn_ref(hidden_states, router_weight, gate_up_proj, gate_up_proj_bias, down_proj, down_proj_bias):
        import jax, jax.numpy as jnp
        import numpy as np
        B, S, H, E, I, K = (2, 512, 256, 8, 256, 2)
        ALPHA, LIMIT = (1.702, 7.0)
        Bt, St, Ht = hidden_states.shape
        x = hidden_states.reshape(-1, Ht)
        T = x.shape[0]
        logits = x @ router_weight
        top_vals, top_idx = jax.lax.top_k(logits, K)
        scores = jax.nn.softmax(top_vals, axis=-1)
        w = jnp.zeros((T, E), x.dtype).at[jnp.arange(T)[:, None], top_idx].set(scores)
        gu = jnp.einsum('th,ehf->tef', x, gate_up_proj) + gate_up_proj_bias
        gate = gu[..., ::2]
        up = gu[..., 1::2]
        gate = jnp.minimum(gate, LIMIT)
        up = jnp.clip(up, -LIMIT, LIMIT)
        glu = gate * jax.nn.sigmoid(gate * ALPHA)
        act = (up + 1.0) * glu
        down = jnp.einsum('tei,eih->teh', act, down_proj) + down_proj_bias
        out = jnp.einsum('te,teh->th', w, down)
        return out.reshape(Bt, St, Ht)

    def _L1_cond_ref(hidden, W1, b1, v, prompt_type_ids):
        import jax, jax.numpy as jnp
        import numpy as np
        NEG_INF = -1e+30
        B, S, D = hidden.shape
        attn_in = jnp.tanh(jnp.einsum('bsd,da->bsa', hidden, W1) + b1)
        scores = jnp.einsum('bsa,a->bs', attn_in, v)
        idx = jnp.arange(S)
        j = idx[:, None]
        l = idx[None, :]
        prefix_m = l <= j
        postfix_m = l >= j
        cloze_m = l != j
        pt = prompt_type_ids[:, None, None]
        mask = jnp.where(pt == 0, prefix_m[None], jnp.where(pt == 1, postfix_m[None], cloze_m[None]))
        masked_scores = jnp.where(mask, scores[:, None, :], NEG_INF)
        p = jax.nn.softmax(masked_scores, axis=-1)
        cnt = jnp.sum(mask, axis=-1).astype(hidden.dtype)
        pooled = jnp.einsum('bjl,bld->bjd', p, hidden) / cnt[..., None]
        return pooled

    def _L1_ffn_ref(x, kernel, input_scale, kernel_scale, bias):
        import jax, jax.numpy as jnp
        import numpy as np
        FEATURES = 256
        D_IN = 256

        def fp8_gemm_optimized(x, input_scale, kernel, kernel_scale):
            s_in = input_scale[0]
            s_k = kernel_scale[0]
            x_q = (x.astype(jnp.float32) / s_in).astype(jnp.float8_e4m3fn)
            k_q = (kernel.astype(jnp.float32) / s_k).astype(jnp.float8_e4m3fn)
            y = jnp.dot(x_q.astype(jnp.float32), k_q.astype(jnp.float32), preferred_element_type=jnp.float32)
            return y * (s_in * s_k)
        dtype = jnp.bfloat16
        x = x.astype(dtype)
        orig_shape = x.shape
        x2 = x.reshape(-1, x.shape[-1])
        y = fp8_gemm_optimized(x2, input_scale, kernel, kernel_scale)
        y = y.astype(dtype) + bias
        return y.reshape(orig_shape[:-1] + (FEATURES,))
    x = x + _L0_ffn_ref(_L0_cond_ref(x, condB_zX[:, None], condB_zY[:, None], condB_zR[:, None], 1, 1), L0_ffn_router_weight, L0_ffn_gate_up_proj, L0_ffn_gate_up_proj_bias, L0_ffn_down_proj, L0_ffn_down_proj_bias)
    x = x + _L1_ffn_ref(_L1_cond_ref(x, L1_cond_W1, L1_cond_b1, L1_cond_v, itok_B_0_2), L1_ffn_kernel, L1_ffn_input_scale, L1_ffn_kernel_scale, L1_ffn_bias)
    return x

_drawn_inputs = setup_inputs


def setup_inputs(seed=0):
    import zlib

    import numpy as np

    out = dict(_drawn_inputs(seed))
    spreads = {'L0_ffn_gate_up_proj_bias': (0.0, 0.363), 'L0_ffn_down_proj_bias': (0.0, 0.1)}
    factors = {'L1_cond_W1': 8.0, 'L1_cond_b1': 8.0, 'L1_cond_v': 8.0}
    for name, (base, spread) in spreads.items():
        noise = np.random.default_rng([zlib.crc32(name.encode()), seed]).standard_normal(out[name].shape)
        drawn = base * np.exp(spread * noise) if base else spread * noise
        out[name] = jnp.asarray(drawn.astype(out[name].dtype))
    for name, factor in factors.items():
        out[name] = (out[name] * factor).astype(out[name].dtype)
    return out
```

```python
from contextlib import ExitStack

import concourse.bass as bass
from concourse import mybir

ALU = mybir.AluOpType
ACT = mybir.ActivationFunctionType
AX = mybir.AxisListType
F32 = mybir.dt.float32
F32R = mybir.dt.float32r
BF16 = mybir.dt.bfloat16
I32 = mybir.dt.int32
U32 = mybir.dt.uint32

P = 128
ALPHA, LIMIT = 1.702, 7.0
NEG = -1.0e30
EXPONENT_BITS = 0x7F800000
FP8_LEAST_NORMAL = 2.0 ** -6
FP8_GRID = 1.5 * 2.0 ** 20
SLOT_BIG = 1.0e6


def ds(i, n=1):
    return bass.ds(i, n)


def wait_count(eng, semaphore, count):
    if not isinstance(count, int) or count > 0:
        eng.wait_ge(semaphore, count)


def wait_alone(eng, semaphore, count, passed, passed_count):
    eng.wait_ge(passed, passed_count)
    eng.wait_ge(semaphore, count)


def steps(eng, count, unroll, step):
    for s in range(unroll):
        step(s, s, 0)
    with eng.Fori(1, count // unroll) as k:
        for s in range(unroll):
            step(k * unroll + s, s, k)


def earlier(n, s, k, back, unroll):
    if isinstance(n, int) and n < back:
        return None
    return n - back, (s - back) % unroll, k - (1 if s < back else 0)


def adaln_ffn_kernel(nc, x, zx, zy, zr, kinds, router_w, gate_up_w, gate_up_b, down_w, down_b,
                     w1, b1, v, ffn_k, in_scale, k_scale, ffn_b, out):
    B, S, H = x.shape
    E = router_w.shape[1]
    I = down_w.shape[1]
    A = w1.shape[1]
    F = ffn_k.shape[1]
    GU = 2 * I
    TB = S // P
    NT = B * TB
    KH, KI = H // P, I // P
    assert B == E and H == I == F == 256 and TB == 4 and B % 2 == 0

    UNROLL = 4
    MOST = (2 * B * S - E) // P + E
    NB = -(-MOST // UNROLL) * UNROLL
    SURE = 2 * B * S // P
    MW = 2 * S - P

    x_v = x.rearrange("b (t p) h -> b p t h", p=P)
    out_v = out.rearrange("b (t p) h -> b p t h", p=P)
    gate_up_v = gate_up_w.rearrange("e (k p) f -> e p k f", p=P)
    down_v = down_w.rearrange("e (k p) h -> e p k h", p=P)

    slot_rows = nc.dram_tensor("slot_rows", [NB * P, H], F32).ap()
    slot_outs = nc.dram_tensor("slot_outs", [NB * P, H], F32).ap()
    score_rows = nc.dram_tensor("score_rows", [B, S], F32).ap()
    max_rows = nc.dram_tensor("max_rows", [B, S], F32).ap()

    with ExitStack() as ctx:
        def sem(name):
            return ctx.enter_context(nc.semaphore(name))

        def memory(scope):
            return lambda name, shape, dt=F32: scope.enter_context(nc.sbuf_tensor(name, shape, dt))

        bank = [ctx.enter_context(nc.psum_tensor(f"bank{i}", [P, 512], F32)) for i in range(8)]

        sb = memory(ctx)
        U = sb("U", [P, NT, H + 1])
        tok_w = sb("tok_w", [P, 2, NT])
        slot_of = sb("slot_of", [P, 2, NT], U32)
        ident = sb("ident", [P, P])

        with ExitStack() as ab:
            sb = memory(ab)
            gu_hi = sb("gu_hi", [P, E, KH, GU], F32R)
            gu_lo = sb("gu_lo", [P, E, KH, GU], F32R)
            dn_hi = sb("dn_hi", [P, E, KI, H], F32R)
            dn_lo = sb("dn_lo", [P, E, KI, H], F32R)
            gu_bias = sb("gu_bias", [2, E, GU], F32R)
            dn_bias = sb("dn_bias", [2, E, H], F32R)
            ones2 = sb("ones2", [2, P], F32R)
            block_expert = sb("block_expert", [1, NB], I32)
            with ExitStack() as a:
                sb = memory(a)
                xb = sb("xb", [P, 2, TB, H])
                halo = sb("halo", [2, 2, TB, H])
                flow = sb("flow", [P, 2, TB, H])
                uT = sb("uT", [P, KH, TB, P])
                raw_gu = sb("raw_gu", [P, KH, GU])
                raw_dn = sb("raw_dn", [P, KI, H])
                raw_b = sb("raw_b", [2, GU + H])
                row_sel = sb("row_sel", [2, 2])
                diff = sb("diff", [P, P])
                edge = sb("edge", [2, P])
                above = sb("above", [P, P], BF16)
                ones_b = sb("ones_b", [P, P], BF16)
                zs = sb("zs", [P, 5, B])
                router_sb = sb("router_sb", [P, KH, E])
                logits = sb("logits", [P, TB, E])
                best = sb("best", [P, TB, 8])
                best_i = sb("best_i", [P, TB, 8], U32)
                top = sb("top", [P, NT, 2])
                top_i = sb("top_i", [P, NT, 2])
                expert_i = sb("expert_i", [P, E], I32)
                expert_f = sb("expert_f", [P, E])
                pick = sb("pick", [P, 2, E, NT])
                picked = sb("picked", [P, E, NT], BF16)
                follow = sb("follow", [P, E, NT])
                totals = sb("totals", [P, E, NT])
                upto = sb("upto", [P, E, NT])
                ends = sb("ends", [P, 6, E])
                ends_i = sb("ends_i", [P, 2, E], I32)
                row_i = sb("row_i", [P, 1], I32)
                row_f = sb("row_f", [P, 1])
                pad_slot = sb("pad_slot", [P, E], U32)
                slot_f = sb("slot_f", [P, 2, NT])
                odds = sb("odds", [P, 3, NT])
                zero_rows = sb("zero_rows", [P, H])
                blk_i = sb("blk_i", [1, NB], I32)
                blk_f = sb("blk_f", [1, NB])
                blk_past = sb("blk_past", [1, NB, E])
                blk_e = sb("blk_e", [1, NB])
            with ExitStack() as b_:
                sb = memory(b_)
                rows = sb("rows", [P, UNROLL, H])
                rowT_hi = sb("rowT_hi", [P, 2, KH, P], F32R)
                rowT_lo = sb("rowT_lo", [P, 2, KH, P], F32R)
                gate = sb("gate", [P, 2, I])
                up = sb("up", [P, 2, I])
                tanh = sb("tanh", [P, 2, I])
                glu = sb("glu", [P, 2, I])
                act = sb("act", [P, 2, I])
                actT_hi = sb("actT_hi", [P, 2, KI, P], F32R)
                actT_lo = sb("actT_lo", [P, 2, KI, P], F32R)
                outs = sb("outs", [P, UNROLL, H])

        sb = memory(ctx)
        picks = sb("picks", [P, 2, 2, TB, H])
        mix = sb("mix", [P, 2, TB, H])
        xT = sb("xT", [P, KH, S])
        hidden = sb("hidden", [A, S])
        score_row = sb("score_row", [1, 2, S])
        score_col = sb("score_col", [P, TB, B])
        scores = sb("scores", [B, S])
        from_left = sb("from_left", [B, S])
        from_right = sb("from_right", [B, S])
        around = sb("around", [B, S])
        row_max = sb("row_max", [B, S])
        kind_of = sb("kind_of", [B, 6])
        kind_i = sb("kind_i", [B, 1], I32)
        kind_row = sb("kind_row", [1, 4, B])
        kind_row_i = sb("kind_row_i", [1, 2, B], I32)
        masks = sb("masks", [P, 3, MW])
        counts = sb("counts", [P, 3, TB])
        counts_i = sb("counts_i", [P, TB], I32)
        w1_sb = sb("w1_sb", [P, KH, A])
        b1_sb = sb("b1_sb", [A, 1])
        v_sb = sb("v_sb", [A, 1])
        neg_max = sb("neg_max", [P, 2, S])
        expo = sb("expo", [P, 2, S])
        probs = sb("probs", [P, TB, S])
        norm = sb("norm", [P, TB])
        pooled = sb("pooled", [P, TB, H], BF16)
        scaled = sb("scaled", [P, TB, H])
        grid = sb("grid", [P, TB, H])
        quant = sb("quant", [P, TB, H], BF16)
        quantT = sb("quantT", [P, KH, S], BF16)
        ident_b = sb("ident_b", [P, P], BF16)
        k_raw = sb("k_raw", [P, KH, F], BF16)
        k_scaled = sb("k_scaled", [P, KH, F])
        k_grid = sb("k_grid", [P, KH, F])
        k_quant = sb("k_quant", [P, KH, F], BF16)
        scales = sb("scales", [P, 5])
        bias_f = sb("bias_f", [P, F], BF16)
        ffn = sb("ffn", [P, TB, F], BF16)
        ffn_sum = sb("ffn_sum", [P, TB, F], BF16)
        result = sb("result", [P, 2, TB, H])

        pool_const = sem("pool_const")
        diff_step = sem("diff_step")
        z_loaded = sem("z_loaded")
        router_loaded = sem("router_loaded")
        z_step = sem("z_step")
        x_loaded = [sem(f"x_loaded{i}") for i in range(2)]
        w_loaded = sem("w_loaded")
        lap_ready = sem("lap_ready")
        slope_ready = sem("slope_ready")
        react_ready = sem("react_ready")
        flow_step = sem("flow_step")
        u_ready = sem("u_ready")
        u_kept = [sem(f"u_kept{i}") for i in range(2)]
        uT_psum = sem("uT_psum")
        uT_ready = sem("uT_ready")
        logits_psum = sem("logits_psum")
        logits_ready = sem("logits_ready")
        best_step = sem("best_step")
        index_step = sem("index_step")
        top_ready = sem("top_ready")
        hi_ready = sem("hi_ready")
        raw_used = sem("raw_used")
        bias_plus = sem("bias_plus")
        bias_hi = sem("bias_hi")
        bias_step = sem("bias_step")
        route_step = sem("route_step")
        picked_ready = sem("picked_ready")
        ranks_ready = sem("ranks_ready")
        gap_ready = sem("gap_ready")
        odds_ready = sem("odds_ready")
        slots_ready = sem("slots_ready")
        experts_ready = sem("experts_ready")
        tail_zeroed = sem("tail_zeroed")
        scattered = sem("scattered")
        rows_loaded = [sem(f"rows_loaded{i}") for i in range(UNROLL)]
        rowT_psum = sem("rowT_psum")
        rowT_hi_ready = sem("rowT_hi_ready")
        rowT_lo_ready = sem("rowT_lo_ready")
        gu_psum = sem("gu_psum")
        gate_ready = sem("gate_ready")
        up_ready = sem("up_ready")
        tanh_ready = sem("tanh_ready")
        glu_ready = sem("glu_ready")
        act_ready = sem("act_ready")
        actT_psum = sem("actT_psum")
        actT_hi_ready = sem("actT_hi_ready")
        actT_lo_ready = sem("actT_lo_ready")
        down_psum = sem("down_psum")
        outs_ready = sem("outs_ready")
        outs_stored = [sem(f"outs_stored{i}") for i in range(UNROLL)]
        c_loaded = sem("c_loaded")
        x_again = [sem(f"x_again{i}") for i in range(2)]
        gathered = [sem(f"gathered{i}") for i in range(2)]
        mix_step = sem("mix_step")
        mixed = sem("mixed")
        mixed_kept = [sem(f"mixed_kept{i}") for i in range(2)]
        xT_psum = sem("xT_psum")
        xT_ready = sem("xT_ready")
        hidden_psum = sem("hidden_psum")
        hidden_ready = sem("hidden_ready")
        score_psum = sem("score_psum")
        row_ready = sem("row_ready")
        col_ready = sem("col_ready")
        row_stored = [sem(f"row_stored{i}") for i in range(2)]
        scores_loaded = sem("scores_loaded")
        tables = sem("tables")
        table_step = sem("table_step")
        max_step = sem("max_step")
        max_ready = sem("max_ready")
        max_stored = sem("max_stored")
        max_loaded = [sem(f"max_loaded{i}") for i in range(2)]
        expo_ready = sem("expo_ready")
        probs_ready = sem("probs_ready")
        pool_psum = sem("pool_psum")
        norm_ready = sem("norm_ready")
        pooled_ready = sem("pooled_ready")
        scaled_ready = sem("scaled_ready")
        bits_ready = sem("bits_ready")
        grid_ready = sem("grid_ready")
        lifted = sem("lifted")
        quant_ready = sem("quant_ready")
        quantT_psum = sem("quantT_psum")
        quantT_ready = sem("quantT_ready")
        ffn_psum = sem("ffn_psum")
        ffn_ready = sem("ffn_ready")
        ffn_sum_ready = sem("ffn_sum_ready")
        result_ready = sem("result_ready")
        result_stored = [sem(f"result_stored{i}") for i in range(2)]

        ZX, ZY, ZR, ZRN, SLOPE = range(5)
        lap = [bank[0], bank[1]]
        uT_bank = [bank[2], bank[3]]
        logit_bank = bank[4][:, 0:TB * E].rearrange("p (t e) -> p t e", e=E)
        rank_bank = bank[5][:, 0:E * NT].rearrange("p (e t) -> p e t", t=NT)
        total_bank = bank[6][:, 0:E * NT].rearrange("p (e t) -> p e t", t=NT)
        X_DMAS, W_DMAS = 5, 6
        N_CONST_A = 12
        C_DMAS = 9
        SCATTERS = 2 * NT + E
        BEST = TB

        block = ctx.enter_context(nc.Block())

        @block.sync
        def _(sp):
            for i, z in enumerate((zx, zy, zr)):
                sp.dma_start(zs[:, i, :], z.partition_broadcast(P)).then_inc(z_loaded, 16)
            sp.dma_start(router_sb[:], router_w.rearrange("(k p) e -> p k e", p=P)).then_inc(router_loaded, 16)

            def load(n, s, k):
                wait_count(sp, u_ready, n - 1)
                sp.dma_start(xb[:, s], x_v[ds(n)].rearrange("b p t h -> (b p) t h")).then_inc(x_loaded[s], 16)
                for row, tiles, first in ((0, slice(0, 1), 1), (0, slice(1, TB), P - 1),
                                          (1, slice(0, TB - 1), P), (1, slice(TB - 1, TB), S - 2)):
                    count = tiles.stop - tiles.start
                    sp.dma_start(halo[row:row + 1, s, tiles, :],
                                 x[ds(n), first:first + 1 + P * (count - 1):P, :]).then_inc(x_loaded[s], 16)
                wait_count(sp, raw_used, 4 * n)
                sp.dma_start(raw_gu[:], gate_up_v[ds(n)].rearrange("e p k f -> (e p) k f")).then_inc(w_loaded, 16)
                sp.dma_start(raw_dn[:], down_v[ds(n)].rearrange("e p k h -> (e p) k h")).then_inc(w_loaded, 16)
                for r in range(2):
                    sp.dma_start(raw_b[r:r + 1, 0:GU], gate_up_b[ds(n), :]).then_inc(w_loaded, 16)
                    sp.dma_start(raw_b[r:r + 1, GU:], down_b[ds(n), :]).then_inc(w_loaded, 16)
                if (last := earlier(n, s, k, 1, 2)) is not None:
                    keep_u(*last)

            def keep_u(n, s, k):
                sp.wait_ge(u_ready, n + 1)
                sp.dma_start(U[:, ds(n * TB, TB), 0:H], flow[:, s]).then_inc(u_kept[s], 16)

            steps(sp, B, 2, load)
            keep_u(B - 1, 1, 0)
            sp.wait_ge(pool_const, N_CONST_A)
            for n in range(SURE, NB):
                sp.dma_start(slot_rows[n * P:(n + 1) * P, :], zero_rows[:]).then_inc(tail_zeroed, 16)

            sp.wait_ge(scattered, 16 * SCATTERS)

            def load_rows(n, s, k):
                wait_count(sp, rowT_psum, n - UNROLL + 1)
                sp.dma_start(rows[:, s, :], slot_rows[ds(n * P, P), :]).then_inc(rows_loaded[s], 16)

            steps(sp, NB, UNROLL, load_rows)

            sp.wait_ge(outs_ready, NB)
            for s in range(UNROLL):
                sp.wait_ge(outs_stored[s], 16 * (NB // UNROLL))
            for dst, src in ((w1_sb[:], w1.rearrange("(k p) a -> p k a", p=P)),
                             (b1_sb[:], b1.rearrange("(a o) -> a o", o=1)),
                             (v_sb[:], v.rearrange("(a o) -> a o", o=1)),
                             (kind_i[:], kinds.rearrange("(b o) -> b o", o=1)),
                             (kind_row_i[:, 0, :], kinds.rearrange("(o b) -> o b", o=1)),
                             (k_raw[:], ffn_k.rearrange("(k p) f -> p k f", p=P)),
                             (scales[:, 0:1], in_scale.partition_broadcast(P)),
                             (scales[:, 1:2], k_scale.partition_broadcast(P)),
                             (bias_f[:], ffn_b.partition_broadcast(P))):
                sp.dma_start(dst, src).then_inc(c_loaded, 16)

            def load_x(n, s, k):
                if not (isinstance(n, int) and n < 2):
                    sp.wait_ge(mixed_kept[s], 16 * k)
                sp.dma_start(mix[:, s], x_v[ds(n)].rearrange("b p t h -> (b p) t h")).then_inc(x_again[s], 16)
                if (last := earlier(n, s, k, 1, 2)) is not None:
                    keep(*last)

            def keep(n, s, k):
                sp.wait_ge(xT_psum, 2 * n + 2)
                sp.dma_start(U[:, ds(n * TB, TB), 0:H], mix[:, s]).then_inc(mixed_kept[s], 16)
                sp.wait_ge(row_ready, n + 1)
                sp.dma_start(score_rows[ds(n), :], score_row[0:1, s, :]).then_inc(row_stored[s], 16)

            steps(sp, B, 2, load_x)
            keep(B - 1, 1, 0)
            for s in range(2):
                sp.wait_ge(row_stored[s], 16 * (B // 2))
            sp.dma_start(scores[:], score_rows).then_inc(scores_loaded, 16)
            sp.wait_ge(max_ready, 1)
            sp.dma_start(max_rows, row_max[:]).then_inc(max_stored, 16)
            sp.wait_ge(max_stored, 16)

            def spread_max(n, s, k):
                wait_count(sp, expo_ready, TB * (n - 1))
                sp.dma_start(neg_max[:, s, :],
                             max_rows[ds(n), :].rearrange("b s -> (b s)").partition_broadcast(P)).then_inc(max_loaded[s], 16)

            steps(sp, B, 2, spread_max)

        @block.gpsimd
        def _(pool):
            pool.memset(ident[:], 0.0).then_inc(pool_const, 1)
            pool.memset(diff[:], 0.0).then_inc(pool_const, 1)
            pool.memset(edge[:], 0.0).then_inc(pool_const, 1)
            pool.memset(ones_b[:], 1.0).then_inc(pool_const, 1)
            pool.memset(zero_rows[:], 0.0).then_inc(pool_const, 1)
            pool.iota(expert_i[:], [[1, E]], base=0, channel_multiplier=0).then_inc(pool_const, 1)
            pool.iota(row_i[:], [[0, 1]], base=0, channel_multiplier=1).then_inc(pool_const, 1)
            pool.iota(blk_i[:], [[P, NB]], base=0, channel_multiplier=0).then_inc(pool_const, 1)
            pool.wait_ge(pool_const, 8)
            pool.affine_select(out=ident[:], in_=ident[:], compare_op=ALU.not_equal, fill=1.0, base=0,
                               pattern=[[-1, P]], channel_multiplier=1).then_inc(pool_const, 1)
            pool.affine_select(out=above[:], in_=ones_b[:], compare_op=ALU.is_gt, fill=0.0, base=0,
                               pattern=[[1, P]], channel_multiplier=-1).then_inc(pool_const, 1)
            pool.affine_select(out=edge[:], in_=edge[:], compare_op=ALU.not_equal, fill=1.0, base=0,
                               pattern=[[-1, P]], channel_multiplier=P - 1).then_inc(pool_const, 1)
            for i, (base, fill) in enumerate(((0, -2.0), (1, 1.0), (-1, 1.0))):
                wait_count(pool, diff_step, i)
                pool.affine_select(out=diff[:], in_=diff[:], compare_op=ALU.not_equal, fill=fill, base=base,
                                   pattern=[[-1, P]], channel_multiplier=1).then_inc(diff_step, 1)
            pool.memset(U[:, :, H:H + 1], 1.0).then_inc(pool_const, 1)

            pool.wait_ge(pool_const, N_CONST_A)
            one_row = U[0:2, 0, H:H + 1]

            def step_a(n, s, k):
                pool.wait_ge(slope_ready, n + 1)
                pool.tensor_tensor(flow[:, s], flow[:, s], xb[:, s], ALU.mult).then_inc(react_ready, 1)
                pool.wait_ge(w_loaded, 16 * W_DMAS * (n + 1))
                pool.tensor_tensor(raw_b[:, 1:GU:2], raw_b[:, 1:GU:2], one_row.broadcast_to([2, I]),
                                   ALU.add).then_inc(bias_plus, 1)
                pool.wait_ge(hi_ready, 2 * n + 2)
                pool.tensor_tensor(gu_lo[:, ds(n)].rearrange("p e k (two i) -> p (e k) two i", two=2),
                                   raw_gu[:].rearrange("p k (i two) -> p k two i", two=2),
                                   gu_hi[:, ds(n)].bitcast(F32).rearrange("p e k (two i) -> p (e k) two i", two=2),
                                   ALU.subtract).then_inc(raw_used, 1)
                pool.tensor_tensor(dn_lo[:, ds(n)].rearrange("p e k h -> p (e k) h"), raw_dn[:],
                                   dn_hi[:, ds(n)].bitcast(F32).rearrange("p e k h -> p (e k) h"),
                                   ALU.subtract).then_inc(raw_used, 1)

            steps(pool, B, 2, step_a)

            pool.wait_ge(slots_ready, 2)
            for s in range(2):
                pool.wait_ge(u_kept[s], 16 * (B // 2))
            pool.wait_ge(tail_zeroed, 16 * (NB - SURE))
            for e in range(E):
                pool.indirect_dma_start(
                    out=slot_rows, out_offset=bass.IndirectOffsetOnAxis(ap=pad_slot[:, e:e + 1], axis=0),
                    in_=zero_rows[:], in_offset=None, bounds_check=NB * P - 1,
                    oob_is_err=False).then_inc(scattered, 16)
            for t in range(NT):
                for c in range(2):
                    pool.indirect_dma_start(
                        out=slot_rows, out_offset=bass.IndirectOffsetOnAxis(ap=slot_of[:, c, t:t + 1], axis=0),
                        in_=U[:, t, 0:H], in_offset=None).then_inc(scattered, 16)

            def step_b(n, s, k):
                d = s % 2
                pool.wait_ge(gate_ready, n + 1)
                pool.wait_ge(up_ready, n + 1)
                wait_count(pool, act_ready, n - 1)
                pool.tensor_tensor(glu[:, d], gate[:, d], up[:, d], ALU.mult).then_inc(glu_ready, 1)

            steps(pool, NB, UNROLL, step_b)

            for s in range(UNROLL):
                pool.wait_ge(outs_stored[s], 16 * (NB // UNROLL))
            pool.memset(masks[:], 0.0).then_inc(tables, 1)
            pool.memset(ident_b[:], 0.0).then_inc(tables, 1)
            pool.iota(counts_i[:], [[P, TB]], base=1, channel_multiplier=1).then_inc(tables, 1)
            pool.wait_ge(tables, 3)
            for i, (op, sign) in enumerate(((ALU.is_ge, 1), (ALU.is_ge, -1), (ALU.not_equal, 1))):
                pool.affine_select(out=masks[:, i], in_=masks[:, i], compare_op=op, fill=NEG,
                                   base=sign * (P - S), pattern=[[sign, MW]],
                                   channel_multiplier=-sign).then_inc(tables, 1)
            pool.affine_select(out=ident_b[:], in_=ident_b[:], compare_op=ALU.not_equal, fill=1.0, base=0,
                               pattern=[[-1, P]], channel_multiplier=1).then_inc(tables, 1)

            for n in range(B):
                wait_count(pool, mixed, n - 1)
                for c in range(2):
                    for t in range(TB):
                        col = n * TB + t
                        pool.indirect_dma_start(
                            out=picks[:, n % 2, c, t, :], out_offset=None, in_=slot_outs,
                            in_offset=bass.IndirectOffsetOnAxis(ap=slot_of[:, c, col:col + 1], axis=0),
                        ).then_inc(gathered[n % 2], 16)

            def step_c(n, s, k):
                if (last := earlier(n, s, k, 1, 2)) is not None:
                    add_bias(*last)
                pool.wait_ge(grid_ready, n + 1)
                pool.tensor_tensor(scaled[:], scaled[:], grid[:], ALU.add).then_inc(lifted, 1)
                pool.wait_ge(lifted, n + 1)
                wait_count(pool, quantT_psum, n)
                pool.tensor_tensor(quant[:], scaled[:], grid[:], ALU.subtract).then_inc(quant_ready, 1)

            def add_bias(n, s, k):
                pool.wait_ge(ffn_ready, 2 * n + 2)
                wait_count(pool, result_ready, n)
                pool.tensor_tensor(ffn_sum[:], ffn[:], bias_f[:].unsqueeze(1).broadcast_to([P, TB, F]),
                                   ALU.add).then_inc(ffn_sum_ready, 1)

            steps(pool, B, 2, step_c)
            add_bias(B - 1, 1, 0)

        @block.scalar
        def _(a):
            def step_a(n, s, k):
                a.wait_ge(z_step, 3)
                a.wait_ge(x_loaded[s], 16 * X_DMAS * (k + 1))
                if not (isinstance(n, int) and n < 2):
                    a.wait_ge(u_kept[s], 16 * k)
                    a.wait_ge(uT_psum, 2 * n - 2)
                a.activation(flow[:, s], xb[:, s], ACT.Identity, bias=zs[:, SLOPE, ds(n)],
                             scale=zs[:, ZRN, ds(n)]).then_inc(slope_ready, 1)
                a.wait_ge(w_loaded, 16 * W_DMAS * (n + 1))
                a.activation(gu_hi[:, ds(n)].rearrange("p e k (two i) -> p (e k) two i", two=2),
                             raw_gu[:].rearrange("p k (i two) -> p k two i", two=2), ACT.Copy).then_inc(hi_ready, 1)
                a.activation(dn_hi[:, ds(n)].rearrange("p e k h -> p (e k) h"), raw_dn[:],
                             ACT.Copy).then_inc(hi_ready, 1)
                a.wait_ge(bias_plus, n + 1)
                a.activation(gu_bias[:, ds(n)].rearrange("r e (two i) -> r (e two) i", two=2),
                             raw_b[:, 0:GU].rearrange("r (i two) -> r two i", two=2), ACT.Copy).then_inc(bias_hi, 1)
                a.activation(dn_bias[:, ds(n)].rearrange("r e h -> r (e h)"), raw_b[:, GU:],
                             ACT.Copy).then_inc(bias_hi, 1)
                if (last := earlier(n, s, k, 1, 2)) is not None:
                    transposed(*last)

            def transposed(n, s, k):
                wait_count(a, logits_psum, n)
                for half in range(KH):
                    a.wait_ge(uT_psum, 2 * n + half + 1)
                    a.activation(uT[:, half], uT_bank[half][:].rearrange("p (t n) -> p t n", t=TB),
                                 ACT.Copy).then_inc(uT_ready, 1)

            steps(a, B, 2, step_a)
            transposed(B - 1, 1, 0)
            a.wait_ge(gap_ready, 1)
            a.activation(odds[:, 1], odds[:, 0], ACT.Exp).then_inc(odds_ready, 1)

            a.wait_ge(scattered, 16 * SCATTERS)

            def step_b(n, s, k):
                for back, then in ((1, activate), (2, transposed_act)):
                    if (last := earlier(n, s, k, back, UNROLL)) is not None:
                        then(*last)
                d = s % 2
                a.wait_ge(rowT_psum, n + 1)
                wait_count(a, gu_psum, n - 1)
                a.activation(rowT_hi[:, d], bank[2 + d][:, 0:KH * P].rearrange("p (k n) -> p k n", k=KH),
                             ACT.Copy).then_inc(rowT_hi_ready, 1)
                if (last := earlier(n, s, k, 3, UNROLL)) is not None:
                    finish_down(*last)

            def activate(n, s, k):
                a.wait_ge(gate_ready, n + 1)
                wait_count(a, act_ready, n - 1)
                a.activation(tanh[:, s % 2], gate[:, s % 2], ACT.Tanh, scale=ALPHA).then_inc(tanh_ready, 1)

            def transposed_act(n, s, k):
                a.wait_ge(actT_psum, n + 1)
                wait_count(a, down_psum, n - 1)
                a.activation(actT_hi[:, s % 2],
                             bank[4 + s % 2][:, 0:KI * P].rearrange("p (k n) -> p k n", k=KI),
                             ACT.Copy).then_inc(actT_hi_ready, 1)

            def finish_down(n, s, k):
                a.wait_ge(down_psum, n + 1)
                if not (isinstance(n, int) and n < UNROLL):
                    a.wait_ge(outs_stored[s], 16 * k)
                a.activation(outs[:, s, :], bank[6 + s % 2][:, 0:H], ACT.Copy).then_inc(outs_ready, 1)
                a.wait_ge(outs_ready, n + 1)
                a.dma_start(slot_outs[ds(n * P, P), :], outs[:, s, :]).then_inc(outs_stored[s], 16)

            steps(a, NB, UNROLL, step_b)
            K = NB // UNROLL - 1
            activate(NB - 1, UNROLL - 1, K)
            transposed_act(NB - 2, UNROLL - 2, K)
            finish_down(NB - 3, UNROLL - 3, K)
            finish_down(NB - 2, UNROLL - 2, K)
            transposed_act(NB - 1, UNROLL - 1, K)
            finish_down(NB - 1, UNROLL - 1, K)

            a.wait_ge(c_loaded, 16 * C_DMAS)

            def scores_of(n, s, k):
                for half in range(KH):
                    a.wait_ge(xT_psum, 2 * n + half + 1)
                    wait_count(a, hidden_psum, n)
                    a.activation(xT[:, half], bank[half][:], ACT.Copy).then_inc(xT_ready, 1)
                a.wait_ge(hidden_psum, n + 1)
                wait_count(a, score_psum, n)
                a.activation(hidden[:], bank[2][0:A, :], ACT.Tanh, bias=b1_sb[:, 0:1]).then_inc(hidden_ready, 1)

            steps(a, B, 2, scores_of)

            def pool_of(n, s, k):
                for l in range(TB):
                    a.wait_ge(expo_ready, TB * n + l + 1)
                    wait_count(a, pool_psum, n)
                    a.activation(probs[:, l], expo[:, l % 2], ACT.Exp,
                                 bias=score_col[:, l, ds(n)]).then_inc(probs_ready, 1)
                if (last := earlier(n, s, k, 1, 2)) is not None:
                    finish(*last)

            def finish(n, s, k):
                a.wait_ge(quantT_psum, n + 1)
                wait_count(a, ffn_psum, 2 * n)
                a.activation(quantT[:], bank[4][:].bitcast(BF16).rearrange("p (k n) -> p k n", k=KH),
                             ACT.Copy).then_inc(quantT_ready, 1)
                wait_count(a, ffn_sum_ready, n)
                for g in range(2):
                    a.wait_ge(ffn_psum, 2 * n + g + 1)
                    a.activation(ffn[:, 2 * g:2 * g + 2, :], bank[5 + g][:].rearrange("p (t f) -> p t f", f=F),
                                 ACT.Copy, scale=scales[:, 2:3]).then_inc(ffn_ready, 1)
                a.wait_ge(result_ready, n + 1)
                a.dma_start(out_v[ds(n)].rearrange("b p t h -> (b p) t h"), result[:, s]).then_inc(result_stored[s], 16)

            steps(a, B, 2, pool_of)
            finish(B - 1, 1, 0)
            for s in range(2):
                a.wait_ge(result_stored[s], 16 * (B // 2))

        @block.tensor
        def _(pe):
            def step_a(n, s, k):
                pe.wait_ge(x_loaded[s], 16 * X_DMAS * (k + 1))
                wait_count(pe, u_ready, n)
                for g in range(2):
                    pe.matmul(lap[g][:], diff[:], xb[:, s, 2 * g:2 * g + 2, :], start=True, stop=False)
                    pe.matmul(lap[g][:], edge[:], halo[:, s, 2 * g:2 * g + 2, :], start=False,
                              stop=True).then_inc(lap_ready, 1)
                if (last := earlier(n, s, k, 1, 2)) is not None:
                    route(*last)

            def route(n, s, k):
                pe.wait_ge(u_ready, n + 1)
                wait_count(pe, uT_ready, 2 * n)
                for half in range(KH):
                    for t in range(TB):
                        mm = pe.transpose(uT_bank[half][:, t * P:(t + 1) * P],
                                          flow[:, s, t, half * P:(half + 1) * P], ident[:])
                    mm.then_inc(uT_psum, 1)
                pe.wait_ge(uT_ready, 2 * n + 2)
                wait_count(pe, logits_ready, n)
                for t in range(TB):
                    for half in range(KH):
                        mm = pe.matmul(logit_bank[:, t, :], uT[:, half, t, :], router_sb[:, half, :],
                                       start=(half == 0), stop=(half == KH - 1))
                mm.then_inc(logits_psum, 1)

            pe.wait_ge(pool_const, N_CONST_A)
            pe.wait_ge(diff_step, 3)
            pe.wait_ge(router_loaded, 16)
            steps(pe, B, 2, step_a)
            route(B - 1, 1, 0)
            pe.wait_ge(picked_ready, 1)
            pe.matmul(rank_bank, above[:], picked[:], start=True, stop=True)
            pe.matmul(total_bank, ones_b[:], picked[:], start=True, stop=True).then_inc(ranks_ready, 1)

            def rows_transposed(n, s, k):
                pe.wait_ge(rows_loaded[s], 16 * (k + 1))
                wait_count(pe, rowT_lo_ready, n - 1)
                for half in range(KH):
                    mm = pe.transpose(bank[2 + s % 2][:, half * P:(half + 1) * P],
                                      rows[:, s, half * P:(half + 1) * P], ident[:])
                mm.then_inc(rowT_psum, 1)

            def split_product(acc, hi, lo, w_hi, w_lo, bias, expert, parts):
                pe.matmul(acc, ones2[:], bias[:, ds(expert), :].rearrange("r e f -> r (e f)"),
                          start=True, stop=False)
                for part in range(parts):
                    for left, right in ((hi, w_hi), (hi, w_lo), (lo, w_hi)):
                        mm = pe.matmul(acc, left[:, part, :],
                                       right[:, ds(expert), part, :].rearrange("p e f -> p (e f)"),
                                       start=False, stop=(part == parts - 1 and left is lo))
                return mm

            def gate_up(n, s, k):
                d = s % 2
                expert = pe.value_load(block_expert[0:1, ds(n)], min_val=0, max_val=E - 1)
                pe.wait_ge(rowT_hi_ready, n + 1)
                pe.wait_ge(rowT_lo_ready, n + 1)
                wait_count(pe, up_ready, n - 1)
                split_product(bank[d][:], rowT_hi[:, d], rowT_lo[:, d], gu_hi, gu_lo, gu_bias, expert,
                              KH).then_inc(gu_psum, 1)

            def act_transposed(n, s, k):
                d = s % 2
                pe.wait_ge(act_ready, n + 1)
                wait_count(pe, actT_lo_ready, n - 1)
                for half in range(KI):
                    mm = pe.transpose(bank[4 + d][:, half * P:(half + 1) * P],
                                      act[:, d, half * P:(half + 1) * P], ident[:])
                mm.then_inc(actT_psum, 1)

            def down(n, s, k):
                d = s % 2
                expert = pe.value_load(block_expert[0:1, ds(n)], min_val=0, max_val=E - 1)
                pe.wait_ge(actT_hi_ready, n + 1)
                pe.wait_ge(actT_lo_ready, n + 1)
                wait_count(pe, outs_ready, n - 1)
                split_product(bank[6 + d][:, 0:H], actT_hi[:, d], actT_lo[:, d], dn_hi, dn_lo, dn_bias,
                              expert, KI).then_inc(down_psum, 1)

            def step_b(n, s, k):
                gate_up(n, s, k)
                for back, then in ((2, down), (1, act_transposed)):
                    if (last := earlier(n, s, k, back, UNROLL)) is not None:
                        then(*last)
                if not (isinstance(n, int) and n == NB - 1):
                    rows_transposed(n + 1, (s + 1) % UNROLL, k + (1 if s == UNROLL - 1 else 0))

            pe.wait_ge(experts_ready, 1)
            pe.wait_ge(slots_ready, 2)
            rows_transposed(0, 0, 0)
            for s in range(UNROLL):
                step_b(s, s, 0)
            with pe.Fori(1, NB // UNROLL - 1) as k:
                for s in range(UNROLL):
                    step_b(k * UNROLL + s, s, k)
            K = NB // UNROLL - 1
            for s in range(UNROLL):
                step_b(K * UNROLL + s, s, K)
            down(NB - 2, UNROLL - 2, K)
            act_transposed(NB - 1, UNROLL - 1, K)
            down(NB - 1, UNROLL - 1, K)

            def scores_of(n, s, k):
                pe.wait_ge(mixed, n + 1)
                for half in range(KH):
                    wait_count(pe, xT_ready, 2 * n - 1 + half)
                    for t in range(TB):
                        mm = pe.transpose(bank[half][:, t * P:(t + 1) * P],
                                          mix[:, s, t, half * P:(half + 1) * P], ident[:])
                    mm.then_inc(xT_psum, 1)
                pe.wait_ge(xT_ready, 2 * n + 2)
                wait_count(pe, hidden_ready, n)
                for half in range(KH):
                    mm = pe.matmul(bank[2][0:A, :], w1_sb[:, half, :], xT[:, half, :],
                                   start=(half == 0), stop=(half == KH - 1))
                mm.then_inc(hidden_psum, 1)
                pe.wait_ge(hidden_ready, n + 1)
                wait_count(pe, col_ready, n)
                wait_count(pe, row_ready, n)
                for t in range(TB):
                    pe.matmul(bank[4][:, t:t + 1], hidden[:, t * P:(t + 1) * P], v_sb[:],
                              start=True, stop=True)
                pe.matmul(bank[3][0:1, :], v_sb[:], hidden[:], start=True,
                          stop=True).then_inc(score_psum, 1)

            pe.wait_ge(outs_ready, NB)
            pe.wait_ge(c_loaded, 16 * C_DMAS)
            steps(pe, B, 2, scores_of)

            def pool_of(n, s, k):
                wait_count(pe, pooled_ready, TB * n)
                for l in range(TB):
                    pe.wait_ge(probs_ready, TB * n + l + 1)
                    for j in range(TB):
                        mm = pe.matmul(bank[j][:, 0:H + 1], probs[:, l, j * P:(j + 1) * P],
                                       U[:, ds(n * TB + l), :].rearrange("p t h -> p (t h)"),
                                       start=(l == 0), stop=(l == TB - 1))
                mm.then_inc(pool_psum, 1)
                if (last := earlier(n, s, k, 1, 2)) is not None:
                    finish(*last)

            def finish(n, s, k):
                pe.wait_ge(quant_ready, n + 1)
                wait_count(pe, quantT_ready, n)
                qT = bank[4][:].bitcast(BF16)
                for half in range(KH):
                    for t in range(TB):
                        mm = pe.transpose(qT[:, half * S + t * P:half * S + (t + 1) * P],
                                          quant[:, t, half * P:(half + 1) * P], ident_b[:])
                mm.then_inc(quantT_psum, 1)
                pe.wait_ge(quantT_ready, n + 1)
                wait_count(pe, ffn_ready, 2 * n)
                for t in range(TB):
                    for half in range(KH):
                        mm = pe.matmul(bank[5 + t // 2][:, (t % 2) * F:(t % 2 + 1) * F],
                                       quantT[:, half, t * P:(t + 1) * P], k_quant[:, half, :],
                                       start=(half == 0), stop=(half == KH - 1))
                    if t % 2:
                        mm.then_inc(ffn_psum, 1)

            for s in range(2):
                pe.wait_ge(mixed_kept[s], 16 * (B // 2))
            pe.wait_ge(table_step, 6)
            pe.wait_ge(col_ready, B)
            pe.wait_ge(row_ready, B)
            pe.wait_ge(tables, 7)
            steps(pe, B, 2, pool_of)
            finish(B - 1, 1, 0)

        @block.vector
        def _(dve):
            dve.wait_ge(z_loaded, 48)
            dve.tensor_scalar(zs[:, ZRN, :], zs[:, ZR, :], -1.0, None, ALU.mult).then_inc(z_step, 1)
            dve.scalar_tensor_tensor(out=zs[:, SLOPE, :], in0=zs[:, ZX, :], scalar=-2.0, in1=zs[:, ZR, :],
                                     op0=ALU.mult, op1=ALU.add).then_inc(z_step, 1)
            dve.wait_ge(pool_const, 8)
            dve.tensor_copy(row_f[:], row_i[:]).then_inc(z_step, 1)
            dve.tensor_copy(expert_f[:], expert_i[:]).then_inc(z_step, 1)
            dve.tensor_copy(blk_f[:], blk_i[:]).then_inc(z_step, 1)
            dve.wait_ge(z_step, 5)
            dve.tensor_copy(row_sel[:, 0:1], row_f[0:2, :]).then_inc(z_step, 1)
            dve.tensor_scalar(row_sel[:, 1:2], row_f[0:2, :], -2.0, 1.0, ALU.mult, ALU.add).then_inc(z_step, 1)
            dve.memset(ones2[:].bitcast(F32), 1.0).then_inc(z_step, 1)
            dve.memset(follow[:], 1.0).then_inc(z_step, 1)
            dve.wait_ge(z_step, 9)
            dve.memset(follow[:, :, 0:1], 0.0).then_inc(z_step, 1)
            dve.wait_ge(z_step, 10)

            def step_a(n, s, k):
                u = flow[:, s]
                zx_n, zy_n = zs[:, ZX, ds(n)], zs[:, ZY, ds(n)]
                dve.wait_ge(react_ready, n + 1)
                dve.scalar_tensor_tensor(out=u[:, :, 1:H], in0=xb[:, s, :, 0:H - 1], scalar=zx_n,
                                         in1=u[:, :, 1:H], op0=ALU.mult, op1=ALU.add).then_inc(flow_step, 1)
                dve.wait_ge(flow_step, 3 * n + 1)
                dve.scalar_tensor_tensor(out=u[:, :, 0:H - 1], in0=xb[:, s, :, 1:H], scalar=zx_n,
                                         in1=u[:, :, 0:H - 1], op0=ALU.mult, op1=ALU.add).then_inc(flow_step, 1)
                dve.wait_ge(flow_step, 3 * n + 2)
                dve.scalar_tensor_tensor(out=u[:, :, 0:H:H - 1], in0=xb[:, s, :, 1:H - 1:H - 3], scalar=zx_n,
                                         in1=u[:, :, 0:H:H - 1], op0=ALU.mult, op1=ALU.add).then_inc(flow_step, 1)
                dve.wait_ge(flow_step, 3 * n + 3)
                dve.wait_ge(lap_ready, 2 * n + 2)
                for g in range(2):
                    ug = u[:, 2 * g:2 * g + 2, :]
                    op = dve.scalar_tensor_tensor(out=ug, in0=lap[g][:].rearrange("p (t h) -> p t h", h=H),
                                                  scalar=zy_n, in1=ug, op0=ALU.mult, op1=ALU.add)
                op.then_inc(u_ready, 1)
                dve.wait_ge(bias_hi, 2 * n + 2)
                dve.tensor_scalar(raw_b[:], raw_b[:], row_sel[:, 0:1], None, ALU.mult).then_inc(bias_step, 1)
                dve.wait_ge(bias_step, n + 1)
                gb = gu_bias[:, ds(n)].rearrange("r e (two i) -> r (e two) i", two=2)
                db = dn_bias[:, ds(n)].rearrange("r e h -> r (e h)")
                dve.scalar_tensor_tensor(out=gb, in0=gb.bitcast(F32), scalar=row_sel[:, 1:2],
                                         in1=raw_b[:, 0:GU].rearrange("r (i two) -> r two i", two=2),
                                         op0=ALU.mult, op1=ALU.add).then_inc(raw_used, 1)
                dve.scalar_tensor_tensor(out=db, in0=db.bitcast(F32), scalar=row_sel[:, 1:2], in1=raw_b[:, GU:],
                                         op0=ALU.mult, op1=ALU.add).then_inc(raw_used, 1)
                if (last := earlier(n, s, k, 1, 2)) is not None:
                    best_two(*last)

            def best_two(n, s, k):
                dve.wait_ge(logits_psum, n + 1)
                dve.tensor_copy(logits[:], logit_bank).then_inc(logits_ready, 1)
                wait_alone(dve, logits_ready, n + 1, z_step, 10)
                for t in range(TB):
                    dve.max(best[:, t], logits[:, t]).then_inc(best_step, 1)
                wait_alone(dve, best_step, TB * (n + 1), z_step, 10)
                for t in range(TB):
                    dve.max_index(best_i[:, t], best[:, t], logits[:, t]).then_inc(index_step, 1)
                dve.wait_ge(index_step, TB * (n + 1))
                dve.tensor_copy(top[:, ds(n * TB, TB), :], best[:, :, 0:2]).then_inc(top_ready, 1)
                dve.tensor_copy(top_i[:, ds(n * TB, TB), :], best_i[:, :, 0:2]).then_inc(top_ready, 1)

            steps(dve, B, 2, step_a)
            best_two(B - 1, 1, 0)

            done = [0]

            def then(instruction):
                done[0] += 1
                instruction.then_inc(route_step, 1)
                dve.wait_ge(route_step, done[0])

            dve.wait_ge(top_ready, 2 * B)
            dve.tensor_tensor(odds[:, 0], top[:, :, 1], top[:, :, 0], ALU.subtract).then_inc(gap_ready, 1)
            for c in range(2):
                op = dve.tensor_tensor(pick[:, c], expert_f[:].unsqueeze(2).broadcast_to([P, E, NT]),
                                       top_i[:, :, c].unsqueeze(1).broadcast_to([P, E, NT]), ALU.is_equal)
            then(op)
            dve.tensor_tensor(picked[:], pick[:, 0], pick[:, 1], ALU.add).then_inc(picked_ready, 1)
            dve.wait_ge(ranks_ready, 1)
            then(dve.tensor_copy(totals[:], total_bank))
            flat = lambda m: m[:].rearrange("p e t -> p (e t)")
            then(dve.tensor_tensor_scan(flat(upto), flat(follow), flat(totals), 0.0, ALU.mult, ALU.add))
            COUNT, PADDED, END, FILLED, ONE = range(5)
            ends_of = lambda i: ends[:, i, :]
            dve.tensor_copy(ends_of(COUNT), upto[:, :, NT - 1])
            then(dve.memset(ends_of(ONE), 1.0))
            then(dve.tensor_scalar(ends_i[:, 0, :], ends_of(COUNT), float(P - 1), None, ALU.add))
            then(dve.tensor_scalar(ends_i[:, 1, :], ends_i[:, 0, :], 7, 7, ALU.logical_shift_right,
                                   ALU.logical_shift_left))
            then(dve.tensor_copy(ends_of(PADDED), ends_i[:, 1, :]))
            then(dve.tensor_tensor_scan(ends_of(END), ends_of(ONE), ends_of(PADDED), 0.0, ALU.mult, ALU.add))
            then(dve.tensor_tensor(ends_of(PADDED), ends_of(END), ends_of(PADDED), ALU.subtract))
            then(dve.tensor_tensor(ends_of(FILLED), ends_of(PADDED), ends_of(COUNT), ALU.add))
            then(dve.tensor_tensor(upto[:], upto[:], totals[:], ALU.subtract))
            then(dve.tensor_tensor(upto[:], upto[:], rank_bank, ALU.add))
            then(dve.tensor_tensor(upto[:], upto[:], ends_of(PADDED).unsqueeze(2).broadcast_to([P, E, NT]),
                                   ALU.add))
            for c in range(2):
                op = dve.tensor_tensor(pick[:, c], pick[:, c], upto[:], ALU.mult)
            then(op)
            for c in range(2):
                op = dve.tensor_reduce(slot_f[:, c, :], pick[:, c].rearrange("p e t -> p t e"), AX.X, ALU.add)
            then(op)
            dve.tensor_copy(slot_of[:], slot_f[:]).then_inc(slots_ready, 1)
            then(dve.tensor_scalar(ends_of(FILLED), ends_of(FILLED), row_f[:, 0:1], None, ALU.add))
            then(dve.tensor_tensor(ends_of(ONE), ends_of(FILLED), ends_of(END), ALU.is_ge))
            then(dve.scalar_tensor_tensor(out=ends_of(ONE), in0=ends_of(ONE), scalar=SLOT_BIG,
                                          in1=ends_of(FILLED), op0=ALU.mult, op1=ALU.add))
            dve.tensor_copy(pad_slot[:], ends_of(ONE)).then_inc(slots_ready, 1)
            then(dve.tensor_tensor(blk_past[:], blk_f[:].unsqueeze(2).broadcast_to([1, NB, E]),
                                   ends[0:1, END, :].unsqueeze(1).broadcast_to([1, NB, E]), ALU.is_ge))
            then(dve.tensor_reduce(blk_e[:], blk_past[:], AX.X, ALU.add))
            dve.tensor_scalar(block_expert[:], blk_e[:], float(E - 1), None, ALU.min).then_inc(experts_ready, 1)
            dve.wait_ge(odds_ready, 1)
            then(dve.tensor_scalar(odds[:, 2], odds[:, 1], 1.0, None, ALU.add))
            then(dve.reciprocal(tok_w[:, 0, :], odds[:, 2]))
            then(dve.tensor_tensor(tok_w[:, 1, :], odds[:, 1], tok_w[:, 0, :], ALU.mult))

            dve.wait_ge(scattered, 16 * SCATTERS)

            def step_b(n, s, k):
                if (last := earlier(n, s, k, 1, UNROLL)) is not None:
                    clip(*last)
                if (last := earlier(n, s, k, 2, UNROLL)) is not None:
                    act_low(*last)
                d = s % 2
                dve.wait_ge(rowT_hi_ready, n + 1)
                wait_count(dve, gu_psum, n - 1)
                dve.tensor_tensor(rowT_lo[:, d], bank[2 + d][:, 0:KH * P].rearrange("p (k n) -> p k n", k=KH),
                                  rowT_hi[:, d].bitcast(F32), ALU.subtract).then_inc(rowT_lo_ready, 1)
                if (last := earlier(n, s, k, 1, UNROLL)) is not None:
                    activated(*last)

            def clip(n, s, k):
                d = s % 2
                dve.wait_ge(gu_psum, n + 1)
                wait_count(dve, act_ready, n - 1)
                dve.tensor_scalar(gate[:, d], bank[d][:, 0:I], LIMIT, 0.5, ALU.min,
                                  ALU.mult).then_inc(gate_ready, 1)
                dve.tensor_scalar(up[:, d], bank[d][:, I:GU], LIMIT + 1.0, 1.0 - LIMIT, ALU.min,
                                  ALU.max).then_inc(up_ready, 1)

            def activated(n, s, k):
                d = s % 2
                dve.wait_ge(tanh_ready, n + 1)
                dve.wait_ge(glu_ready, n + 1)
                wait_count(dve, actT_psum, n - 1)
                dve.scalar_tensor_tensor(out=act[:, d], in0=tanh[:, d], scalar=1.0, in1=glu[:, d],
                                         op0=ALU.add, op1=ALU.mult).then_inc(act_ready, 1)

            def act_low(n, s, k):
                d = s % 2
                dve.wait_ge(actT_hi_ready, n + 1)
                wait_count(dve, down_psum, n - 1)
                dve.tensor_tensor(actT_lo[:, d], bank[4 + d][:, 0:KI * P].rearrange("p (k n) -> p k n", k=KI),
                                  actT_hi[:, d].bitcast(F32), ALU.subtract).then_inc(actT_lo_ready, 1)

            steps(dve, NB, UNROLL, step_b)
            K = NB // UNROLL - 1
            clip(NB - 1, UNROLL - 1, K)
            act_low(NB - 2, UNROLL - 2, K)
            activated(NB - 1, UNROLL - 1, K)
            act_low(NB - 1, UNROLL - 1, K)

            tdone = [0]

            def table(instruction):
                tdone[0] += 1
                instruction.then_inc(table_step, 1)
                dve.wait_ge(table_step, tdone[0])

            dve.wait_ge(c_loaded, 16 * C_DMAS)
            dve.wait_ge(tables, 7)
            table(dve.reciprocal(scales[:, 3:5], scales[:, 0:2]))
            table(dve.tensor_scalar(k_scaled[:], k_raw[:], scales[:, 4:5], None, ALU.mult))
            table(dve.tensor_scalar(k_grid[:].bitcast(I32), k_scaled[:].bitcast(I32), EXPONENT_BITS, None,
                                    ALU.bitwise_and))
            table(dve.tensor_scalar(k_grid[:], k_grid[:], FP8_LEAST_NORMAL, FP8_GRID, ALU.max, ALU.mult))
            table(dve.tensor_tensor(k_scaled[:], k_scaled[:], k_grid[:], ALU.add))
            table(dve.tensor_tensor(k_quant[:], k_scaled[:], k_grid[:], ALU.subtract))
            table(dve.tensor_tensor(scales[:, 2:3], scales[:, 0:1], scales[:, 1:2], ALU.mult))
            table(dve.tensor_copy(counts[:, 0, :], counts_i[:]))
            table(dve.tensor_scalar(counts[:, 1, :], counts[:, 0, :], -1.0, float(S + 1), ALU.mult, ALU.add))
            dve.memset(counts[:, 2, :], float(S - 1))
            table(dve.tensor_copy(kind_row[:, 0, :], kind_row_i[:, 0, :]))
            table(dve.reciprocal(counts[:], counts[:]))
            dve.tensor_scalar(kind_row[:, 1, :], kind_row[:, 0, :], 0.0, -2.0, ALU.is_equal, ALU.mult)
            table(dve.tensor_scalar(kind_row[:, 2, :], kind_row[:, 0, :], 1.0, None, ALU.is_equal))
            table(dve.tensor_tensor(kind_row[:, 1, :], kind_row[:, 1, :], kind_row[:, 2, :], ALU.subtract))
            table(dve.tensor_scalar(kind_row_i[:, 1, :], kind_row[:, 1, :], 2.0, None, ALU.add))
            table(dve.tensor_copy(kind_of[:, 0:1], kind_i[:]))
            dve.tensor_scalar(kind_of[:, 1:2], kind_of[:, 0:1], 0.0, NEG, ALU.not_equal, ALU.mult)
            dve.tensor_scalar(kind_of[:, 2:3], kind_of[:, 0:1], 1.0, NEG, ALU.not_equal, ALU.mult)
            dve.tensor_scalar(kind_of[:, 4:5], kind_of[:, 0:1], 1.0, None, ALU.is_equal)
            table(dve.tensor_scalar(kind_of[:, 5:6], kind_of[:, 0:1], 0.0, None, ALU.is_equal))
            table(dve.tensor_tensor(kind_of[:, 4:5], kind_of[:, 4:5], kind_of[:, 5:6], ALU.add))
            table(dve.tensor_scalar(kind_of[:, 3:4], kind_of[:, 4:5], NEG, None, ALU.mult))

            def mix_of(n, s, k):
                dve.wait_ge(gathered[s], 16 * 2 * TB * (k + 1))
                dve.wait_ge(x_again[s], 16 * (k + 1))
                for c in range(2):
                    for t in range(TB):
                        op = dve.scalar_tensor_tensor(out=mix[:, s, t, :], in0=picks[:, s, c, t, :],
                                                      scalar=tok_w[:, c, ds(n * TB + t)], in1=mix[:, s, t, :],
                                                      op0=ALU.mult, op1=ALU.add)
                    if c == 0:
                        op.then_inc(mix_step, 1)
                        dve.wait_ge(mix_step, n + 1)
                op.then_inc(mixed, 1)
                if (last := earlier(n, s, k, 1, 2)) is not None:
                    copy_scores(*last)

            def copy_scores(n, s, k):
                dve.wait_ge(score_psum, n + 1)
                if not (isinstance(n, int) and n < 2):
                    dve.wait_ge(row_stored[s], 16 * k)
                dve.tensor_copy(score_row[:, s, :], bank[3][0:1, :]).then_inc(row_ready, 1)
                dve.tensor_copy(score_col[:, :, ds(n)].rearrange("p t n -> p (t n)"),
                                bank[4][:, 0:TB]).then_inc(col_ready, 1)

            steps(dve, B, 2, mix_of)
            copy_scores(B - 1, 1, B // 2 - 1)

            mdone = [0]

            def stat(instruction):
                mdone[0] += 1
                instruction.then_inc(max_step, 1)
                dve.wait_ge(max_step, mdone[0])

            dve.wait_ge(scores_loaded, 16)
            LOWEST = -3.0e38
            stat(dve.tensor_tensor_scan(from_left[:], scores[:], scores[:], LOWEST, ALU.max, ALU.max))
            stat(dve.tensor_tensor_scan(from_right[:, ::-1], scores[:, ::-1], scores[:, ::-1], LOWEST,
                                        ALU.max, ALU.max))
            dve.tensor_tensor(around[:, 1:S - 1], from_left[:, 0:S - 2], from_right[:, 2:S], ALU.max)
            dve.tensor_copy(around[:, 0:1], from_right[:, 1:2])
            dve.tensor_copy(around[:, S - 1:S], from_left[:, S - 2:S - 1])
            stat(dve.tensor_scalar(row_max[:], from_left[:], kind_of[:, 1:2], None, ALU.add))
            stat(dve.scalar_tensor_tensor(out=row_max[:], in0=from_right[:], scalar=kind_of[:, 2:3],
                                          in1=row_max[:], op0=ALU.add, op1=ALU.max))
            stat(dve.scalar_tensor_tensor(out=row_max[:], in0=around[:], scalar=kind_of[:, 3:4],
                                          in1=row_max[:], op0=ALU.add, op1=ALU.max))
            dve.tensor_scalar(row_max[:], row_max[:], -1.0, None, ALU.mult).then_inc(max_ready, 1)

            def pool_of(n, s, k):
                kind = dve.value_load(kind_row_i[0:1, 1, ds(n)], min_val=0, max_val=2)
                dve.wait_ge(max_loaded[s], 16 * (k + 1))
                for l in range(TB):
                    lo = S - P - P * l
                    wait_count(dve, probs_ready, TB * n + l - 1)
                    dve.tensor_tensor(expo[:, l % 2], neg_max[:, s, :],
                                      masks[:, ds(kind), lo:lo + S].rearrange("p m s -> p (m s)"),
                                      ALU.add).then_inc(expo_ready, 1)
                dve.wait_ge(pool_psum, n + 1)
                for j in range(TB):
                    op = dve.reciprocal(norm[:, j:j + 1], bank[j][:, H:H + 1])
                op.then_inc(norm_ready, 1)
                dve.wait_ge(norm_ready, n + 1)
                for j in range(TB):
                    dve.tensor_scalar(pooled[:, j, :], bank[j][:, 0:H], norm[:, j:j + 1],
                                      counts[:, ds(kind), j], ALU.mult, ALU.mult).then_inc(pooled_ready, 1)
                dve.wait_ge(pooled_ready, TB * (n + 1))
                wait_count(dve, quant_ready, n)
                dve.tensor_scalar(scaled[:], pooled[:], scales[:, 3:4], None,
                                  ALU.mult).then_inc(scaled_ready, 1)
                dve.wait_ge(scaled_ready, n + 1)
                dve.tensor_scalar(grid[:].bitcast(I32), scaled[:].bitcast(I32), EXPONENT_BITS, None,
                                  ALU.bitwise_and).then_inc(bits_ready, 1)
                dve.wait_ge(bits_ready, n + 1)
                dve.tensor_scalar(grid[:], grid[:], FP8_LEAST_NORMAL, FP8_GRID, ALU.max,
                                  ALU.mult).then_inc(grid_ready, 1)
                if (last := earlier(n, s, k, 1, 2)) is not None:
                    add_up(*last)

            def add_up(n, s, k):
                dve.wait_ge(ffn_sum_ready, n + 1)
                if not (isinstance(n, int) and n < 2):
                    dve.wait_ge(result_stored[s], 16 * k)
                dve.tensor_tensor(result[:, s], U[:, ds(n * TB, TB), 0:H], ffn_sum[:],
                                  ALU.add).then_inc(result_ready, 1)

            steps(dve, B, 2, pool_of)
            add_up(B - 1, 1, B // 2 - 1)


_INS = ["x", "condB_zX", "condB_zY", "condB_zR", "itok_B_0_2", "L0_ffn_router_weight", "L0_ffn_gate_up_proj",
        "L0_ffn_gate_up_proj_bias", "L0_ffn_down_proj", "L0_ffn_down_proj_bias", "L1_cond_W1", "L1_cond_b1",
        "L1_cond_v", "L1_ffn_kernel", "L1_ffn_input_scale", "L1_ffn_kernel_scale", "L1_ffn_bias"]


def kernel(**inputs):
    import numpy as np
    import concourse.bacc as bacc
    from concourse.bass_utils import run_bass_kernel_spmd

    nc = bacc.Bacc("TRN2", target_bir_lowering=False, num_devices=1)
    arrays, args = {}, []
    for name in _INS:
        a = np.ascontiguousarray(inputs[name])
        arrays[f"in_{name}"] = a
        args.append(nc.dram_tensor(f"in_{name}", a.shape, mybir.dt.from_np(a.dtype), kind="ExternalInput").ap())
    args.append(nc.dram_tensor("out_0", inputs["x"].shape, F32, kind="ExternalOutput").ap())
    adaln_ffn_kernel(nc, *args)
    r = run_bass_kernel_spmd(nc, [arrays], core_ids=[0])
    return r.results[0]["out_0"]
```

```python
from contextlib import ExitStack

import concourse.bass as bass
from concourse import mybir

ALU = mybir.AluOpType
ACT = mybir.ActivationFunctionType
AX = mybir.AxisListType
F32 = mybir.dt.float32
F32R = mybir.dt.float32r
BF16 = mybir.dt.bfloat16
I32 = mybir.dt.int32
U32 = mybir.dt.uint32

P = 128
ALPHA, LIMIT = 1.702, 7.0
NEG = -1.0e30
EXPONENT_BITS = 0x7F800000
FP8_LEAST_NORMAL = 2.0 ** -6
FP8_GRID = 1.5 * 2.0 ** 20
ROW_BIG = 1.0e6


def later(n, s, k, unroll, count):
    if isinstance(n, int) and n == count - 1:
        return None
    return n + 1, (s + 1) % unroll, k + (1 if s == unroll - 1 else 0)


def steps_peeled(eng, count, unroll, step):
    last = count // unroll - 1
    for n in range(2 * unroll):
        step(n, n % unroll, n // unroll)
    with eng.Fori(2, last) as k:
        for s in range(unroll):
            step(k * unroll + s, s, k)
    for s in range(unroll):
        step(last * unroll + s, s, last)
    return last


def ds(i, n=1):
    return bass.ds(i, n)


def wait_count(eng, semaphore, count):
    if not isinstance(count, int) or count > 0:
        eng.wait_ge(semaphore, count)


def wait_alone(eng, semaphore, count, passed, passed_count):
    eng.wait_ge(passed, passed_count)
    eng.wait_ge(semaphore, count)


def steps(eng, count, unroll, step):
    for n in range(2 * unroll):
        step(n, n % unroll, n // unroll)
    with eng.Fori(2, count // unroll) as k:
        for s in range(unroll):
            step(k * unroll + s, s, k)


def earlier(n, s, k, back, unroll):
    if isinstance(n, int) and n < back:
        return None
    return n - back, (s - back) % unroll, k - (1 if s < back else 0)


def adaln_ffn_kernel(nc, x, zx, zy, zr, kinds, router_w, gate_up_w, gate_up_b, down_w, down_b,
                     w1, b1, v, ffn_k, in_scale, k_scale, ffn_b, out):
    B, S, H = x.shape
    E = router_w.shape[1]
    I = down_w.shape[1]
    A = w1.shape[1]
    F = ffn_k.shape[1]
    GU = 2 * I
    TB = S // P
    NT = B * TB
    KH, KI = H // P, I // P
    assert B == E and H == I == F == 256 and TB == 4 and B % 2 == 0

    UNROLL = 4
    MOST = (2 * B * S - E) // P + E
    NB = -(-MOST // UNROLL) * UNROLL
    T = B * S
    GT = 8
    MW = 2 * S - P

    x_v = x.rearrange("b (t p) h -> b p t h", p=P)
    out_v = out.rearrange("b (t p) h -> b p t h", p=P)
    gate_up_v = gate_up_w.rearrange("e (k p) f -> e p k f", p=P)
    down_v = down_w.rearrange("e (k p) h -> e p k h", p=P)

    u_rows = nc.dram_tensor("u_rows", [T, H], F32).ap()
    y_rows = nc.dram_tensor("y_rows", [2 * T, H], F32).ap()
    u_v = u_rows.rearrange("(b t p) h -> b p t h", p=P, t=TB)
    y_v = y_rows.rearrange("(c b t p) h -> c b p t h", p=P, t=TB, b=B)
    score_rows = nc.dram_tensor("score_rows", [B, S], F32).ap()
    max_rows = nc.dram_tensor("max_rows", [B, S], F32).ap()

    with ExitStack() as ctx:
        def sem(name):
            return ctx.enter_context(nc.semaphore(name))

        def memory(scope):
            return lambda name, shape, dt=F32: scope.enter_context(nc.sbuf_tensor(name, shape, dt))

        bank = [ctx.enter_context(nc.psum_tensor(f"bank{i}", [P, 512], F32)) for i in range(8)]

        sb = memory(ctx)
        X = sb("X", [P, NT, H + 1])
        tok_w = sb("tok_w", [P, 2, NT])
        ident = sb("ident", [P, P])

        with ExitStack() as ab:
            sb = memory(ab)
            gu_hi = sb("gu_hi", [P, E, KH, GU], F32R)
            gu_lo = sb("gu_lo", [P, E, KH, GU], F32R)
            dn_hi = sb("dn_hi", [P, E, KI, H], F32R)
            dn_lo = sb("dn_lo", [P, E, KI, H], F32R)
            gu_bias = sb("gu_bias", [2, 2, E, I], F32R)
            dn_bias = sb("dn_bias", [2, E, H], F32R)
            ones2 = sb("ones2", [2, P], F32R)
            block_expert = sb("block_expert", [1, NB], I32)
            slot_src = sb("slot_src", [P, NB], U32)
            slot_dst = sb("slot_dst", [P, NB], U32)
            with ExitStack() as a:
                sb = memory(a)
                halo_memory = sb("halo_memory", [P, 2 * TB * H])
                halo = halo_memory[0:2].rearrange("r (s t h) -> r s t h", s=2, t=TB)
                flow = sb("flow", [P, 2, TB, H])
                pair = sb("pair", [P, 2, TB, H])
                uT = sb("uT", [P, KH, S])
                raw_gu = sb("raw_gu", [P, KH, GU])
                raw_dn = sb("raw_dn", [P, KI, H])
                raw_gb = sb("raw_gb", [P, E * GU // P])
                raw_db = sb("raw_db", [P, E * H // P])
                flat_gb = sb("flat_gb", [P, 2, E * GU // P], F32R)
                flat_db = sb("flat_db", [P, 2, E * H // P], F32R)
                diff = sb("diff", [P, P])
                edge = sb("edge", [2, P])
                diff_n = sb("diff_n", [P, 2, P])
                edge_n = sb("edge_n", [2, 2, P])
                slant = sb("slant", [P, 2, P])
                logitsT = sb("logitsT", [E, S])
                above = sb("above", [P, P], BF16)
                ones_b = sb("ones_b", [P, P], BF16)
                zs = sb("zs", [P, 5, B])
                router_sb = sb("router_sb", [P, KH, E])
                logits = sb("logits", [P, TB, E])
                best = sb("best", [P, TB, 8])
                best_i = sb("best_i", [P, TB, 8], U32)
                top = sb("top", [P, NT, 2])
                top_i = sb("top_i", [P, NT, 2])
                expert_f = sb("expert_f", [P, E])
                pick = sb("pick", [P, 2, E, NT])
                picked = sb("picked", [P, E, NT], BF16)
                follow = sb("follow", [P, E, NT])
                totals = sb("totals", [P, E, NT])
                upto = sb("upto", [P, E, NT])
                ends = sb("ends", [P, 6, E])
                ends_i = sb("ends_i", [P, 2, E], I32)
                slot_i = sb("slot_i", [P, 3, 2, NT], I32)
                slot_q = sb("slot_q", [P, 2, NT])
                slot_b = sb("slot_b", [P, 2, NT])
                column_i = sb("column_i", [P, P], I32)
                column = sb("column", [P, P], BF16)
                is_q = pair[:, 0].bitcast(BF16).rearrange("p t (g n) -> p (t g) n", n=P
                                                          ).rearrange("p (d g) n -> p d g n", d=2)
                is_b = pair[:, 1].rearrange("p t h -> p (t h)")[:, 0:GT * NB].bitcast(BF16).rearrange(
                    "p (d g n) -> p d g n", d=2, g=GT)
                is_b_of = halo_memory[:, 0:2 * GT * NB].bitcast(BF16).rearrange(
                    "p (d g v n) -> p d g v n", d=2, g=GT, v=2)
                tile_no = sb("tile_no", [P, 2 * NT], BF16)
                row_one = sb("row_one", [P, 1])
                pair_no = sb("pair_no", [P, 4, NB])
                row_i = sb("row_i", [P, 1], I32)
                row_f = sb("row_f", [P, 1])
                slot_f = sb("slot_f", [P, 2, NT])
                odds = sb("odds", [P, 3, NT])
                blk_i = sb("blk_i", [1, NB], I32)
                blk_f = sb("blk_f", [1, NB])
                blk_past = uT[0:1].rearrange("p k s -> p (k s)")[:, 0:NB * E].rearrange("p (n e) -> p n e", e=E)
                blk_e = sb("blk_e", [1, NB])
            with ExitStack() as b_:
                sb = memory(b_)
                rows = sb("rows", [P, UNROLL, H])
                rowT_hi = sb("rowT_hi", [P, 2, KH, P], F32R)
                rowT_lo = sb("rowT_lo", [P, 2, KH, P], F32R)
                gate = sb("gate", [P, 2, I])
                up = sb("up", [P, 2, I])
                tanh = sb("tanh", [P, 2, I])
                glu = sb("glu", [P, 2, I])
                act = sb("act", [P, 2, I])
                actT_hi = sb("actT_hi", [P, 2, KI, P], F32R)
                actT_lo = sb("actT_lo", [P, 2, KI, P], F32R)
                outs = sb("outs", [P, UNROLL, H])

        sb = memory(ctx)
        picks = sb("picks", [P, 2, 2, TB, H])
        mix = sb("mix", [P, 2, TB, H])
        xT = sb("xT", [P, KH, S])
        hidden = sb("hidden", [A, S])
        score_row = sb("score_row", [1, 2, S])
        score_col = sb("score_col", [P, TB, B])
        scores = sb("scores", [B, S])
        from_left = sb("from_left", [B, S])
        from_right = sb("from_right", [B, S])
        around = sb("around", [B, S])
        row_max = sb("row_max", [B, S])
        kind_of = sb("kind_of", [B, 6])
        kind_i = sb("kind_i", [B, 1], I32)
        kind_row = sb("kind_row", [1, 4, B])
        kind_row_i = sb("kind_row_i", [1, 2, B], I32)
        masks = sb("masks", [P, 3, MW])
        counts = sb("counts", [P, 3, TB])
        counts_i = sb("counts_i", [P, TB], I32)
        w1_sb = sb("w1_sb", [P, KH, A])
        b1_sb = sb("b1_sb", [A, 1])
        v_sb = sb("v_sb", [A, 1])
        neg_max = sb("neg_max", [P, 2, S])
        expo = sb("expo", [P, 2, S])
        probs = sb("probs", [P, 2, TB, S])
        norm = sb("norm", [P, TB])
        pooled = sb("pooled", [P, TB, H], BF16)
        scaled = sb("scaled", [P, TB, H])
        grid = sb("grid", [P, TB, H])
        quant = sb("quant", [P, TB, H], BF16)
        quantT = sb("quantT", [P, KH, S], BF16)
        ident_b = sb("ident_b", [P, P], BF16)
        k_raw = sb("k_raw", [P, KH, F], BF16)
        k_scaled = sb("k_scaled", [P, KH, F])
        k_grid = sb("k_grid", [P, KH, F])
        k_quant = sb("k_quant", [P, KH, F], BF16)
        scales = sb("scales", [P, 5])
        bias_f = sb("bias_f", [P, F], BF16)
        ffn = sb("ffn", [P, TB, F], BF16)
        ffn_sum = sb("ffn_sum", [P, TB, F], BF16)
        result = sb("result", [P, 2, TB, H])

        pool_const = sem("pool_const")
        diff_step = sem("diff_step")
        z_loaded = sem("z_loaded")
        router_loaded = sem("router_loaded")
        z_step = sem("z_step")
        x_loaded = [sem(f"x_loaded{i}") for i in range(2)]
        w_loaded = sem("w_loaded")
        matrix_step = sem("matrix_step")
        matrix_ready = sem("matrix_ready")
        lap_ready = sem("lap_ready")
        pair_step = sem("pair_step")
        pair_ready = sem("pair_ready")
        flow_step = sem("flow_step")
        u_ready = sem("u_ready")
        u_kept = [sem(f"u_kept{i}") for i in range(2)]
        uT_psum = sem("uT_psum")
        uT_ready = sem("uT_ready")
        logitsT_psum = sem("logitsT_psum")
        logitsT_ready = sem("logitsT_ready")
        logits_psum = sem("logits_psum")
        logits_ready = sem("logits_ready")
        best_step = sem("best_step")
        index_step = sem("index_step")
        top_ready = sem("top_ready")
        hi_ready = sem("hi_ready")
        raw_used = sem("raw_used")
        bias_loaded = sem("bias_loaded")
        bias_step = sem("bias_step")
        bias_placed = sem("bias_placed")
        route_step = sem("route_step")
        picked_ready = sem("picked_ready")
        ranks_ready = sem("ranks_ready")
        gap_ready = sem("gap_ready")
        odds_ready = sem("odds_ready")
        slots_ready = sem("slots_ready")
        is_q_ready = sem("is_q_ready")
        is_b_ready = sem("is_b_ready")
        is_b_tile = sem("is_b_tile")
        turned = sem("turned")
        experts_ready = sem("experts_ready")
        rows_loaded = [sem(f"rows_loaded{i}") for i in range(UNROLL)]
        rowT_psum = sem("rowT_psum")
        rowT_hi_ready = sem("rowT_hi_ready")
        rowT_lo_ready = sem("rowT_lo_ready")
        gu_psum = sem("gu_psum")
        gate_ready = sem("gate_ready")
        up_ready = sem("up_ready")
        tanh_ready = sem("tanh_ready")
        glu_ready = sem("glu_ready")
        act_ready = sem("act_ready")
        actT_psum = sem("actT_psum")
        actT_hi_ready = sem("actT_hi_ready")
        actT_lo_ready = sem("actT_lo_ready")
        down_psum = sem("down_psum")
        outs_ready = sem("outs_ready")
        outs_stored = [sem(f"outs_stored{i}") for i in range(UNROLL)]
        c_loaded = sem("c_loaded")
        y_loaded = [sem(f"y_loaded{i}") for i in range(2)]
        mix_step = sem("mix_step")
        mixed = sem("mixed")
        mixed_kept = [sem(f"mixed_kept{i}") for i in range(2)]
        xT_psum = sem("xT_psum")
        xT_ready = sem("xT_ready")
        hidden_psum = sem("hidden_psum")
        hidden_ready = sem("hidden_ready")
        score_psum = sem("score_psum")
        row_ready = sem("row_ready")
        col_ready = sem("col_ready")
        row_stored = [sem(f"row_stored{i}") for i in range(2)]
        scores_loaded = sem("scores_loaded")
        tables = sem("tables")
        table_step = sem("table_step")
        max_step = sem("max_step")
        max_ready = sem("max_ready")
        max_stored = sem("max_stored")
        max_loaded = [sem(f"max_loaded{i}") for i in range(2)]
        expo_ready = sem("expo_ready")
        probs_ready = sem("probs_ready")
        pool_psum = sem("pool_psum")
        norm_ready = sem("norm_ready")
        pooled_ready = sem("pooled_ready")
        scaled_ready = sem("scaled_ready")
        bits_ready = sem("bits_ready")
        grid_ready = sem("grid_ready")
        lifted = sem("lifted")
        quant_ready = sem("quant_ready")
        quantT_psum = sem("quantT_psum")
        quantT_ready = sem("quantT_ready")
        ffn_psum = sem("ffn_psum")
        ffn_ready = sem("ffn_ready")
        ffn_sum_ready = sem("ffn_sum_ready")
        result_ready = sem("result_ready")
        result_stored = [sem(f"result_stored{i}") for i in range(2)]

        ZX, ZY, ZR, ZRN, SLOPE = range(5)
        lap = [bank[0], bank[1]]
        uT_bank = [bank[2], bank[3]]
        logit_bank = bank[4][:, 0:TB * E].rearrange("p (t e) -> p t e", e=E)
        rank_bank = bank[5][:, 0:E * NT].rearrange("p (e t) -> p e t", t=NT)
        total_bank = bank[6][:, 0:E * NT].rearrange("p (e t) -> p e t", t=NT)
        logitT_bank = bank[7][0:E, :]
        turn_bank = bank[0][:, 0:2 * NB].rearrange("p (v n) -> p v n", v=2)
        X_DMAS, W_DMAS, BIAS_DMAS, PLACE_DMAS = 5, 2, 2, 6
        N_CONST_A = 12
        N_Z = 9
        C_DMAS = 9
        GROUPS = 2 * NT // GT

        block = ctx.enter_context(nc.Block())

        @block.sync
        def _(sp):
            for i, z in enumerate((zx, zy, zr)):
                sp.dma_start(zs[:, i, :], z.partition_broadcast(P)).then_inc(z_loaded, 16)
            sp.dma_start(router_sb[:], router_w.rearrange("(k p) e -> p k e", p=P)).then_inc(router_loaded, 16)

            sp.dma_start(raw_gb[:], gate_up_b.rearrange("e (a f) -> (e a) f", a=P // E)).then_inc(bias_loaded, 16)
            sp.dma_start(raw_db[:], down_b.rearrange("e (a f) -> (e a) f", a=P // E)).then_inc(bias_loaded, 16)

            def load(n, s, k):
                sp.dma_start(X[:, ds(n * TB, TB), 0:H],
                             x_v[ds(n)].rearrange("b p t h -> (b p) t h")).then_inc(x_loaded[s], 16)
                wait_count(sp, lap_ready, 2 * (n - 1))
                for row, tiles, first in ((0, slice(0, 1), 1), (0, slice(1, TB), P - 1),
                                          (1, slice(0, TB - 1), P), (1, slice(TB - 1, TB), S - 2)):
                    count = tiles.stop - tiles.start
                    sp.dma_start(halo[row:row + 1, s, tiles, :],
                                 x[ds(n), first:first + 1 + P * (count - 1):P, :]).then_inc(x_loaded[s], 16)
                wait_count(sp, raw_used, 2 * n)
                sp.dma_start(raw_gu[:], gate_up_v[ds(n)].rearrange("e p k f -> (e p) k f")).then_inc(w_loaded, 16)
                sp.dma_start(raw_dn[:], down_v[ds(n)].rearrange("e p k h -> (e p) k h")).then_inc(w_loaded, 16)

            steps(sp, B, 2, load)
            sp.wait_ge(bias_step, 5)
            for half in range(2):
                for two in range(2):
                    part = E * GU // P // 2
                    sp.dma_start(gu_bias[half:half + 1, two].bitcast(F32).rearrange("r e i -> r (e i)"),
                                 flat_gb[:, half, two * part:(two + 1) * part].bitcast(F32)
                                 ).then_inc(bias_placed, 16)
                sp.dma_start(dn_bias[half:half + 1].bitcast(F32).rearrange("r e i -> r (e i)"),
                             flat_db[:, half, :].bitcast(F32)).then_inc(bias_placed, 16)

            for s in range(UNROLL):
                sp.wait_ge(outs_stored[s], 16 * (NB // UNROLL))
            for dst, src in ((w1_sb[:], w1.rearrange("(k p) a -> p k a", p=P)),
                             (b1_sb[:], b1.rearrange("(a o) -> a o", o=1)),
                             (v_sb[:], v.rearrange("(a o) -> a o", o=1)),
                             (kind_i[:], kinds.rearrange("(b o) -> b o", o=1)),
                             (kind_row_i[:, 0, :], kinds.rearrange("(o b) -> o b", o=1)),
                             (k_raw[:], ffn_k.rearrange("(k p) f -> p k f", p=P)),
                             (scales[:, 0:1], in_scale.partition_broadcast(P)),
                             (scales[:, 1:2], k_scale.partition_broadcast(P)),
                             (bias_f[:], ffn_b.partition_broadcast(P))):
                sp.dma_start(dst, src).then_inc(c_loaded, 16)

            def load_y(n, s, k):
                wait_count(sp, mixed, n - 1)
                for c in range(2):
                    sp.dma_start(picks[:, s, c], y_v[c, ds(n)].rearrange("b p t h -> (b p) t h")).then_inc(y_loaded[s], 16)
                if (last := earlier(n, s, k, 1, 2)) is not None:
                    keep(*last)

            def keep(n, s, k):
                sp.wait_ge(xT_psum, 2 * n + 2)
                sp.dma_start(X[:, ds(n * TB, TB), 0:H], mix[:, s]).then_inc(mixed_kept[s], 16)
                sp.wait_ge(row_ready, n + 1)
                sp.dma_start(score_rows[ds(n), :], score_row[0:1, s, :]).then_inc(row_stored[s], 16)

            steps(sp, B, 2, load_y)
            keep(B - 1, 1, 0)
            for s in range(2):
                sp.wait_ge(row_stored[s], 16 * (B // 2))
            sp.dma_start(scores[:], score_rows).then_inc(scores_loaded, 16)
            sp.wait_ge(max_ready, 1)
            sp.dma_start(max_rows, row_max[:]).then_inc(max_stored, 16)
            sp.wait_ge(max_stored, 16)

            def spread_max(n, s, k):
                wait_count(sp, expo_ready, TB * (n - 1))
                sp.dma_start(neg_max[:, s, :],
                             max_rows[ds(n), :].rearrange("b s -> (b s)").partition_broadcast(P)).then_inc(max_loaded[s], 16)

            steps(sp, B, 2, spread_max)

        @block.gpsimd
        def _(pool):
            pool.memset(ident[:], 0.0).then_inc(pool_const, 1)
            pool.memset(diff[:], 0.0).then_inc(pool_const, 1)
            pool.memset(edge[:], 0.0).then_inc(pool_const, 1)
            pool.memset(ones_b[:], 1.0).then_inc(pool_const, 1)
            pool.iota(column_i[:], [[1, P]], base=0, channel_multiplier=0).then_inc(pool_const, 1)
            pool.iota(slot_i[:, 2], [[NT, 2], [1, NT]], base=0, channel_multiplier=0).then_inc(pool_const, 1)
            pool.iota(row_i[:], [[0, 1]], base=0, channel_multiplier=1).then_inc(pool_const, 1)
            pool.iota(blk_i[:], [[P, NB]], base=0, channel_multiplier=0).then_inc(pool_const, 1)
            pool.wait_ge(pool_const, 8)
            pool.affine_select(out=ident[:], in_=ident[:], compare_op=ALU.not_equal, fill=1.0, base=0,
                               pattern=[[-1, P]], channel_multiplier=1).then_inc(pool_const, 1)
            pool.affine_select(out=above[:], in_=ones_b[:], compare_op=ALU.is_gt, fill=0.0, base=0,
                               pattern=[[1, P]], channel_multiplier=-1).then_inc(pool_const, 1)
            pool.affine_select(out=edge[:], in_=edge[:], compare_op=ALU.not_equal, fill=1.0, base=0,
                               pattern=[[-1, P]], channel_multiplier=P - 1).then_inc(pool_const, 1)
            for i, (base, fill) in enumerate(((0, -2.0), (1, 1.0), (-1, 1.0))):
                wait_count(pool, diff_step, i)
                pool.affine_select(out=diff[:], in_=diff[:], compare_op=ALU.not_equal, fill=fill, base=base,
                                   pattern=[[-1, P]], channel_multiplier=1).then_inc(diff_step, 1)
            pool.memset(X[:, :, H:H + 1], 1.0).then_inc(pool_const, 1)

            def step_a(n, s, k):
                pool.wait_ge(x_loaded[s], 16 * X_DMAS * (k + 1))
                wait_count(pool, u_ready, n - 1)
                xn = X[:, ds(n * TB, TB), :]
                pool.tensor_tensor(pair[:, s, :, 1:H - 1], xn[:, :, 0:H - 2], xn[:, :, 2:H],
                                   ALU.add).then_inc(pair_ready, 1)
                pool.tensor_tensor(pair[:, s, :, 0:H:H - 1], xn[:, :, 1:H - 1:H - 3], xn[:, :, 1:H - 1:H - 3],
                                   ALU.add).then_inc(pair_ready, 1)
                pool.wait_ge(hi_ready, 2 * n + 2)
                pool.tensor_tensor(dn_lo[:, ds(n)].rearrange("p e k h -> p (e k) h"), raw_dn[:],
                                   dn_hi[:, ds(n)].bitcast(F32).rearrange("p e k h -> p (e k) h"),
                                   ALU.subtract).then_inc(raw_used, 1)

            steps(pool, B, 2, step_a)

            for g in range(GROUPS):
                pool.wait_ge(is_b_ready, 2 * g + 1)
                wait_count(pool, turned, g - 1)
                pool.tensor_tensor(is_b_of[:, g % 2, :, 1, :], is_b[:, g % 2],
                                   tile_no[:, g * GT:(g + 1) * GT].unsqueeze(2).broadcast_to([P, GT, NB]),
                                   ALU.mult).then_inc(is_b_tile, 1)

            pool.wait_ge(slots_ready, 2)
            for s in range(2):
                pool.wait_ge(u_kept[s], 16 * (B // 2))
            AHEAD = 2 * UNROLL
            for n in range(NB + AHEAD):
                if n < NB:
                    s = n % UNROLL
                    wait_count(pool, rowT_psum, n - UNROLL + 1)
                    pool.indirect_dma_start(
                        out=rows[:, s, :], out_offset=None, in_=u_rows,
                        in_offset=bass.IndirectOffsetOnAxis(ap=slot_src[:, n:n + 1], axis=0),
                    ).then_inc(rows_loaded[s], 16)
                m = n - AHEAD
                if m >= 0:
                    pool.wait_ge(outs_ready, m + 1)
                    pool.indirect_dma_start(
                        out=y_rows, out_offset=bass.IndirectOffsetOnAxis(ap=slot_dst[:, m:m + 1], axis=0),
                        in_=outs[:, m % UNROLL, :], in_offset=None, bounds_check=2 * T - 1,
                        oob_is_err=False).then_inc(outs_stored[m % UNROLL], 16)

            for s in range(UNROLL):
                pool.wait_ge(outs_stored[s], 16 * (NB // UNROLL))
            pool.memset(masks[:], 0.0).then_inc(tables, 1)
            pool.memset(ident_b[:], 0.0).then_inc(tables, 1)
            pool.iota(counts_i[:], [[P, TB]], base=1, channel_multiplier=1).then_inc(tables, 1)
            pool.wait_ge(tables, 3)
            for i, (op, sign) in enumerate(((ALU.is_ge, 1), (ALU.is_ge, -1), (ALU.not_equal, 1))):
                pool.affine_select(out=masks[:, i], in_=masks[:, i], compare_op=op, fill=NEG,
                                   base=sign * (P - S), pattern=[[sign, MW]],
                                   channel_multiplier=-sign).then_inc(tables, 1)
            pool.affine_select(out=ident_b[:], in_=ident_b[:], compare_op=ALU.not_equal, fill=1.0, base=0,
                               pattern=[[-1, P]], channel_multiplier=1).then_inc(tables, 1)

            def step_c(n, s, k):
                if (last := earlier(n, s, k, 1, 2)) is not None:
                    add_bias(*last)
                pool.wait_ge(grid_ready, n + 1)
                pool.tensor_tensor(scaled[:], scaled[:], grid[:], ALU.add).then_inc(lifted, 1)
                pool.wait_ge(lifted, n + 1)
                wait_count(pool, quantT_psum, n)
                pool.tensor_tensor(quant[:], scaled[:], grid[:], ALU.subtract).then_inc(quant_ready, 1)

            def add_bias(n, s, k):
                pool.wait_ge(ffn_ready, 2 * n + 2)
                wait_count(pool, result_ready, n)
                pool.tensor_tensor(ffn_sum[:], ffn[:], bias_f[:].unsqueeze(1).broadcast_to([P, TB, F]),
                                   ALU.add).then_inc(ffn_sum_ready, 1)

            steps(pool, B, 2, step_c)
            add_bias(B - 1, 1, 0)

        @block.scalar
        def _(a):
            def step_a(n, s, k):
                a.wait_ge(w_loaded, 16 * W_DMAS * (n + 1))
                a.activation(gu_hi[:, ds(n)].rearrange("p e k (two i) -> p (e k) two i", two=2),
                             raw_gu[:].rearrange("p k (i two) -> p k two i", two=2), ACT.Copy).then_inc(hi_ready, 1)
                a.activation(dn_hi[:, ds(n)].rearrange("p e k h -> p (e k) h"), raw_dn[:],
                             ACT.Copy).then_inc(hi_ready, 1)
                a.wait_ge(u_ready, n + 1)
                a.dma_start(u_v[ds(n)].rearrange("b p t h -> (b p) t h"), flow[:, s]).then_inc(u_kept[s], 16)
                transposed(n)

            def transposed(n):
                wait_count(a, logitsT_psum, n)
                for half in range(KH):
                    a.wait_ge(uT_psum, 2 * n + half + 1)
                    a.activation(uT[:, half], uT_bank[half][:], ACT.Copy).then_inc(uT_ready, 1)
                a.wait_ge(logitsT_psum, n + 1)
                wait_count(a, logits_psum, n)
                a.activation(logitsT[:], logitT_bank, ACT.Copy).then_inc(logitsT_ready, 1)

            steps(a, B, 2, step_a)
            a.wait_ge(gap_ready, 1)
            a.activation(odds[:, 1], odds[:, 0], ACT.Exp).then_inc(odds_ready, 1)

            a.wait_ge(slots_ready, 2)

            def rows_rounded(n, s, k):
                d = s % 2
                a.wait_ge(rowT_psum, n + 1)
                wait_count(a, gu_psum, n - 1)
                a.activation(rowT_hi[:, d], bank[2 + d][:, 0:KH * P].rearrange("p (k n) -> p k n", k=KH),
                             ACT.Copy).then_inc(rowT_hi_ready, 1)

            def step_b(n, s, k):
                if (last := earlier(n, s, k, 2, UNROLL)) is not None:
                    transposed_act(*last)
                if (after := later(n, s, k, UNROLL, NB)) is not None:
                    rows_rounded(*after)
                if (last := earlier(n, s, k, 3, UNROLL)) is not None:
                    finish_down(*last)
                activate(n, s, k)

            def activate(n, s, k):
                a.wait_ge(gate_ready, n + 1)
                wait_count(a, act_ready, n - 1)
                a.activation(tanh[:, s % 2], gate[:, s % 2], ACT.Tanh, scale=ALPHA).then_inc(tanh_ready, 1)

            def transposed_act(n, s, k):
                a.wait_ge(actT_psum, n + 1)
                wait_count(a, down_psum, n - 1)
                a.activation(actT_hi[:, s % 2],
                             bank[4 + s % 2][:, 0:KI * P].rearrange("p (k n) -> p k n", k=KI),
                             ACT.Copy).then_inc(actT_hi_ready, 1)

            def finish_down(n, s, k):
                a.wait_ge(down_psum, n + 1)
                if not (isinstance(n, int) and n < UNROLL):
                    a.wait_ge(outs_stored[s], 16 * k)
                a.activation(outs[:, s, :], bank[6 + s % 2][:, 0:H], ACT.Copy).then_inc(outs_ready, 1)

            rows_rounded(0, 0, 0)
            K = steps_peeled(a, NB, UNROLL, step_b)
            transposed_act(NB - 2, UNROLL - 2, K)
            finish_down(NB - 3, UNROLL - 3, K)
            finish_down(NB - 2, UNROLL - 2, K)
            transposed_act(NB - 1, UNROLL - 1, K)
            finish_down(NB - 1, UNROLL - 1, K)

            a.wait_ge(c_loaded, 16 * C_DMAS)

            def scores_of(n, s, k):
                for half in range(KH):
                    a.wait_ge(xT_psum, 2 * n + half + 1)
                    wait_count(a, hidden_psum, n)
                    a.activation(xT[:, half], bank[half][:], ACT.Copy).then_inc(xT_ready, 1)
                a.wait_ge(hidden_psum, n + 1)
                wait_count(a, score_psum, n)
                a.activation(hidden[:], bank[2][0:A, :], ACT.Tanh, bias=b1_sb[:, 0:1]).then_inc(hidden_ready, 1)

            steps(a, B, 2, scores_of)

            def pool_of(n, s, k):
                for l in range(TB):
                    a.wait_ge(expo_ready, TB * n + l + 1)
                    wait_count(a, pool_psum, TB * (n - 1))
                    a.activation(probs[:, s, l], expo[:, l % 2], ACT.Exp,
                                 bias=score_col[:, l, ds(n)]).then_inc(probs_ready, 1)
                if (last := earlier(n, s, k, 1, 2)) is not None:
                    finish(*last)
                if (last := earlier(n, s, k, 2, 2)) is not None:
                    store(*last)

            def finish(n, s, k):
                a.wait_ge(quantT_psum, n + 1)
                wait_count(a, ffn_psum, 2 * n)
                a.activation(quantT[:], bank[4][:].bitcast(BF16).rearrange("p (k n) -> p k n", k=KH),
                             ACT.Copy).then_inc(quantT_ready, 1)
                wait_count(a, ffn_sum_ready, n)
                for g in range(2):
                    a.wait_ge(ffn_psum, 2 * n + g + 1)
                    a.activation(ffn[:, 2 * g:2 * g + 2, :], bank[5 + g][:].rearrange("p (t f) -> p t f", f=F),
                                 ACT.Copy, scale=scales[:, 2:3]).then_inc(ffn_ready, 1)

            def store(n, s, k):
                a.wait_ge(result_ready, n + 1)
                a.dma_start(out_v[ds(n)].rearrange("b p t h -> (b p) t h"), result[:, s]).then_inc(result_stored[s], 16)

            steps(a, B, 2, pool_of)
            store(B - 2, 0, 0)
            finish(B - 1, 1, 0)
            store(B - 1, 1, 0)
            for s in range(2):
                a.wait_ge(result_stored[s], 16 * (B // 2))

        @block.tensor
        def _(pe):
            def step_a(n, s, k):
                pe.wait_ge(x_loaded[s], 16 * X_DMAS * (k + 1))
                pe.wait_ge(matrix_ready, 2 * n + 2)
                wait_count(pe, u_ready, n)
                wait_count(pe, logitsT_ready, n - 1)
                wait_count(pe, logits_ready, n - 2)
                for g in range(2):
                    pe.matmul(lap[g][:], diff_n[:, s], X[:, ds(n * TB + 2 * g, 2), 0:H], start=True, stop=False)
                    pe.matmul(lap[g][:], edge_n[:, s], halo[:, s, 2 * g:2 * g + 2, :], start=False,
                              stop=True).then_inc(lap_ready, 1)
                if (last := earlier(n, s, k, 2, 2)) is not None:
                    logits_transposed(*last)
                if (last := earlier(n, s, k, 1, 2)) is not None:
                    route(*last)

            def route(n, s, k):
                pe.wait_ge(u_ready, n + 1)
                wait_count(pe, uT_ready, 2 * n)
                for half in range(KH):
                    for t in range(TB):
                        mm = pe.transpose(uT_bank[half][:, t * P:(t + 1) * P],
                                          flow[:, s, t, half * P:(half + 1) * P], ident[:])
                    mm.then_inc(uT_psum, 1)
                pe.wait_ge(uT_ready, 2 * n + 2)
                wait_count(pe, logitsT_ready, n)
                for half in range(KH):
                    mm = pe.matmul(logitT_bank, router_sb[:, half, :], uT[:, half, :],
                                   start=(half == 0), stop=(half == KH - 1))
                mm.then_inc(logitsT_psum, 1)

            def logits_transposed(n, s, k):
                for t in range(TB):
                    mm = pe.transpose(logit_bank[:, t, :], logitsT[:, t * P:(t + 1) * P], ident[0:E, 0:E])
                mm.then_inc(logits_psum, 1)

            pe.wait_ge(pool_const, N_CONST_A)
            pe.wait_ge(router_loaded, 16)
            steps(pe, B, 2, step_a)
            pe.wait_ge(logitsT_ready, B - 1)
            pe.wait_ge(logits_ready, B - 2)
            logits_transposed(B - 2, 0, 0)
            route(B - 1, 1, 0)
            pe.wait_ge(logitsT_ready, B)
            pe.wait_ge(logits_ready, B - 1)
            logits_transposed(B - 1, 1, 0)
            pe.wait_ge(picked_ready, 1)
            pe.matmul(rank_bank, above[:], picked[:], start=True, stop=True)
            pe.matmul(total_bank, ones_b[:], picked[:], start=True, stop=True).then_inc(ranks_ready, 1)
            for g in range(GROUPS):
                pe.wait_ge(is_q_ready, g + 1)
                pe.wait_ge(is_b_ready, 2 * g + 2)
                pe.wait_ge(is_b_tile, g + 1)
                for j in range(GT):
                    mm = pe.matmul(turn_bank, is_q[:, g % 2, j, :], is_b_of[:, g % 2, j],
                                   start=(g == 0 and j == 0), stop=(g == GROUPS - 1 and j == GT - 1))
                mm.then_inc(turned, 1)

            def rows_transposed(n, s, k):
                pe.wait_ge(rows_loaded[s], 16 * (k + 1))
                wait_count(pe, rowT_lo_ready, n - 1)
                for half in range(KH):
                    mm = pe.transpose(bank[2 + s % 2][:, half * P:(half + 1) * P],
                                      rows[:, s, half * P:(half + 1) * P], ident[:])
                mm.then_inc(rowT_psum, 1)

            def split_product(acc, hi, lo, w_hi, w_lo, bias, expert, parts):
                pe.matmul(acc, ones2[:], bias, start=True, stop=False)
                for part in range(parts):
                    for left, right in ((hi, w_hi), (hi, w_lo), (lo, w_hi)):
                        mm = pe.matmul(acc, left[:, part, :],
                                       right[:, ds(expert), part, :].rearrange("p e f -> p (e f)"),
                                       start=False, stop=(part == parts - 1 and left is lo))
                return mm

            def gate_up(n, s, k):
                d = s % 2
                expert = pe.value_load(block_expert[0:1, ds(n)], min_val=0, max_val=E - 1)
                pe.wait_ge(rowT_hi_ready, n + 1)
                pe.wait_ge(rowT_lo_ready, n + 1)
                wait_count(pe, up_ready, n - 1)
                split_product(bank[d][:], rowT_hi[:, d], rowT_lo[:, d], gu_hi, gu_lo,
                              gu_bias[:, :, ds(expert), :].rearrange("r two e i -> r two (e i)"), expert, KH).then_inc(gu_psum, 1)

            def act_transposed(n, s, k):
                d = s % 2
                pe.wait_ge(act_ready, n + 1)
                wait_count(pe, actT_lo_ready, n - 1)
                for half in range(KI):
                    mm = pe.transpose(bank[4 + d][:, half * P:(half + 1) * P],
                                      act[:, d, half * P:(half + 1) * P], ident[:])
                mm.then_inc(actT_psum, 1)

            def down(n, s, k):
                d = s % 2
                expert = pe.value_load(block_expert[0:1, ds(n)], min_val=0, max_val=E - 1)
                pe.wait_ge(actT_hi_ready, n + 1)
                pe.wait_ge(actT_lo_ready, n + 1)
                wait_count(pe, outs_ready, n - 1)
                split_product(bank[6 + d][:, 0:H], actT_hi[:, d], actT_lo[:, d], dn_hi, dn_lo,
                              dn_bias[:, ds(expert), :].rearrange("r e h -> r (e h)"), expert, KI).then_inc(down_psum, 1)

            def step_b(n, s, k):
                if (after := later(n, s, k, UNROLL, NB)) is not None:
                    rows_transposed(*after)
                gate_up(n, s, k)
                for back, then in ((2, down), (1, act_transposed)):
                    if (last := earlier(n, s, k, back, UNROLL)) is not None:
                        then(*last)

            pe.wait_ge(experts_ready, 1)
            pe.wait_ge(slots_ready, 2)
            pe.wait_ge(bias_placed, 16 * PLACE_DMAS)
            rows_transposed(0, 0, 0)
            K = steps_peeled(pe, NB, UNROLL, step_b)
            down(NB - 2, UNROLL - 2, K)
            act_transposed(NB - 1, UNROLL - 1, K)
            down(NB - 1, UNROLL - 1, K)

            def scores_of(n, s, k):
                pe.wait_ge(mixed, n + 1)
                for half in range(KH):
                    wait_count(pe, xT_ready, 2 * n - 1 + half)
                    for t in range(TB):
                        mm = pe.transpose(bank[half][:, t * P:(t + 1) * P],
                                          mix[:, s, t, half * P:(half + 1) * P], ident[:])
                    mm.then_inc(xT_psum, 1)
                pe.wait_ge(xT_ready, 2 * n + 2)
                wait_count(pe, hidden_ready, n)
                for half in range(KH):
                    mm = pe.matmul(bank[2][0:A, :], w1_sb[:, half, :], xT[:, half, :],
                                   start=(half == 0), stop=(half == KH - 1))
                mm.then_inc(hidden_psum, 1)
                pe.wait_ge(hidden_ready, n + 1)
                wait_count(pe, col_ready, n)
                wait_count(pe, row_ready, n)
                for t in range(TB):
                    pe.matmul(bank[4][:, t:t + 1], hidden[:, t * P:(t + 1) * P], v_sb[:],
                              start=True, stop=True)
                pe.matmul(bank[3][0:1, :], v_sb[:], hidden[:], start=True,
                          stop=True).then_inc(score_psum, 1)

            pe.wait_ge(outs_ready, NB)
            pe.wait_ge(c_loaded, 16 * C_DMAS)
            steps(pe, B, 2, scores_of)

            def pool_of(n, s, k):
                pe.wait_ge(probs_ready, TB * (n + 1))
                for j in range(TB):
                    wait_count(pe, pooled_ready, TB * (n - 1) + j + 1)
                    for l in range(TB):
                        mm = pe.matmul(bank[j][:, 0:H + 1], probs[:, s, l, j * P:(j + 1) * P],
                                       X[:, ds(n * TB + l), :].rearrange("p t h -> p (t h)"),
                                       start=(l == 0), stop=(l == TB - 1))
                    mm.then_inc(pool_psum, 1)
                if (last := earlier(n, s, k, 1, 2)) is not None:
                    finish(*last)

            def finish(n, s, k):
                pe.wait_ge(quant_ready, n + 1)
                wait_count(pe, quantT_ready, n)
                qT = bank[4][:].bitcast(BF16)
                for half in range(KH):
                    for t in range(TB):
                        mm = pe.transpose(qT[:, half * S + t * P:half * S + (t + 1) * P],
                                          quant[:, t, half * P:(half + 1) * P], ident_b[:])
                mm.then_inc(quantT_psum, 1)
                pe.wait_ge(quantT_ready, n + 1)
                wait_count(pe, ffn_ready, 2 * n)
                for t in range(TB):
                    for half in range(KH):
                        mm = pe.matmul(bank[5 + t // 2][:, (t % 2) * F:(t % 2 + 1) * F],
                                       quantT[:, half, t * P:(t + 1) * P], k_quant[:, half, :],
                                       start=(half == 0), stop=(half == KH - 1))
                    if t % 2:
                        mm.then_inc(ffn_psum, 1)

            for s in range(2):
                pe.wait_ge(mixed_kept[s], 16 * (B // 2))
            pe.wait_ge(table_step, 6)
            pe.wait_ge(col_ready, B)
            pe.wait_ge(row_ready, B)
            pe.wait_ge(tables, 7)
            steps(pe, B, 2, pool_of)
            finish(B - 1, 1, 0)

        @block.vector
        def _(dve):
            dve.wait_ge(z_loaded, 48)
            dve.tensor_scalar(zs[:, ZRN, :], zs[:, ZR, :], -1.0, None, ALU.mult).then_inc(z_step, 1)
            dve.scalar_tensor_tensor(out=zs[:, SLOPE, :], in0=zs[:, ZX, :], scalar=-2.0, in1=zs[:, ZR, :],
                                     op0=ALU.mult, op1=ALU.add).then_inc(z_step, 1)
            dve.wait_ge(pool_const, 8)
            dve.tensor_copy(row_f[:], row_i[:]).then_inc(z_step, 1)
            dve.tensor_copy(expert_f[:], column_i[:, 0:E]).then_inc(z_step, 1)
            dve.tensor_copy(blk_f[:], blk_i[:]).then_inc(z_step, 1)
            dve.wait_ge(z_step, 5)
            dve.tensor_scalar(row_one[:], row_f[:], 1.0, None, ALU.add).then_inc(z_step, 1)
            dve.tensor_copy(column[:], column_i[:]).then_inc(z_step, 1)
            dve.tensor_copy(tile_no[:], slot_i[:, 2].rearrange("p c t -> p (c t)")).then_inc(z_step, 1)
            dve.memset(follow[:], 1.0).then_inc(z_step, 1)
            dve.wait_ge(z_step, N_Z)
            dve.memset(follow[:, :, 0:1], 0.0).then_inc(z_step, 1)
            dve.memset(ones2[:].bitcast(F32), 1.0).then_inc(z_step, 1)
            dve.wait_ge(z_step, N_Z + 2)
            dve.wait_ge(diff_step, 3)
            dve.wait_ge(pool_const, N_CONST_A)
            dve.wait_ge(bias_loaded, 16 * BIAS_DMAS)
            dve.tensor_scalar(raw_gb[:, 1:E * GU // P:2], raw_gb[:, 1:E * GU // P:2], 1.0, None,
                              ALU.add).then_inc(bias_step, 1)
            dve.tensor_copy(flat_db[:, 0, :], raw_db[:]).then_inc(bias_step, 1)
            dve.wait_ge(bias_step, 2)
            mixed_gb = raw_gb[:].rearrange("p (i two) -> p two i", two=2)
            flat = lambda i: flat_gb[:, i, :].rearrange("p (two i) -> p two i", two=2)
            dve.tensor_copy(flat(0), mixed_gb).then_inc(bias_step, 1)
            dve.tensor_tensor(flat_db[:, 1, :], raw_db[:], flat_db[:, 0, :].bitcast(F32),
                              ALU.subtract).then_inc(bias_step, 1)
            dve.wait_ge(bias_step, 4)
            dve.tensor_tensor(flat(1), mixed_gb, flat(0).bitcast(F32), ALU.subtract).then_inc(bias_step, 1)

            def matrices(n, s, k):
                wait_count(dve, lap_ready, 2 * (n - 1))
                dve.tensor_scalar(slant[:, s], ident[:], zs[:, SLOPE, ds(n)], None, ALU.mult).then_inc(matrix_step, 1)
                dve.wait_ge(matrix_step, n + 1)
                dve.scalar_tensor_tensor(out=diff_n[:, s], in0=diff[:], scalar=zs[:, ZY, ds(n)],
                                         in1=slant[:, s], op0=ALU.mult, op1=ALU.add).then_inc(matrix_ready, 1)
                dve.tensor_scalar(edge_n[:, s], edge[:], zs[0:2, ZY, ds(n)], None,
                                  ALU.mult).then_inc(matrix_ready, 1)

            def step_a(n, s, k):
                if isinstance(n, int) and n == 0:
                    matrices(0, 0, 0)
                u = flow[:, s]
                xn = X[:, ds(n * TB, TB), 0:H]
                dve.wait_ge(x_loaded[s], 16 * X_DMAS * (k + 1))
                if not (isinstance(n, int) and n < 2):
                    dve.wait_ge(u_kept[s], 16 * k)
                    dve.wait_ge(uT_psum, 2 * n - 2)
                dve.scalar_tensor_tensor(out=u, in0=xn, scalar=zs[:, ZRN, ds(n)], in1=xn, op0=ALU.mult,
                                         op1=ALU.mult).then_inc(flow_step, 1)
                if (after := later(n, s, k, 2, B)) is not None:
                    matrices(*after)
                dve.wait_ge(pair_ready, 2 * n + 2)
                dve.wait_ge(flow_step, 2 * n + 1)
                dve.scalar_tensor_tensor(out=u, in0=pair[:, s], scalar=zs[:, ZX, ds(n)], in1=u, op0=ALU.mult,
                                         op1=ALU.add).then_inc(flow_step, 1)
                dve.wait_ge(flow_step, 2 * n + 2)
                dve.wait_ge(lap_ready, 2 * n + 2)
                for g in range(2):
                    ug = u[:, 2 * g:2 * g + 2, :]
                    op = dve.tensor_tensor(ug, lap[g][:].rearrange("p (t h) -> p t h", h=H), ug, ALU.add)
                op.then_inc(u_ready, 1)
                dve.wait_ge(hi_ready, 2 * n + 2)
                dve.tensor_tensor(gu_lo[:, ds(n)].rearrange("p e k (two i) -> p (e k) two i", two=2),
                                  raw_gu[:].rearrange("p k (i two) -> p k two i", two=2),
                                  gu_hi[:, ds(n)].bitcast(F32).rearrange("p e k (two i) -> p (e k) two i", two=2),
                                  ALU.subtract).then_inc(raw_used, 1)
                if (last := earlier(n, s, k, 2, 2)) is not None:
                    best_two(*last)

            def best_two(n, s, k):
                dve.wait_ge(logits_psum, n + 1)
                dve.tensor_copy(logits[:], logit_bank).then_inc(logits_ready, 1)
                wait_alone(dve, logits_ready, n + 1, z_step, N_Z)
                for t in range(TB):
                    op = dve.max(best[:, t], logits[:, t])
                op.then_inc(best_step, 1)
                wait_alone(dve, best_step, n + 1, z_step, N_Z)
                for t in range(TB):
                    op = dve.max_index(best_i[:, t], best[:, t], logits[:, t])
                op.then_inc(index_step, 1)
                dve.wait_ge(index_step, n + 1)
                dve.tensor_copy(top[:, ds(n * TB, TB), :], best[:, :, 0:2]).then_inc(top_ready, 1)
                dve.tensor_copy(top_i[:, ds(n * TB, TB), :], best_i[:, :, 0:2]).then_inc(top_ready, 1)

            K = steps_peeled(dve, B, 2, step_a)
            best_two(B - 2, 0, K)
            best_two(B - 1, 1, K)

            done = [0]

            def then(instruction):
                done[0] += 1
                instruction.then_inc(route_step, 1)
                dve.wait_ge(route_step, done[0])

            dve.wait_ge(top_ready, 2 * B)
            dve.tensor_tensor(odds[:, 0], top[:, :, 1], top[:, :, 0], ALU.subtract).then_inc(gap_ready, 1)
            for c in range(2):
                op = dve.tensor_tensor(pick[:, c], expert_f[:].unsqueeze(2).broadcast_to([P, E, NT]),
                                       top_i[:, :, c].unsqueeze(1).broadcast_to([P, E, NT]), ALU.is_equal)
            then(op)
            dve.tensor_tensor(picked[:], pick[:, 0], pick[:, 1], ALU.add).then_inc(picked_ready, 1)
            dve.wait_ge(ranks_ready, 1)
            then(dve.tensor_copy(totals[:], total_bank))
            flat = lambda m: m[:].rearrange("p e t -> p (e t)")
            then(dve.tensor_tensor_scan(flat(upto), flat(follow), flat(totals), 0.0, ALU.mult, ALU.add))
            COUNT, PADDED, END, FILLED, ONE = range(5)
            ends_of = lambda i: ends[:, i, :]
            dve.tensor_copy(ends_of(COUNT), upto[:, :, NT - 1])
            then(dve.memset(ends_of(ONE), 1.0))
            then(dve.tensor_scalar(ends_i[:, 0, :], ends_of(COUNT), float(P - 1), None, ALU.add))
            then(dve.tensor_scalar(ends_i[:, 1, :], ends_i[:, 0, :], 7, 7, ALU.logical_shift_right,
                                   ALU.logical_shift_left))
            then(dve.tensor_copy(ends_of(PADDED), ends_i[:, 1, :]))
            then(dve.tensor_tensor_scan(ends_of(END), ends_of(ONE), ends_of(PADDED), 0.0, ALU.mult, ALU.add))
            then(dve.tensor_tensor(ends_of(PADDED), ends_of(END), ends_of(PADDED), ALU.subtract))
            then(dve.tensor_tensor(ends_of(FILLED), ends_of(PADDED), ends_of(COUNT), ALU.add))
            then(dve.tensor_tensor(upto[:], upto[:], totals[:], ALU.subtract))
            then(dve.tensor_tensor(upto[:], upto[:], rank_bank, ALU.add))
            then(dve.tensor_tensor(upto[:], upto[:], ends_of(PADDED).unsqueeze(2).broadcast_to([P, E, NT]),
                                   ALU.add))
            for c in range(2):
                op = dve.tensor_tensor(pick[:, c], pick[:, c], upto[:], ALU.mult)
            then(op)
            for c in range(2):
                op = dve.tensor_reduce(slot_f[:, c, :], pick[:, c].rearrange("p e t -> p t e"), AX.X, ALU.add)
            then(op)
            then(dve.tensor_copy(slot_i[:, 0], slot_f[:]))
            dve.tensor_scalar(slot_i[:, 1], slot_i[:, 0], P - 1, None, ALU.bitwise_and)
            then(dve.tensor_scalar(slot_i[:, 2], slot_i[:, 0], 7, None, ALU.logical_shift_right))
            dve.tensor_copy(slot_q[:], slot_i[:, 1])
            then(dve.tensor_copy(slot_b[:], slot_i[:, 2]))
            q_all, b_all = (m[:].rearrange("p c t -> p (c t)") for m in (slot_q, slot_b))
            for g in range(GROUPS):
                d, tiles = g % 2, slice(g * GT, (g + 1) * GT)
                wait_count(dve, turned, g - 1)
                dve.tensor_tensor(is_b[:, d], column[:, 0:NB].unsqueeze(1).broadcast_to([P, GT, NB]),
                                  b_all[:, tiles].unsqueeze(2).broadcast_to([P, GT, NB]),
                                  ALU.is_equal).then_inc(is_b_ready, 1)
                dve.tensor_tensor(is_q[:, d], column[:].unsqueeze(1).broadcast_to([P, GT, P]),
                                  q_all[:, tiles].unsqueeze(2).broadcast_to([P, GT, P]),
                                  ALU.is_equal).then_inc(is_q_ready, 1)
                dve.wait_ge(is_b_ready, 2 * g + 1)
                dve.tensor_scalar(is_b_of[:, d, :, 0, :], is_b[:, d], row_one[:, 0:1], None,
                                  ALU.mult).then_inc(is_b_ready, 1)
            then(dve.tensor_tensor(blk_past, blk_f[:].unsqueeze(2).broadcast_to([1, NB, E]),
                                   ends[0:1, END, :].unsqueeze(1).broadcast_to([1, NB, E]), ALU.is_ge))
            then(dve.tensor_reduce(blk_e[:], blk_past, AX.X, ALU.add))
            dve.tensor_scalar(block_expert[:], blk_e[:], float(E - 1), None, ALU.min).then_inc(experts_ready, 1)
            NUMBER, OUTSIDE, SECOND, ROW = range(4)
            dve.wait_ge(turned, GROUPS)
            then(dve.tensor_copy(pair_no[:, ROW], turn_bank[:, 0, :]))
            then(dve.scalar_tensor_tensor(out=pair_no[:, NUMBER], in0=turn_bank[:, 1, :], scalar=float(P),
                                          in1=pair_no[:, ROW], op0=ALU.mult, op1=ALU.add))
            dve.tensor_scalar(pair_no[:, OUTSIDE], pair_no[:, NUMBER], 1.0, ROW_BIG, ALU.is_lt, ALU.mult)
            then(dve.tensor_scalar(pair_no[:, SECOND], pair_no[:, NUMBER], float(T) + 0.5, -float(T),
                                   ALU.is_gt, ALU.mult))
            dve.scalar_tensor_tensor(out=slot_dst[:], in0=pair_no[:, NUMBER], scalar=-1.0,
                                     in1=pair_no[:, OUTSIDE], op0=ALU.add,
                                     op1=ALU.add).then_inc(slots_ready, 1)
            then(dve.scalar_tensor_tensor(out=pair_no[:, ROW], in0=pair_no[:, NUMBER], scalar=-1.0,
                                          in1=pair_no[:, SECOND], op0=ALU.add, op1=ALU.add))
            dve.tensor_scalar(slot_src[:], pair_no[:, ROW], 0.0, None, ALU.max).then_inc(slots_ready, 1)
            dve.wait_ge(odds_ready, 1)
            then(dve.tensor_scalar(odds[:, 2], odds[:, 1], 1.0, None, ALU.add))
            then(dve.reciprocal(tok_w[:, 0, :], odds[:, 2]))
            then(dve.tensor_tensor(tok_w[:, 1, :], odds[:, 1], tok_w[:, 0, :], ALU.mult))

            def rows_low(n, s, k):
                d = s % 2
                dve.wait_ge(rowT_hi_ready, n + 1)
                wait_count(dve, gu_psum, n - 1)
                dve.tensor_tensor(rowT_lo[:, d], bank[2 + d][:, 0:KH * P].rearrange("p (k n) -> p k n", k=KH),
                                  rowT_hi[:, d].bitcast(F32), ALU.subtract).then_inc(rowT_lo_ready, 1)

            def step_b(n, s, k):
                if (last := earlier(n, s, k, 2, UNROLL)) is not None:
                    act_low(*last)
                if (after := later(n, s, k, UNROLL, NB)) is not None:
                    rows_low(*after)
                if (last := earlier(n, s, k, 1, UNROLL)) is not None:
                    activated(*last)
                clip(n, s, k)

            def clip(n, s, k):
                d = s % 2
                dve.wait_ge(gu_psum, n + 1)
                wait_count(dve, act_ready, n - 1)
                dve.tensor_scalar(gate[:, d], bank[d][:, 0:I], LIMIT, 0.5, ALU.min,
                                  ALU.mult).then_inc(gate_ready, 1)
                dve.tensor_scalar(up[:, d], bank[d][:, I:GU], LIMIT + 1.0, 1.0 - LIMIT, ALU.min,
                                  ALU.max).then_inc(up_ready, 1)
                dve.wait_ge(up_ready, n + 1)
                dve.tensor_tensor(glu[:, d], gate[:, d], up[:, d], ALU.mult).then_inc(glu_ready, 1)

            def activated(n, s, k):
                d = s % 2
                dve.wait_ge(tanh_ready, n + 1)
                dve.wait_ge(glu_ready, n + 1)
                wait_count(dve, actT_psum, n - 1)
                dve.scalar_tensor_tensor(out=act[:, d], in0=tanh[:, d], scalar=1.0, in1=glu[:, d],
                                         op0=ALU.add, op1=ALU.mult).then_inc(act_ready, 1)

            def act_low(n, s, k):
                d = s % 2
                dve.wait_ge(actT_hi_ready, n + 1)
                wait_count(dve, down_psum, n - 1)
                dve.tensor_tensor(actT_lo[:, d], bank[4 + d][:, 0:KI * P].rearrange("p (k n) -> p k n", k=KI),
                                  actT_hi[:, d].bitcast(F32), ALU.subtract).then_inc(actT_lo_ready, 1)

            rows_low(0, 0, 0)
            K = steps_peeled(dve, NB, UNROLL, step_b)
            act_low(NB - 2, UNROLL - 2, K)
            activated(NB - 1, UNROLL - 1, K)
            act_low(NB - 1, UNROLL - 1, K)

            tdone = [0]

            def table(instruction):
                tdone[0] += 1
                instruction.then_inc(table_step, 1)
                dve.wait_ge(table_step, tdone[0])

            dve.wait_ge(c_loaded, 16 * C_DMAS)
            dve.wait_ge(tables, 7)
            table(dve.reciprocal(scales[:, 3:5], scales[:, 0:2]))
            table(dve.tensor_scalar(k_scaled[:], k_raw[:], scales[:, 4:5], None, ALU.mult))
            table(dve.tensor_scalar(k_grid[:].bitcast(I32), k_scaled[:].bitcast(I32), EXPONENT_BITS, None,
                                    ALU.bitwise_and))
            table(dve.tensor_scalar(k_grid[:], k_grid[:], FP8_LEAST_NORMAL, FP8_GRID, ALU.max, ALU.mult))
            table(dve.tensor_tensor(k_scaled[:], k_scaled[:], k_grid[:], ALU.add))
            table(dve.tensor_tensor(k_quant[:], k_scaled[:], k_grid[:], ALU.subtract))
            table(dve.tensor_tensor(scales[:, 2:3], scales[:, 0:1], scales[:, 1:2], ALU.mult))
            table(dve.tensor_copy(counts[:, 0, :], counts_i[:]))
            table(dve.tensor_scalar(counts[:, 1, :], counts[:, 0, :], -1.0, float(S + 1), ALU.mult, ALU.add))
            dve.memset(counts[:, 2, :], float(S - 1))
            table(dve.tensor_copy(kind_row[:, 0, :], kind_row_i[:, 0, :]))
            table(dve.reciprocal(counts[:], counts[:]))
            dve.tensor_scalar(kind_row[:, 1, :], kind_row[:, 0, :], 0.0, -2.0, ALU.is_equal, ALU.mult)
            table(dve.tensor_scalar(kind_row[:, 2, :], kind_row[:, 0, :], 1.0, None, ALU.is_equal))
            table(dve.tensor_tensor(kind_row[:, 1, :], kind_row[:, 1, :], kind_row[:, 2, :], ALU.subtract))
            table(dve.tensor_scalar(kind_row_i[:, 1, :], kind_row[:, 1, :], 2.0, None, ALU.add))
            table(dve.tensor_copy(kind_of[:, 0:1], kind_i[:]))
            dve.tensor_scalar(kind_of[:, 1:2], kind_of[:, 0:1], 0.0, NEG, ALU.not_equal, ALU.mult)
            dve.tensor_scalar(kind_of[:, 2:3], kind_of[:, 0:1], 1.0, NEG, ALU.not_equal, ALU.mult)
            dve.tensor_scalar(kind_of[:, 4:5], kind_of[:, 0:1], 1.0, None, ALU.is_equal)
            table(dve.tensor_scalar(kind_of[:, 5:6], kind_of[:, 0:1], 0.0, None, ALU.is_equal))
            table(dve.tensor_tensor(kind_of[:, 4:5], kind_of[:, 4:5], kind_of[:, 5:6], ALU.add))
            table(dve.tensor_scalar(kind_of[:, 3:4], kind_of[:, 4:5], NEG, None, ALU.mult))

            def mix_of(n, s, k):
                dve.wait_ge(y_loaded[s], 16 * 2 * (k + 1))
                if not (isinstance(n, int) and n < 2):
                    dve.wait_ge(mixed_kept[s], 16 * k)
                for c in range(2):
                    for t in range(TB):
                        last_sum = X[:, ds(n * TB + t), 0:H].rearrange("p t h -> p (t h)") if c == 0 else mix[:, s, t, :]
                        op = dve.scalar_tensor_tensor(out=mix[:, s, t, :], in0=picks[:, s, c, t, :],
                                                      scalar=tok_w[:, c, ds(n * TB + t)], in1=last_sum,
                                                      op0=ALU.mult, op1=ALU.add)
                    if c == 0:
                        op.then_inc(mix_step, 1)
                        dve.wait_ge(mix_step, n + 1)
                op.then_inc(mixed, 1)
                if (last := earlier(n, s, k, 1, 2)) is not None:
                    copy_scores(*last)

            def copy_scores(n, s, k):
                dve.wait_ge(score_psum, n + 1)
                if not (isinstance(n, int) and n < 2):
                    dve.wait_ge(row_stored[s], 16 * k)
                dve.tensor_copy(score_row[:, s, :], bank[3][0:1, :]).then_inc(row_ready, 1)
                dve.tensor_copy(score_col[:, :, ds(n)].rearrange("p t n -> p (t n)"),
                                bank[4][:, 0:TB]).then_inc(col_ready, 1)

            steps(dve, B, 2, mix_of)
            copy_scores(B - 1, 1, B // 2 - 1)

            mdone = [0]

            def stat(instruction):
                mdone[0] += 1
                instruction.then_inc(max_step, 1)
                dve.wait_ge(max_step, mdone[0])

            dve.wait_ge(scores_loaded, 16)
            LOWEST = -3.0e38
            stat(dve.tensor_tensor_scan(from_left[:], scores[:], scores[:], LOWEST, ALU.max, ALU.max))
            stat(dve.tensor_tensor_scan(from_right[:, ::-1], scores[:, ::-1], scores[:, ::-1], LOWEST,
                                        ALU.max, ALU.max))
            dve.tensor_tensor(around[:, 1:S - 1], from_left[:, 0:S - 2], from_right[:, 2:S], ALU.max)
            dve.tensor_copy(around[:, 0:1], from_right[:, 1:2])
            dve.tensor_copy(around[:, S - 1:S], from_left[:, S - 2:S - 1])
            stat(dve.tensor_scalar(row_max[:], from_left[:], kind_of[:, 1:2], None, ALU.add))
            stat(dve.scalar_tensor_tensor(out=row_max[:], in0=from_right[:], scalar=kind_of[:, 2:3],
                                          in1=row_max[:], op0=ALU.add, op1=ALU.max))
            stat(dve.scalar_tensor_tensor(out=row_max[:], in0=around[:], scalar=kind_of[:, 3:4],
                                          in1=row_max[:], op0=ALU.add, op1=ALU.max))
            dve.tensor_scalar(row_max[:], row_max[:], -1.0, None, ALU.mult).then_inc(max_ready, 1)

            def exponents(n, s, k):
                kind = dve.value_load(kind_row_i[0:1, 1, ds(n)], min_val=0, max_val=2)
                dve.wait_ge(max_loaded[s], 16 * (k + 1))
                for l in range(TB):
                    lo = S - P - P * l
                    wait_count(dve, probs_ready, TB * n + l - 1)
                    dve.tensor_tensor(expo[:, l % 2], neg_max[:, s, :],
                                      masks[:, ds(kind), lo:lo + S].rearrange("p m s -> p (m s)"),
                                      ALU.add).then_inc(expo_ready, 1)

            def pool_of(n, s, k):
                if (after := later(n, s, k, 2, B)) is not None:
                    exponents(*after)
                kind = dve.value_load(kind_row_i[0:1, 1, ds(n)], min_val=0, max_val=2)
                for j in range(TB):
                    dve.wait_ge(pool_psum, TB * n + j + 1)
                    dve.reciprocal(norm[:, j:j + 1], bank[j][:, H:H + 1]).then_inc(norm_ready, 1)
                    dve.wait_ge(norm_ready, TB * n + j + 1)
                    dve.tensor_scalar(pooled[:, j, :], bank[j][:, 0:H], norm[:, j:j + 1],
                                      counts[:, ds(kind), j], ALU.mult, ALU.mult).then_inc(pooled_ready, 1)
                dve.wait_ge(pooled_ready, TB * (n + 1))
                wait_count(dve, quant_ready, n)
                dve.tensor_scalar(scaled[:], pooled[:], scales[:, 3:4], None,
                                  ALU.mult).then_inc(scaled_ready, 1)
                dve.wait_ge(scaled_ready, n + 1)
                dve.tensor_scalar(grid[:].bitcast(I32), scaled[:].bitcast(I32), EXPONENT_BITS, None,
                                  ALU.bitwise_and).then_inc(bits_ready, 1)
                dve.wait_ge(bits_ready, n + 1)
                dve.tensor_scalar(grid[:], grid[:], FP8_LEAST_NORMAL, FP8_GRID, ALU.max,
                                  ALU.mult).then_inc(grid_ready, 1)
                if (last := earlier(n, s, k, 1, 2)) is not None:
                    add_up(*last)

            def add_up(n, s, k):
                dve.wait_ge(ffn_sum_ready, n + 1)
                if not (isinstance(n, int) and n < 2):
                    dve.wait_ge(result_stored[s], 16 * k)
                dve.tensor_tensor(result[:, s], X[:, ds(n * TB, TB), 0:H], ffn_sum[:],
                                  ALU.add).then_inc(result_ready, 1)

            exponents(0, 0, 0)
            steps_peeled(dve, B, 2, pool_of)
            add_up(B - 1, 1, B // 2 - 1)


_INS = ["x", "condB_zX", "condB_zY", "condB_zR", "itok_B_0_2", "L0_ffn_router_weight", "L0_ffn_gate_up_proj",
        "L0_ffn_gate_up_proj_bias", "L0_ffn_down_proj", "L0_ffn_down_proj_bias", "L1_cond_W1", "L1_cond_b1",
        "L1_cond_v", "L1_ffn_kernel", "L1_ffn_input_scale", "L1_ffn_kernel_scale", "L1_ffn_bias"]


def kernel(**inputs):
    import numpy as np
    import concourse.bacc as bacc
    from concourse.bass_utils import run_bass_kernel_spmd

    nc = bacc.Bacc("TRN2", target_bir_lowering=False, num_devices=1)
    arrays, args = {}, []
    for name in _INS:
        a = np.ascontiguousarray(inputs[name])
        arrays[f"in_{name}"] = a
        args.append(nc.dram_tensor(f"in_{name}", a.shape, mybir.dt.from_np(a.dtype), kind="ExternalInput").ap())
    args.append(nc.dram_tensor("out_0", inputs["x"].shape, F32, kind="ExternalOutput").ap())
    adaln_ffn_kernel(nc, *args)
    r = run_bass_kernel_spmd(nc, [arrays], core_ids=[0])
    return r.results[0]["out_0"]
```

```python
from contextlib import ExitStack

import concourse.bass as bass
from concourse import mybir

ALU = mybir.AluOpType
ACT = mybir.ActivationFunctionType
AX = mybir.AxisListType
F32 = mybir.dt.float32
F32R = mybir.dt.float32r
BF16 = mybir.dt.bfloat16
I32 = mybir.dt.int32
U32 = mybir.dt.uint32

P = 128
ALPHA, LIMIT = 1.702, 7.0
NEG = -1.0e30
EXPONENT_BITS = 0x7F800000
FP8_LEAST_NORMAL = 2.0 ** -6
FP8_GRID = 1.5 * 2.0 ** 20
ROW_BIG = 1.0e6


def later(n, s, k, unroll, count):
    if isinstance(n, int) and n == count - 1:
        return None
    return n + 1, (s + 1) % unroll, k + (1 if s == unroll - 1 else 0)


def steps_peeled(eng, count, unroll, step):
    last = count // unroll - 1
    for n in range(2 * unroll):
        step(n, n % unroll, n // unroll)
    with eng.Fori(2, last) as k:
        for s in range(unroll):
            step(k * unroll + s, s, k)
    for s in range(unroll):
        step(last * unroll + s, s, last)
    return last


def ds(i, n=1):
    return bass.ds(i, n)


def wait_count(eng, semaphore, count):
    if not isinstance(count, int) or count > 0:
        eng.wait_ge(semaphore, count)


def wait_alone(eng, semaphore, count, passed, passed_count):
    eng.wait_ge(passed, passed_count)
    eng.wait_ge(semaphore, count)


def steps(eng, count, unroll, step, straight=2):
    for n in range(straight * unroll):
        step(n, n % unroll, n // unroll)
    with eng.Fori(straight, count // unroll) as k:
        for s in range(unroll):
            step(k * unroll + s, s, k)


def earlier(n, s, k, back, unroll):
    if isinstance(n, int) and n < back:
        return None
    return n - back, (s - back) % unroll, k + (s - back) // unroll


def adaln_ffn_kernel(nc, x, zx, zy, zr, kinds, router_w, gate_up_w, gate_up_b, down_w, down_b,
                     w1, b1, v, ffn_k, in_scale, k_scale, ffn_b, out):
    B, S, H = x.shape
    E = router_w.shape[1]
    I = down_w.shape[1]
    A = w1.shape[1]
    F = ffn_k.shape[1]
    GU = 2 * I
    TB = S // P
    NT = B * TB
    KH, KI = H // P, I // P
    assert B == E and H == I == F == 256 and TB == 4 and B % 2 == 0

    UNROLL = 8
    MOST = (2 * B * S - E) // P + E
    NB = -(-MOST // UNROLL) * UNROLL
    T = B * S
    GT = 8
    MW = 2 * S - P

    x_v = x.rearrange("b (t p) h -> b p t h", p=P)
    out_v = out.rearrange("b (t p) h -> b p t h", p=P)
    gate_up_v = gate_up_w.rearrange("e (k p) f -> e p k f", p=P)
    down_v = down_w.rearrange("e (k p) h -> e p k h", p=P)

    u_rows = nc.dram_tensor("u_rows", [T, H], F32).ap()
    y_rows = nc.dram_tensor("y_rows", [2 * T, H], F32).ap()
    u_v = u_rows.rearrange("(b t p) h -> b p t h", p=P, t=TB)
    y_v = y_rows.rearrange("(c b t p) h -> c b p t h", p=P, t=TB, b=B)
    score_rows = nc.dram_tensor("score_rows", [B, S], F32).ap()
    max_rows = nc.dram_tensor("max_rows", [B, S], F32).ap()

    with ExitStack() as ctx:
        def sem(name):
            return ctx.enter_context(nc.semaphore(name))

        def memory(scope):
            return lambda name, shape, dt=F32: scope.enter_context(nc.sbuf_tensor(name, shape, dt))

        bank = [ctx.enter_context(nc.psum_tensor(f"bank{i}", [P, 512], F32)) for i in range(8)]

        sb = memory(ctx)
        X = sb("X", [P, NT, H])
        tok_w = sb("tok_w", [P, 2, NT])
        ident = sb("ident", [P, P])

        with ExitStack() as ab:
            sb = memory(ab)
            gu_hi = sb("gu_hi", [P, E, KH, GU], F32R)
            gu_lo = sb("gu_lo", [P, E, KH, GU], F32R)
            dn_hi = sb("dn_hi", [P, E, KI, H], F32R)
            dn_lo = sb("dn_lo", [P, E, KI, H], F32R)
            gu_bias = sb("gu_bias", [2, 2, E, I], F32R)
            dn_bias = sb("dn_bias", [2, E, H], F32R)
            ones2 = sb("ones2", [2, P], F32R)
            block_expert = sb("block_expert", [1, NB], I32)
            slot_src = sb("slot_src", [P, NB], U32)
            slot_dst = sb("slot_dst", [P, NB], U32)
            with ExitStack() as a:
                sb = memory(a)
                x_hi = sb("x_hi", [P, 2, TB, H], F32R)
                x_lo = sb("x_lo", [P, 2, TB, H], F32R)
                flow = sb("flow", [P, 2, TB, H])
                pair = sb("pair", [P, TB, H])
                uT = sb("uT", [P, KH, S])
                raw_gu = sb("raw_gu", [P, 2, KH, GU])
                raw_dn = sb("raw_dn", [P, 2, KI, H])
                raw_gb = sb("raw_gb", [P, E * GU // P])
                raw_db = sb("raw_db", [P, E * H // P])
                flat_gb = sb("flat_gb", [P, 2, E * GU // P], F32R)
                flat_db = sb("flat_db", [P, 2, E * H // P], F32R)
                diff_f = uT[:].rearrange("p k s -> p (k s)")[:, 0:5 * P].rearrange("p (m c) -> p m c", c=P)
                diff = sb("diff", [P, 5, P], F32R)
                above = sb("above", [P, P], BF16)
                ones_b = sb("ones_b", [P, P], BF16)
                zs = sb("zs", [P, 5, B])
                router_sb = sb("router_sb", [P, KH, E])
                logits = sb("logits", [P, TB, E])
                best = sb("best", [P, TB, 8])
                best_i = sb("best_i", [P, TB, 8], U32)
                top = sb("top", [P, NT, 2])
                top_i = sb("top_i", [P, NT, 2])
                expert_f = sb("expert_f", [P, E])
                raw_row, NE = raw_gu[:].rearrange("p s k f -> p (s k f)"), E * NT
                part = lambda i, n: raw_row[:, i * NE:(i + n) * NE]
                pick = part(0, 2).rearrange("p (c e t) -> p c e t", c=2, e=E)
                follow, totals, upto = (part(i, 1).rearrange("p (e t) -> p e t", e=E) for i in (2, 3, 4))
                picked = part(5, 1).bitcast(BF16)[:, 0:NE].rearrange("p (e t) -> p e t", e=E)
                pair_no = raw_row[:, 6 * NE:6 * NE + 4 * NB].rearrange("p (v n) -> p v n", v=4)
                ends = sb("ends", [P, 6, E])
                ends_i = sb("ends_i", [P, 2, E], I32)
                slot_i = sb("slot_i", [P, 3, 2, NT], I32)
                slot_q = sb("slot_q", [P, 2, NT], BF16)
                slot_b = sb("slot_b", [P, 2, NT], BF16)
                column_i = sb("column_i", [P, P], I32)
                column = sb("column", [P, P], BF16)
                is_q = pair[:].rearrange("p t h -> p (t h)").bitcast(BF16).rearrange("p (d g n) -> p d g n", d=2, g=GT)
                flow_row = flow[:].rearrange("p s t h -> p (s t h)")
                is_b_of = flow_row[:, 0:2 * GT * NB].bitcast(BF16).rearrange(
                    "p (d g v n) -> p d g v n", d=2, g=GT, v=2)
                is_b = flow_row[:, 2 * GT * NB:3 * GT * NB].bitcast(BF16).rearrange(
                    "p (d g n) -> p d g n", d=2, g=GT)
                tile_no = sb("tile_no", [P, 2 * NT], BF16)
                row_one = sb("row_one", [P, 1])
                row_i = sb("row_i", [P, 1], I32)
                row_f = sb("row_f", [P, 1])
                slot_f = sb("slot_f", [P, 2, NT])
                odds = sb("odds", [P, 3, NT])
                blk_i = sb("blk_i", [1, NB], I32)
                blk_f = sb("blk_f", [1, NB])
                blk_past = uT[0:1].rearrange("p k s -> p (k s)")[:, 0:NB * E].rearrange("p (n e) -> p n e", e=E)
                blk_e = sb("blk_e", [1, NB])
            with ExitStack() as b_:
                sb = memory(b_)
                rows = sb("rows", [P, UNROLL, H])
                rowT_hi = sb("rowT_hi", [P, 2, KH, P], F32R)
                rowT_lo = sb("rowT_lo", [P, 2, KH, P], F32R)
                gate = sb("gate", [P, 2, I])
                up = sb("up", [P, 2, I])
                tanh = sb("tanh", [P, 2, I])
                glu = sb("glu", [P, 2, I])
                act = sb("act", [P, 2, I])
                actT_hi = sb("actT_hi", [P, 2, KI, P], F32R)
                actT_lo = sb("actT_lo", [P, 2, KI, P], F32R)
                outs = sb("outs", [P, UNROLL, H])

        sb = memory(ctx)
        X_hi = sb("X_hi", [P, NT, H + 2], F32R)
        X_lo = sb("X_lo", [P, NT, H + 2], F32R)
        score_col = sb("score_col", [P, TB, B])
        scores = sb("scores", [B, S])
        kind_of = sb("kind_of", [B, 6])
        kind_i = sb("kind_i", [B, 1], I32)
        kind_row = sb("kind_row", [1, 4, B])
        kind_row_i = sb("kind_row_i", [1, 2, B], I32)
        masks = sb("masks", [P, 3, MW])
        counts = sb("counts", [P, 3, TB])
        counts_i = sb("counts_i", [P, TB], I32)
        w1_sb = sb("w1_sb", [P, KH, A])
        w1_hi = sb("w1_hi", [P, KH, A], F32R)
        w1_lo = sb("w1_lo", [P, KH, A], F32R)
        b1_sb = sb("b1_sb", [A, 1])
        v_sb = sb("v_sb", [A, 1])
        ident_b = sb("ident_b", [P, P], BF16)
        k_raw = sb("k_raw", [P, KH, F], BF16)
        k_quant = sb("k_quant", [P, KH, F], BF16)
        scales = sb("scales", [P, 5])
        bias_f = sb("bias_f", [P, F], BF16)
        row_max = sb("row_max", [B, S])
        with ExitStack() as c1:
            sb = memory(c1)
            picks = sb("picks", [P, 2, 2, TB, H])
            mix = sb("mix", [P, 2, TB, H])
            xT_hi = sb("xT_hi", [P, 2, KH, S], F32R)
            xT_lo = sb("xT_lo", [P, 2, KH, S], F32R)
            hidden = sb("hidden", [A, 2, S])
            score_row = sb("score_row", [1, 2, S])
            from_left = sb("from_left", [B, S])
            from_right = sb("from_right", [B, S])
            around = sb("around", [B, S])
            k_scaled = sb("k_scaled", [P, KH, F])
            k_grid = sb("k_grid", [P, KH, F])
        with ExitStack() as c2:
            sb = memory(c2)
            neg_max = sb("neg_max", [P, 2, S])
            expo = sb("expo", [P, 2, S])
            probs = sb("probs", [P, 2, S])
            probs_hi = sb("probs_hi", [P, 2, TB, S], F32R)
            probs_lo = sb("probs_lo", [P, 2, TB, S], F32R)
            norm = sb("norm", [P, TB])
            pooled = sb("pooled", [P, TB, H], BF16)
            scaled = sb("scaled", [P, TB, H])
            grid = sb("grid", [P, TB, H])
            quant = sb("quant", [P, TB, H], BF16)
            quantT = sb("quantT", [P, KH, S], BF16)
            ffn = sb("ffn", [P, 2, TB, F], BF16)
            ffn_sum = sb("ffn_sum", [P, TB, F], BF16)
            result = sb("result", [P, 2, TB, H])

        pool_const = sem("pool_const")
        diff_step = sem("diff_step")
        z_loaded = sem("z_loaded")
        router_loaded = sem("router_loaded")
        z_step = sem("z_step")
        x_loaded = [sem(f"x_loaded{i}") for i in range(2)]
        w_loaded = [sem(f"w_loaded{i}") for i in range(2)]
        matrix_ready = sem("matrix_ready")
        x_hi_ready = sem("x_hi_ready")
        x_lo_ready = sem("x_lo_ready")
        flow_ready = sem("flow_ready")
        lap_ready = sem("lap_ready")
        pair_ready = sem("pair_ready")
        flow_step = sem("flow_step")
        u_ready = sem("u_ready")
        u_kept = [sem(f"u_kept{i}") for i in range(2)]
        uT_psum = sem("uT_psum")
        uT_ready = sem("uT_ready")
        logits_psum = sem("logits_psum")
        logits_ready = sem("logits_ready")
        best_step = sem("best_step")
        index_step = sem("index_step")
        top_ready = sem("top_ready")
        hi_ready = sem("hi_ready")
        gu_used = sem("gu_used")
        dn_used = sem("dn_used")
        bias_loaded = sem("bias_loaded")
        bias_step = sem("bias_step")
        bias_placed = sem("bias_placed")
        route_step = sem("route_step")
        picked_ready = sem("picked_ready")
        ranks_ready = sem("ranks_ready")
        gap_ready = sem("gap_ready")
        odds_ready = sem("odds_ready")
        slots_ready = sem("slots_ready")
        is_q_ready = sem("is_q_ready")
        is_b_ready = sem("is_b_ready")
        is_b_tile = sem("is_b_tile")
        turned = sem("turned")
        experts_ready = sem("experts_ready")
        rows_loaded = [sem(f"rows_loaded{i}") for i in range(UNROLL)]
        rowT_psum = sem("rowT_psum")
        rowT_hi_ready = sem("rowT_hi_ready")
        rowT_lo_ready = sem("rowT_lo_ready")
        gu_psum = sem("gu_psum")
        gate_ready = sem("gate_ready")
        up_ready = sem("up_ready")
        tanh_ready = sem("tanh_ready")
        glu_ready = sem("glu_ready")
        act_ready = sem("act_ready")
        actT_psum = sem("actT_psum")
        actT_hi_ready = sem("actT_hi_ready")
        actT_lo_ready = sem("actT_lo_ready")
        down_psum = sem("down_psum")
        outs_ready = sem("outs_ready")
        outs_stored = [sem(f"outs_stored{i}") for i in range(UNROLL)]
        w1_loaded = sem("w1_loaded")
        w1_split = sem("w1_split")
        ends_set = sem("ends_set")
        c_loaded = sem("c_loaded")
        y_loaded = [[sem(f"y_loaded{c}_{i}") for i in range(2)] for c in range(2)]
        mix_step = sem("mix_step")
        mixed = sem("mixed")
        mixed_kept = [sem(f"mixed_kept{i}") for i in range(2)]
        xT_psum = sem("xT_psum")
        xT_hi_ready = sem("xT_hi_ready")
        xT_lo_ready = sem("xT_lo_ready")
        X_hi_ready = sem("X_hi_ready")
        X_lo_ready = sem("X_lo_ready")
        hidden_psum = sem("hidden_psum")
        hidden_ready = sem("hidden_ready")
        score_psum = sem("score_psum")
        row_ready = sem("row_ready")
        col_psum = sem("col_psum")
        col_ready = sem("col_ready")
        row_stored = [sem(f"row_stored{i}") for i in range(2)]
        scores_loaded = sem("scores_loaded")
        tables = sem("tables")
        table_step = sem("table_step")
        max_step = sem("max_step")
        max_ready = sem("max_ready")
        max_stored = sem("max_stored")
        max_loaded = [sem(f"max_loaded{i}") for i in range(2)]
        expo_ready = sem("expo_ready")
        probs_ready = sem("probs_ready")
        probs_lo_ready = sem("probs_lo_ready")
        pool_psum = sem("pool_psum")
        norm_ready = sem("norm_ready")
        pooled_ready = sem("pooled_ready")
        scaled_ready = sem("scaled_ready")
        bits_ready = sem("bits_ready")
        grid_ready = sem("grid_ready")
        lifted = sem("lifted")
        quant_ready = sem("quant_ready")
        quantT_psum = sem("quantT_psum")
        quantT_ready = sem("quantT_ready")
        ffn_psum = sem("ffn_psum")
        ffn_ready = sem("ffn_ready")
        ffn_sum_ready = sem("ffn_sum_ready")
        result_ready = sem("result_ready")
        result_stored = [sem(f"result_stored{i}") for i in range(2)]

        ZX, ZY, ZR, ZRN, SLOPE = range(5)
        lap = [[bank[0], bank[1]], [bank[2], bank[3]]]
        uT_bank = [bank[4], bank[5]]
        logit_bank = bank[6][:, 0:TB * E].rearrange("p (t e) -> p t e", e=E)
        rank_bank = bank[7][:, 0:E * NT].rearrange("p (e t) -> p e t", t=NT)
        total_bank = bank[1][:, 0:E * NT].rearrange("p (e t) -> p e t", t=NT)
        turn_bank = bank[0][:, 0:2 * NB].rearrange("p (v n) -> p v n", v=2)
        W_DMAS, BIAS_DMAS, PLACE_DMAS = 2, 2, 6
        MIDDLE, FIRST, LAST, BEFORE, AFTER = range(5)
        N_CONST_A = 8
        DIFF_STEPS = 14
        N_Z = 9
        C_DMAS = 6
        GROUPS = 2 * NT // GT

        block = ctx.enter_context(nc.Block())

        @block.sync
        def _(sp):
            for i, z in enumerate((zx, zy, zr)):
                sp.dma_start(zs[:, i, :], z.partition_broadcast(P)).then_inc(z_loaded, 16)
            sp.dma_start(router_sb[:], router_w.rearrange("(k p) e -> p k e", p=P)).then_inc(router_loaded, 16)

            sp.dma_start(raw_gb[:], gate_up_b.rearrange("e (a f) -> (e a) f", a=P // E)).then_inc(bias_loaded, 16)
            sp.dma_start(raw_db[:], down_b.rearrange("e (a f) -> (e a) f", a=P // E)).then_inc(bias_loaded, 16)

            def load(n, s, k):
                wait_count(sp, x_hi_ready, n - 1)
                sp.dma_start(X[:, ds(n * TB, TB), 0:H],
                             x_v[ds(n)].rearrange("b p t h -> (b p) t h")).then_inc(x_loaded[s], 16)
                wait_count(sp, gu_used, n - 1)
                sp.dma_start(raw_gu[:, s], gate_up_v[ds(n)].rearrange("e p k f -> (e p) k f")).then_inc(w_loaded[s], 16)
                wait_count(sp, dn_used, n - 1)
                sp.dma_start(raw_dn[:, s], down_v[ds(n)].rearrange("e p k h -> (e p) k h")).then_inc(w_loaded[s], 16)

            steps(sp, B, 2, load)
            sp.wait_ge(bias_step, 5)
            for half in range(2):
                for two in range(2):
                    part = E * GU // P // 2
                    sp.dma_start(gu_bias[half:half + 1, two].bitcast(F32).rearrange("r e i -> r (e i)"),
                                 flat_gb[:, half, two * part:(two + 1) * part].bitcast(F32)
                                 ).then_inc(bias_placed, 16)
                sp.dma_start(dn_bias[half:half + 1].bitcast(F32).rearrange("r e i -> r (e i)"),
                             flat_db[:, half, :].bitcast(F32)).then_inc(bias_placed, 16)

            for s in range(UNROLL):
                sp.wait_ge(outs_stored[s], 16 * (NB // UNROLL))
            for dst, src in ((w1_sb[:], w1.rearrange("(k p) a -> p k a", p=P)),
                             (b1_sb[:], b1.rearrange("(a o) -> a o", o=1)),
                             (v_sb[:], v.rearrange("(a o) -> a o", o=1))):
                sp.dma_start(dst, src).then_inc(w1_loaded, 16)

            def load_y(n, s, k):
                for c, used in enumerate((mix_step, mixed)):
                    wait_count(sp, used, n - 1)
                    sp.dma_start(picks[:, s, c],
                                 y_v[c, ds(n)].rearrange("b p t h -> (b p) t h")).then_inc(y_loaded[c][s], 16)
                if (last := earlier(n, s, k, 1, 2)) is not None:
                    keep(*last)
                if (last := earlier(n, s, k, 3, 2)) is not None:
                    keep_row(*last)

            def keep(n, s, k):
                sp.wait_ge(mixed, n + 1)
                sp.dma_start(X[:, ds(n * TB, TB), 0:H], mix[:, s]).then_inc(mixed_kept[s], 16)

            def keep_row(n, s, k):
                sp.wait_ge(row_ready, n + 1)
                sp.dma_start(score_rows[ds(n), :], score_row[0:1, s, :]).then_inc(row_stored[s], 16)

            steps(sp, B, 2, load_y)
            for dst, src in ((kind_i[:], kinds.rearrange("(b o) -> b o", o=1)),
                             (kind_row_i[:, 0, :], kinds.rearrange("(o b) -> o b", o=1)),
                             (k_raw[:], ffn_k.rearrange("(k p) f -> p k f", p=P)),
                             (scales[:, 0:1], in_scale.partition_broadcast(P)),
                             (scales[:, 1:2], k_scale.partition_broadcast(P)),
                             (bias_f[:], ffn_b.partition_broadcast(P))):
                sp.dma_start(dst, src).then_inc(c_loaded, 16)
            keep(B - 1, 1, 0)
            for n in range(B - 3, B):
                keep_row(n, n % 2, 0)
            for s in range(2):
                sp.wait_ge(row_stored[s], 16 * (B // 2))
            sp.dma_start(scores[:], score_rows).then_inc(scores_loaded, 16)
            sp.wait_ge(max_ready, 1)
            sp.dma_start(max_rows, row_max[:]).then_inc(max_stored, 16)
            sp.wait_ge(max_stored, 16)
            for s in range(2):
                sp.wait_ge(mixed_kept[s], 16 * (B // 2))

            def spread_max(n, s, k):
                wait_count(sp, expo_ready, TB * (n - 1))
                sp.dma_start(neg_max[:, s, :],
                             max_rows[ds(n), :].rearrange("b s -> (b s)").partition_broadcast(P)).then_inc(max_loaded[s], 16)

            steps(sp, B, 2, spread_max)

        @block.gpsimd
        def _(pool):
            pool.memset(ident[:], 0.0).then_inc(pool_const, 1)
            pool.memset(diff_f, 0.0).then_inc(diff_step, 1)
            pool.memset(ones_b[:], 1.0).then_inc(pool_const, 1)
            pool.iota(column_i[:], [[1, P]], base=0, channel_multiplier=0).then_inc(pool_const, 1)
            pool.iota(slot_i[:, 2], [[NT, 2], [1, NT]], base=0, channel_multiplier=0).then_inc(pool_const, 1)
            pool.iota(row_i[:], [[0, 1]], base=0, channel_multiplier=1).then_inc(pool_const, 1)
            pool.iota(blk_i[:], [[P, NB]], base=0, channel_multiplier=0).then_inc(pool_const, 1)
            pool.wait_ge(pool_const, 6)
            pool.affine_select(out=ident[:], in_=ident[:], compare_op=ALU.not_equal, fill=1.0, base=0,
                               pattern=[[-1, P]], channel_multiplier=1).then_inc(pool_const, 1)
            pool.affine_select(out=above[:], in_=ones_b[:], compare_op=ALU.is_gt, fill=0.0, base=0,
                               pattern=[[1, P]], channel_multiplier=-1).then_inc(pool_const, 1)
            for i, (matrix, fill, base) in enumerate((
                    (MIDDLE, -2.0, 0), (MIDDLE, 1.0, 1), (MIDDLE, 1.0, -1),
                    (FIRST, -2.0, 0), (FIRST, 1.0, 1), (FIRST, 1.0, -1),
                    (LAST, -2.0, 0), (LAST, 1.0, 1), (LAST, 1.0, -1),
                    (BEFORE, 1.0, 1 - P), (AFTER, 1.0, P - 1))):
                pool.wait_ge(diff_step, i + 1)
                pool.affine_select(out=diff_f[:, matrix], in_=diff_f[:, matrix], compare_op=ALU.not_equal,
                                   fill=fill, base=base, pattern=[[-1, P]], channel_multiplier=1).then_inc(diff_step, 1)
            for i, (matrix, column_at, base) in enumerate(((FIRST, 0, -1), (LAST, P - 1, 2 - P))):
                pool.wait_ge(diff_step, DIFF_STEPS - 2 + i)
                pool.affine_select(out=diff_f[:, matrix, column_at:column_at + 1],
                                   in_=diff_f[:, matrix, column_at:column_at + 1], compare_op=ALU.not_equal,
                                   fill=2.0, base=base, pattern=[[0, 1]], channel_multiplier=1).then_inc(diff_step, 1)

            def step_a(n, s, k):
                xn = X[:, ds(n * TB, TB), :]
                pool.wait_ge(x_hi_ready, n + 1)
                pool.tensor_tensor(x_lo[:, s], xn[:, :, 0:H], x_hi[:, s].bitcast(F32),
                                   ALU.subtract).then_inc(x_lo_ready, 1)
                wait_count(pool, flow_step, 2 * n)
                pool.tensor_tensor(pair[:, :, 1:H - 1], xn[:, :, 0:H - 2], xn[:, :, 2:H],
                                   ALU.add).then_inc(pair_ready, 1)
                pool.tensor_tensor(pair[:, :, 0:H:H - 1], xn[:, :, 1:H - 1:H - 3], xn[:, :, 1:H - 1:H - 3],
                                   ALU.add).then_inc(pair_ready, 1)
                pool.wait_ge(hi_ready, 2 * n + 2)
                pool.tensor_tensor(dn_lo[:, ds(n)].rearrange("p e k h -> p (e k) h"), raw_dn[:, s],
                                   dn_hi[:, ds(n)].bitcast(F32).rearrange("p e k h -> p (e k) h"),
                                   ALU.subtract).then_inc(dn_used, 1)

            steps(pool, B, 2, step_a)

            for g in range(GROUPS):
                pool.wait_ge(is_b_ready, 2 * g + 1)
                wait_count(pool, turned, g - 1)
                pool.tensor_tensor(is_b_of[:, g % 2, :, 1, :], is_b[:, g % 2],
                                   tile_no[:, g * GT:(g + 1) * GT].unsqueeze(2).broadcast_to([P, GT, NB]),
                                   ALU.mult).then_inc(is_b_tile, 1)

            pool.wait_ge(slots_ready, 2)
            for s in range(2):
                pool.wait_ge(u_kept[s], 16 * (B // 2))
            AHEAD = 8
            for n in range(NB + AHEAD):
                if n < NB:
                    s = n % UNROLL
                    wait_count(pool, rowT_psum, n - UNROLL + 1)
                    pool.indirect_dma_start(
                        out=rows[:, s, :], out_offset=None, in_=u_rows,
                        in_offset=bass.IndirectOffsetOnAxis(ap=slot_src[:, n:n + 1], axis=0),
                    ).then_inc(rows_loaded[s], 16)
                m = n - AHEAD
                if m >= 0:
                    pool.wait_ge(outs_ready, m + 1)
                    pool.indirect_dma_start(
                        out=y_rows, out_offset=bass.IndirectOffsetOnAxis(ap=slot_dst[:, m:m + 1], axis=0),
                        in_=outs[:, m % UNROLL, :], in_offset=None, bounds_check=2 * T - 1,
                        oob_is_err=False).then_inc(outs_stored[m % UNROLL], 16)

            for s in range(UNROLL):
                pool.wait_ge(outs_stored[s], 16 * (NB // UNROLL))
            pool.memset(X_hi[:, :, H:H + 2].bitcast(F32), 1.0).then_inc(ends_set, 1)
            pool.memset(X_lo[:, :, H:H + 2].bitcast(F32), 0.0).then_inc(ends_set, 1)

            pool.memset(masks[:], 0.0).then_inc(tables, 1)
            pool.memset(ident_b[:], 0.0).then_inc(tables, 1)
            pool.iota(counts_i[:], [[P, TB]], base=1, channel_multiplier=1).then_inc(tables, 1)
            pool.wait_ge(tables, 3)
            for i, (op, sign) in enumerate(((ALU.is_ge, 1), (ALU.is_ge, -1), (ALU.not_equal, 1))):
                pool.affine_select(out=masks[:, i], in_=masks[:, i], compare_op=op, fill=NEG,
                                   base=sign * (P - S), pattern=[[sign, MW]],
                                   channel_multiplier=-sign).then_inc(tables, 1)
            pool.affine_select(out=ident_b[:], in_=ident_b[:], compare_op=ALU.not_equal, fill=1.0, base=0,
                               pattern=[[-1, P]], channel_multiplier=1).then_inc(tables, 1)

            def x_low(n, s, k):
                pool.wait_ge(X_hi_ready, n + 1)
                pool.tensor_tensor(X_lo[:, ds(n * TB, TB), 0:H], mix[:, s],
                                   X_hi[:, ds(n * TB, TB), 0:H].bitcast(F32), ALU.subtract).then_inc(X_lo_ready, 1)

            steps(pool, B, 2, x_low)
            def step_c(n, s, k):
                if (last := earlier(n, s, k, 3, 2)) is not None:
                    add_up(*last)
                    store(*last)
                pool.wait_ge(grid_ready, n + 1)
                pool.tensor_tensor(scaled[:], scaled[:], grid[:], ALU.add).then_inc(lifted, 1)
                pool.wait_ge(lifted, n + 1)
                wait_count(pool, quantT_psum, n)
                pool.tensor_tensor(quant[:], scaled[:], grid[:], ALU.subtract).then_inc(quant_ready, 1)

            def add_up(n, s, k):
                pool.wait_ge(ffn_sum_ready, n + 1)
                if not (isinstance(n, int) and n < 2):
                    pool.wait_ge(result_stored[s], 16 * k)
                pool.tensor_tensor(result[:, s], X[:, ds(n * TB, TB), 0:H], ffn_sum[:],
                                   ALU.add).then_inc(result_ready, 1)

            def store(n, s, k):
                pool.wait_ge(result_ready, n + 1)
                pool.dma_start(out_v[ds(n)].rearrange("b p t h -> (b p) t h"),
                               result[:, s]).then_inc(result_stored[s], 16)

            steps(pool, B, 2, step_c, straight=3)
            for n in range(B - 3, B):
                add_up(n, n % 2, n // 2)
                store(n, n % 2, n // 2)
            for s in range(2):
                pool.wait_ge(result_stored[s], 16 * (B // 2))

        @block.scalar
        def _(a):
            def step_a(n, s, k):
                after, last = later(n, s, k, 2, B), earlier(n, s, k, 1, 2)
                if after is not None:
                    x_rounded(*after)
                if last is not None:
                    keep(*last)
                weights_rounded(n, s, k)
                if last is not None:
                    transposed(*last)
                if after is not None:
                    flow_begun(*after)

            def x_rounded(n, s, k):
                a.wait_ge(x_loaded[s], 16 * (k + 1))
                wait_count(a, lap_ready, 2 * (n - 1))
                a.activation(x_hi[:, s], X[:, ds(n * TB, TB), 0:H], ACT.Copy).then_inc(x_hi_ready, 1)

            def flow_begun(n, s, k):
                if not (isinstance(n, int) and n < 2):
                    a.wait_ge(u_kept[s], 16 * k)
                    a.wait_ge(uT_psum, 2 * n - 2)
                a.activation(flow[:, s], X[:, ds(n * TB, TB), 0:H], ACT.Identity, scale=zs[:, ZRN, ds(n)],
                             bias=zs[:, SLOPE, ds(n)]).then_inc(flow_ready, 1)

            def weights_rounded(n, s, k):
                a.wait_ge(w_loaded[s], 16 * W_DMAS * (k + 1))
                a.activation(gu_hi[:, ds(n)].rearrange("p e k (two i) -> p (e k) two i", two=2),
                             raw_gu[:, s].rearrange("p k (i two) -> p k two i", two=2), ACT.Copy).then_inc(hi_ready, 1)
                a.activation(dn_hi[:, ds(n)].rearrange("p e k h -> p (e k) h"), raw_dn[:, s],
                             ACT.Copy).then_inc(hi_ready, 1)

            def keep(n, s, k):
                a.wait_ge(u_ready, n + 1)
                a.dma_start(u_v[ds(n)].rearrange("b p t h -> (b p) t h"), flow[:, s]).then_inc(u_kept[s], 16)

            def transposed(n, s, k):
                wait_count(a, logits_psum, n)
                for half in range(KH):
                    a.wait_ge(uT_psum, 2 * n + half + 1)
                    a.activation(uT[:, half], uT_bank[half][:], ACT.Copy).then_inc(uT_ready, 1)

            a.wait_ge(z_step, 2)
            x_rounded(0, 0, 0)
            flow_begun(0, 0, 0)
            steps_peeled(a, B, 2, step_a)
            keep(B - 1, 1, 0)
            transposed(B - 1, 1, 0)
            a.wait_ge(gap_ready, 1)
            a.activation(odds[:, 1], odds[:, 0], ACT.Exp).then_inc(odds_ready, 1)

            a.wait_ge(slots_ready, 2)

            def rows_rounded(n, s, k):
                d = s % 2
                a.wait_ge(rowT_psum, n + 1)
                a.activation(rowT_hi[:, d], bank[2 + d][:, 0:KH * P].rearrange("p (k n) -> p k n", k=KH),
                             ACT.Copy).then_inc(rowT_hi_ready, 1)

            def step_b(n, s, k):
                if (last := earlier(n, s, k, 2, UNROLL)) is not None:
                    transposed_act(*last)
                if (after := later(n, s, k, UNROLL, NB)) is not None:
                    rows_rounded(*after)
                if (last := earlier(n, s, k, 3, UNROLL)) is not None:
                    finish_down(*last)
                activate(n, s, k)

            def activate(n, s, k):
                a.wait_ge(gate_ready, n + 1)
                a.activation(tanh[:, s % 2], gate[:, s % 2], ACT.Tanh, scale=ALPHA).then_inc(tanh_ready, 1)

            def transposed_act(n, s, k):
                a.wait_ge(actT_psum, n + 1)
                a.activation(actT_hi[:, s % 2],
                             bank[4 + s % 2][:, 0:KI * P].rearrange("p (k n) -> p k n", k=KI),
                             ACT.Copy).then_inc(actT_hi_ready, 1)

            def finish_down(n, s, k):
                a.wait_ge(down_psum, n + 1)
                if not (isinstance(n, int) and n < UNROLL):
                    a.wait_ge(outs_stored[s], 16 * k)
                a.activation(outs[:, s, :], bank[6 + s % 2][:, 0:H], ACT.Copy).then_inc(outs_ready, 1)

            rows_rounded(0, 0, 0)
            K = steps_peeled(a, NB, UNROLL, step_b)
            transposed_act(NB - 2, UNROLL - 2, K)
            finish_down(NB - 3, UNROLL - 3, K)
            finish_down(NB - 2, UNROLL - 2, K)
            transposed_act(NB - 1, UNROLL - 1, K)
            finish_down(NB - 1, UNROLL - 1, K)

            a.wait_ge(w1_loaded, 48)
            a.activation(w1_hi[:], w1_sb[:], ACT.Copy).then_inc(w1_split, 1)

            def scores_of(n, s, k):
                a.wait_ge(mixed, n + 1)
                a.activation(X_hi[:, ds(n * TB, TB), 0:H], mix[:, s], ACT.Copy).then_inc(X_hi_ready, 1)
                for half in range(KH):
                    a.wait_ge(xT_psum, 2 * n + half + 1)
                    a.activation(xT_hi[:, s, half], bank[2 * s + half][:], ACT.Copy).then_inc(xT_hi_ready, 1)
                if (last := earlier(n, s, k, 1, 2)) is not None:
                    hide(*last)
                if (last := earlier(n, s, k, 2, 2)) is not None:
                    copy_row(*last)

            def hide(n, s, k):
                a.wait_ge(hidden_psum, n + 1)
                a.activation(hidden[:, s], bank[4 + s][0:A, :], ACT.Tanh, bias=b1_sb[:, 0:1]).then_inc(hidden_ready, 1)

            def copy_row(n, s, k):
                a.wait_ge(score_psum, n + 1)
                if not (isinstance(n, int) and n < 2):
                    a.wait_ge(row_stored[s], 16 * k)
                a.activation(score_row[:, s, :], bank[6 + s][0:1, :], ACT.Copy).then_inc(row_ready, 1)

            K = steps_peeled(a, B, 2, scores_of)
            copy_row(B - 2, 0, K)
            hide(B - 1, 1, K)
            copy_row(B - 1, 1, K)
            a.wait_ge(col_psum, 1)
            a.activation(score_col[:], bank[0][:, 0:TB * B].rearrange("p (t b) -> p t b", b=B),
                         ACT.Copy).then_inc(col_ready, 1)
            a.wait_ge(col_ready, 1)
            a.wait_ge(X_lo_ready, B)

            def pool_of(n, s, k):
                for l in range(TB):
                    wait_count(a, probs_lo_ready, TB * n + l - 1)
                    a.wait_ge(expo_ready, TB * n + l + 1)
                    wait_count(a, pool_psum, TB * (n - 1))
                    a.activation(probs_hi[:, s, l], expo[:, l % 2], ACT.Exp, bias=score_col[:, l, ds(n)])
                    a.activation(probs[:, l % 2], expo[:, l % 2], ACT.Exp,
                                 bias=score_col[:, l, ds(n)]).then_inc(probs_ready, 1)
                if (last := earlier(n, s, k, 3, 2)) is not None:
                    finish(*last)

            def finish(n, s, k):
                a.wait_ge(quantT_psum, n + 1)
                wait_count(a, ffn_psum, 2 * n)
                a.activation(quantT[:], bank[4][:].bitcast(BF16).rearrange("p (k n) -> p k n", k=KH),
                             ACT.Copy).then_inc(quantT_ready, 1)
                wait_count(a, ffn_sum_ready, n - 1)
                for g in range(2):
                    a.wait_ge(ffn_psum, 2 * n + g + 1)
                    a.activation(ffn[:, s, 2 * g:2 * g + 2, :], bank[5 + g][:].rearrange("p (t f) -> p t f", f=F),
                                 ACT.Copy, scale=scales[:, 2:3]).then_inc(ffn_ready, 1)

            steps(a, B, 2, pool_of)
            for n in range(B - 3, B):
                finish(n, n % 2, 0)

        @block.tensor
        def _(pe):
            def step_a(n, s, k):
                if (last := earlier(n, s, k, 2, 2)) is not None:
                    route(*last)
                pe.wait_ge(x_lo_ready, n + 1)
                wait_count(pe, u_ready, n - 1)
                for g in range(2):
                    own = ((FIRST, MIDDLE), (MIDDLE, LAST))[g]
                    both, one, into, source = ((AFTER, BEFORE, 1, 0), (BEFORE, AFTER, 0, 3))[g]
                    pe.matmul(lap[s][g][:], diff[:, both], x_hi[:, s, 1:3, :], start=True, stop=False)
                    for half in (x_hi, x_lo):
                        pe.matmul(lap[s][g][:, into * H:(into + 1) * H], diff[:, one], half[:, s, source, :],
                                  start=False, stop=False)
                        for t in range(2):
                            pe.matmul(lap[s][g][:, t * H:(t + 1) * H], diff[:, own[t]], half[:, s, 2 * g + t, :],
                                      start=False, stop=False)
                    mm = pe.matmul(lap[s][g][:], diff[:, both], x_lo[:, s, 1:3, :], start=False, stop=True)
                    mm.then_inc(lap_ready, 1)
                if (last := earlier(n, s, k, 1, 2)) is not None:
                    u_transposed(*last)

            def u_transposed(n, s, k):
                pe.wait_ge(u_ready, n + 1)
                wait_count(pe, uT_ready, 2 * n)
                for half in range(KH):
                    for t in range(TB):
                        mm = pe.transpose(uT_bank[half][:, t * P:(t + 1) * P],
                                          flow[:, s, t, half * P:(half + 1) * P], ident[:])
                    mm.then_inc(uT_psum, 1)

            def route(n, s, k):
                wait_count(pe, logits_ready, n)
                pe.wait_ge(uT_ready, 2 * n + 2)
                for t in range(TB):
                    for half in range(KH):
                        mm = pe.matmul(logit_bank[:, t, :], uT[:, half, t * P:(t + 1) * P], router_sb[:, half, :],
                                       start=(half == 0), stop=(half == KH - 1))
                mm.then_inc(logits_psum, 1)

            pe.wait_ge(pool_const, N_CONST_A)
            pe.wait_ge(matrix_ready, 1)
            pe.wait_ge(router_loaded, 16)
            steps(pe, B, 2, step_a)
            route(B - 2, 0, 0)
            u_transposed(B - 1, 1, 0)
            route(B - 1, 1, 0)
            pe.wait_ge(picked_ready, 1)
            pe.matmul(rank_bank, above[:], picked, start=True, stop=True)
            pe.matmul(total_bank, ones_b[:], picked, start=True, stop=True).then_inc(ranks_ready, 1)
            for g in range(GROUPS):
                pe.wait_ge(is_q_ready, g + 1)
                pe.wait_ge(is_b_ready, 2 * g + 2)
                pe.wait_ge(is_b_tile, g + 1)
                for j in range(GT):
                    mm = pe.matmul(turn_bank, is_q[:, g % 2, j, :], is_b_of[:, g % 2, j],
                                   start=(g == 0 and j == 0), stop=(g == GROUPS - 1 and j == GT - 1))
                mm.then_inc(turned, 1)

            def rows_transposed(n, s, k):
                pe.wait_ge(rows_loaded[s], 16 * (k + 1))
                for half in range(KH):
                    mm = pe.transpose(bank[2 + s % 2][:, half * P:(half + 1) * P],
                                      rows[:, s, half * P:(half + 1) * P], ident[:])
                mm.then_inc(rowT_psum, 1)

            def split_product(acc, hi, lo, w_hi, w_lo, bias, expert, parts):
                pe.matmul(acc, ones2[:], bias, start=True, stop=False)
                for part in range(parts):
                    for left, right in ((hi, w_hi), (lo, w_hi), (hi, w_lo)):
                        mm = pe.matmul(acc, left[:, part, :],
                                       right[:, ds(expert), part, :].rearrange("p e f -> p (e f)"),
                                       start=False, stop=(part == parts - 1 and right is w_lo))
                return mm

            def gate_up(n, s, k, expert):
                d = s % 2
                pe.wait_ge(rowT_lo_ready, n + 1)
                split_product(bank[d][:], rowT_hi[:, d], rowT_lo[:, d], gu_hi, gu_lo,
                              gu_bias[:, :, ds(expert), :].rearrange("r two e i -> r two (e i)"), expert, KH).then_inc(gu_psum, 1)

            def act_transposed(n, s, k):
                d = s % 2
                pe.wait_ge(act_ready, n + 1)
                for half in range(KI):
                    mm = pe.transpose(bank[4 + d][:, half * P:(half + 1) * P],
                                      act[:, d, half * P:(half + 1) * P], ident[:])
                mm.then_inc(actT_psum, 1)

            def down(n, s, k, expert):
                d = s % 2
                pe.wait_ge(actT_lo_ready, n + 1)
                split_product(bank[6 + d][:, 0:H], actT_hi[:, d], actT_lo[:, d], dn_hi, dn_lo,
                              dn_bias[:, ds(expert), :].rearrange("r e h -> r (e h)"), expert, KI).then_inc(down_psum, 1)

            def expert_of(n):
                return pe.value_load(block_expert[0:1, ds(n)], min_val=0, max_val=E - 1)

            experts = {}

            def step_b(n, s, k):
                expert = experts[s] = expert_of(n)
                if (last := earlier(n, s, k, 3, UNROLL)) is not None:
                    down(*last, experts[s - 3] if s >= 3 else expert_of(last[0]))
                if (last := earlier(n, s, k, 2, UNROLL)) is not None:
                    act_transposed(*last)
                if (after := later(n, s, k, UNROLL, NB)) is not None:
                    rows_transposed(*after)
                gate_up(n, s, k, expert)

            pe.wait_ge(experts_ready, 1)
            pe.wait_ge(slots_ready, 2)
            pe.wait_ge(bias_placed, 16 * PLACE_DMAS)
            rows_transposed(0, 0, 0)
            K = steps_peeled(pe, NB, UNROLL, step_b)
            down(NB - 3, UNROLL - 3, K, expert_of(NB - 3))
            act_transposed(NB - 2, UNROLL - 2, K)
            down(NB - 2, UNROLL - 2, K, expert_of(NB - 2))
            act_transposed(NB - 1, UNROLL - 1, K)
            down(NB - 1, UNROLL - 1, K, expert_of(NB - 1))

            def x_transposed(n, s, k):
                pe.wait_ge(mixed, n + 1)
                for half in range(KH):
                    for t in range(TB):
                        mm = pe.transpose(bank[2 * s + half][:, t * P:(t + 1) * P],
                                          mix[:, s, t, half * P:(half + 1) * P], ident[:])
                    mm.then_inc(xT_psum, 1)

            def hide(n, s, k):
                wait_count(pe, hidden_ready, n)
                pe.wait_ge(xT_lo_ready, 2 * n + 2)
                for half in range(KH):
                    for left, right in ((w1_hi, xT_hi), (w1_hi, xT_lo), (w1_lo, xT_hi)):
                        mm = pe.matmul(bank[4 + s][0:A, :], left[:, half, :], right[:, s, half, :],
                                       start=(half == 0 and left is w1_hi and right is xT_hi),
                                       stop=(half == KH - 1 and left is w1_lo))
                mm.then_inc(hidden_psum, 1)

            def score(n, s, k):
                pe.matmul(bank[6 + s][0:1, :], v_sb[:], hidden[:, s], start=True, stop=True).then_inc(score_psum, 1)

            def scores_of(n, s, k):
                x_transposed(n, s, k)
                if (last := earlier(n, s, k, 1, 2)) is not None:
                    hide(*last)
                if (last := earlier(n, s, k, 2, 2)) is not None:
                    score(*last)

            pe.wait_ge(outs_ready, NB)
            pe.wait_ge(w1_split, 2)
            steps(pe, B, 2, scores_of)
            hide(B - 1, 1, 0)
            score(B - 2, 0, 0)
            pe.wait_ge(hidden_ready, B)
            score(B - 1, 1, 0)
            pe.wait_ge(scores_loaded, 16)
            pe.wait_ge(row_ready, B)
            for t in range(TB):
                mm = pe.transpose(bank[0][:, t * B:(t + 1) * B], scores[:, t * P:(t + 1) * P], ident[0:B, 0:B])
            mm.then_inc(col_psum, 1)

            def pool_of(n, s, k):
                if (last := earlier(n, s, k, 3, 2)) is not None:
                    feed_forward(*last)
                pe.wait_ge(probs_lo_ready, TB * (n + 1))
                for j in range(TB):
                    wait_count(pe, pooled_ready, TB * (n - 1) + j + 1)
                    for l in range(TB):
                        for left, right in ((probs_hi, X_hi), (probs_lo, X_hi), (probs_hi, X_lo)):
                            mm = pe.matmul(bank[j][:, 0:H + 2], left[:, s, l, j * P:(j + 1) * P],
                                           right[:, ds(n * TB + l), :].rearrange("p t h -> p (t h)"),
                                           start=(l == 0 and left is probs_hi and right is X_hi),
                                           stop=(l == TB - 1 and right is X_lo))
                    mm.then_inc(pool_psum, 1)
                if (last := earlier(n, s, k, 2, 2)) is not None:
                    quant_transposed(*last)

            def quant_transposed(n, s, k):
                pe.wait_ge(quant_ready, n + 1)
                wait_count(pe, quantT_ready, n)
                qT = bank[4][:].bitcast(BF16)
                for half in range(KH):
                    for t in range(TB):
                        mm = pe.transpose(qT[:, half * S + t * P:half * S + (t + 1) * P],
                                          quant[:, t, half * P:(half + 1) * P], ident_b[:])
                mm.then_inc(quantT_psum, 1)

            def feed_forward(n, s, k):
                pe.wait_ge(quantT_ready, n + 1)
                wait_count(pe, ffn_ready, 2 * n)
                for t in range(TB):
                    for half in range(KH):
                        mm = pe.matmul(bank[5 + t // 2][:, (t % 2) * F:(t % 2 + 1) * F],
                                       quantT[:, half, t * P:(t + 1) * P], k_quant[:, half, :],
                                       start=(half == 0), stop=(half == KH - 1))
                    if t % 2:
                        mm.then_inc(ffn_psum, 1)

            pe.wait_ge(X_lo_ready, B)
            pe.wait_ge(ends_set, 2)
            pe.wait_ge(col_ready, 1)
            pe.wait_ge(table_step, 6)
            pe.wait_ge(tables, 7)
            steps(pe, B, 2, pool_of)
            feed_forward(B - 3, 1, 0)
            for n in (B - 2, B - 1):
                quant_transposed(n, n % 2, 0)
                feed_forward(n, n % 2, 0)

        @block.vector
        def _(dve):
            dve.wait_ge(z_loaded, 48)
            dve.tensor_scalar(zs[:, ZRN, :], zs[:, ZR, :], -1.0, None, ALU.mult).then_inc(z_step, 1)
            dve.scalar_tensor_tensor(out=zs[:, SLOPE, :], in0=zs[:, ZX, :], scalar=-2.0, in1=zs[:, ZR, :],
                                     op0=ALU.mult, op1=ALU.add).then_inc(z_step, 1)
            dve.wait_ge(pool_const, 6)
            dve.tensor_copy(row_f[:], row_i[:]).then_inc(z_step, 1)
            dve.tensor_copy(expert_f[:], column_i[:, 0:E]).then_inc(z_step, 1)
            dve.tensor_copy(blk_f[:], blk_i[:]).then_inc(z_step, 1)
            dve.wait_ge(z_step, 5)
            dve.tensor_scalar(row_one[:], row_f[:], 1.0, None, ALU.add).then_inc(z_step, 1)
            dve.tensor_copy(column[:], column_i[:]).then_inc(z_step, 1)
            dve.tensor_copy(tile_no[:], slot_i[:, 2].rearrange("p c t -> p (c t)")).then_inc(z_step, 1)
            dve.memset(ones2[:].bitcast(F32), 1.0).then_inc(z_step, 1)
            dve.wait_ge(z_step, N_Z)
            dve.wait_ge(diff_step, DIFF_STEPS)
            dve.tensor_copy(diff[:], diff_f).then_inc(matrix_ready, 1)
            dve.wait_ge(pool_const, N_CONST_A)
            dve.wait_ge(bias_loaded, 16 * BIAS_DMAS)
            dve.tensor_scalar(raw_gb[:, 1:E * GU // P:2], raw_gb[:, 1:E * GU // P:2], 1.0, None,
                              ALU.add).then_inc(bias_step, 1)
            dve.tensor_copy(flat_db[:, 0, :], raw_db[:]).then_inc(bias_step, 1)
            dve.wait_ge(bias_step, 2)
            mixed_gb = raw_gb[:].rearrange("p (i two) -> p two i", two=2)
            flat = lambda i: flat_gb[:, i, :].rearrange("p (two i) -> p two i", two=2)
            dve.tensor_copy(flat(0), mixed_gb).then_inc(bias_step, 1)
            dve.tensor_tensor(flat_db[:, 1, :], raw_db[:], flat_db[:, 0, :].bitcast(F32),
                              ALU.subtract).then_inc(bias_step, 1)
            dve.wait_ge(bias_step, 4)
            dve.tensor_tensor(flat(1), mixed_gb, flat(0).bitcast(F32), ALU.subtract).then_inc(bias_step, 1)

            def step_a(n, s, k):
                u = flow[:, s]
                dve.wait_ge(flow_ready, n + 1)
                dve.tensor_tensor(u, u, X[:, ds(n * TB, TB), 0:H], ALU.mult).then_inc(flow_step, 1)
                dve.wait_ge(pair_ready, 2 * n + 2)
                dve.wait_ge(flow_step, 2 * n + 1)
                dve.scalar_tensor_tensor(out=u, in0=pair[:], scalar=zs[:, ZX, ds(n)], in1=u, op0=ALU.mult,
                                         op1=ALU.add).then_inc(flow_step, 1)
                dve.wait_ge(flow_step, 2 * n + 2)
                dve.wait_ge(lap_ready, 2 * n + 2)
                for g in range(2):
                    ug = u[:, 2 * g:2 * g + 2, :]
                    op = dve.scalar_tensor_tensor(out=ug, in0=lap[s][g][:].rearrange("p (t h) -> p t h", h=H),
                                                  scalar=zs[:, ZY, ds(n)], in1=ug, op0=ALU.mult, op1=ALU.add)
                op.then_inc(u_ready, 1)
                dve.wait_ge(hi_ready, 2 * n + 2)
                dve.tensor_tensor(gu_lo[:, ds(n)].rearrange("p e k (two i) -> p (e k) two i", two=2),
                                  raw_gu[:, s].rearrange("p k (i two) -> p k two i", two=2),
                                  gu_hi[:, ds(n)].bitcast(F32).rearrange("p e k (two i) -> p (e k) two i", two=2),
                                  ALU.subtract).then_inc(gu_used, 1)
                if (last := earlier(n, s, k, 2, 2)) is not None:
                    best_two(*last)

            def best_two(n, s, k):
                dve.wait_ge(logits_psum, n + 1)
                dve.tensor_copy(logits[:], logit_bank).then_inc(logits_ready, 1)
                wait_alone(dve, logits_ready, n + 1, z_step, N_Z)
                for t in range(TB):
                    op = dve.max(best[:, t], logits[:, t])
                op.then_inc(best_step, 1)
                wait_alone(dve, best_step, n + 1, z_step, N_Z)
                for t in range(TB):
                    op = dve.max_index(best_i[:, t], best[:, t], logits[:, t])
                op.then_inc(index_step, 1)
                dve.wait_ge(index_step, n + 1)
                dve.tensor_copy(top[:, ds(n * TB, TB), :], best[:, :, 0:2]).then_inc(top_ready, 1)
                dve.tensor_copy(top_i[:, ds(n * TB, TB), :], best_i[:, :, 0:2]).then_inc(top_ready, 1)

            K = steps_peeled(dve, B, 2, step_a)
            best_two(B - 2, 0, K)
            best_two(B - 1, 1, K)

            done = [0]

            def then(instruction):
                done[0] += 1
                instruction.then_inc(route_step, 1)
                dve.wait_ge(route_step, done[0])

            dve.wait_ge(top_ready, 2 * B)
            dve.wait_ge(gu_used, B)
            dve.memset(follow[:, :, 0:1], 0.0)
            dve.memset(follow[:, :, 1:NT], 1.0)
            dve.tensor_tensor(odds[:, 0], top[:, :, 1], top[:, :, 0], ALU.subtract).then_inc(gap_ready, 1)
            for c in range(2):
                op = dve.tensor_tensor(pick[:, c], expert_f[:].unsqueeze(2).broadcast_to([P, E, NT]),
                                       top_i[:, :, c].unsqueeze(1).broadcast_to([P, E, NT]), ALU.is_equal)
            then(op)
            dve.tensor_tensor(picked, pick[:, 0], pick[:, 1], ALU.add).then_inc(picked_ready, 1)
            dve.wait_ge(ranks_ready, 1)
            then(dve.tensor_copy(totals, total_bank))
            flat = lambda m: m[:].rearrange("p e t -> p (e t)")
            then(dve.tensor_tensor_scan(flat(upto), flat(follow), flat(totals), 0.0, ALU.mult, ALU.add))
            COUNT, PADDED, END, FILLED, ONE = range(5)
            ends_of = lambda i: ends[:, i, :]
            dve.tensor_copy(ends_of(COUNT), upto[:, :, NT - 1])
            then(dve.memset(ends_of(ONE), 1.0))
            then(dve.tensor_scalar(ends_i[:, 0, :], ends_of(COUNT), float(P - 1), None, ALU.add))
            then(dve.tensor_scalar(ends_i[:, 1, :], ends_i[:, 0, :], 7, 7, ALU.logical_shift_right,
                                   ALU.logical_shift_left))
            then(dve.tensor_copy(ends_of(PADDED), ends_i[:, 1, :]))
            then(dve.tensor_tensor_scan(ends_of(END), ends_of(ONE), ends_of(PADDED), 0.0, ALU.mult, ALU.add))
            then(dve.tensor_tensor(ends_of(PADDED), ends_of(END), ends_of(PADDED), ALU.subtract))
            then(dve.tensor_tensor(ends_of(FILLED), ends_of(PADDED), ends_of(COUNT), ALU.add))
            then(dve.tensor_tensor(upto, upto, totals, ALU.subtract))
            then(dve.tensor_tensor(upto, upto, rank_bank, ALU.add))
            then(dve.tensor_tensor(upto, upto, ends_of(PADDED).unsqueeze(2).broadcast_to([P, E, NT]),
                                   ALU.add))
            for c in range(2):
                op = dve.tensor_tensor(pick[:, c], pick[:, c], upto, ALU.mult)
            then(op)
            for c in range(2):
                op = dve.tensor_reduce(slot_f[:, c, :], pick[:, c].rearrange("p e t -> p t e"), AX.X, ALU.add)
            then(op)
            then(dve.tensor_copy(slot_i[:, 0], slot_f[:]))
            dve.tensor_scalar(slot_i[:, 1], slot_i[:, 0], P - 1, None, ALU.bitwise_and)
            then(dve.tensor_scalar(slot_i[:, 2], slot_i[:, 0], 7, None, ALU.logical_shift_right))
            dve.tensor_copy(slot_q[:], slot_i[:, 1])
            then(dve.tensor_copy(slot_b[:], slot_i[:, 2]))
            for s in range(2):
                dve.wait_ge(u_kept[s], 16 * (B // 2))
            q_all, b_all = (m[:].rearrange("p c t -> p (c t)") for m in (slot_q, slot_b))
            for g in range(GROUPS):
                d, tiles = g % 2, slice(g * GT, (g + 1) * GT)
                wait_count(dve, turned, g - 1)
                dve.tensor_tensor(is_b[:, d], column[:, 0:NB].unsqueeze(1).broadcast_to([P, GT, NB]),
                                  b_all[:, tiles].unsqueeze(2).broadcast_to([P, GT, NB]),
                                  ALU.is_equal).then_inc(is_b_ready, 1)
                dve.tensor_tensor(is_q[:, d], column[:].unsqueeze(1).broadcast_to([P, GT, P]),
                                  q_all[:, tiles].unsqueeze(2).broadcast_to([P, GT, P]),
                                  ALU.is_equal).then_inc(is_q_ready, 1)
                dve.wait_ge(is_b_ready, 2 * g + 1)
                dve.tensor_scalar(is_b_of[:, d, :, 0, :], is_b[:, d], row_one[:, 0:1], None,
                                  ALU.mult).then_inc(is_b_ready, 1)
            then(dve.tensor_tensor(blk_past, blk_f[:].unsqueeze(2).broadcast_to([1, NB, E]),
                                   ends[0:1, END, :].unsqueeze(1).broadcast_to([1, NB, E]), ALU.is_ge))
            then(dve.tensor_reduce(blk_e[:], blk_past, AX.X, ALU.add))
            dve.tensor_scalar(block_expert[:], blk_e[:], float(E - 1), None, ALU.min).then_inc(experts_ready, 1)
            NUMBER, OUTSIDE, SECOND, ROW = range(4)
            dve.wait_ge(turned, GROUPS)
            then(dve.tensor_copy(pair_no[:, ROW], turn_bank[:, 0, :]))
            then(dve.scalar_tensor_tensor(out=pair_no[:, NUMBER], in0=turn_bank[:, 1, :], scalar=float(P),
                                          in1=pair_no[:, ROW], op0=ALU.mult, op1=ALU.add))
            dve.tensor_scalar(pair_no[:, OUTSIDE], pair_no[:, NUMBER], 1.0, ROW_BIG, ALU.is_lt, ALU.mult)
            then(dve.tensor_scalar(pair_no[:, SECOND], pair_no[:, NUMBER], float(T) + 0.5, -float(T),
                                   ALU.is_gt, ALU.mult))
            dve.scalar_tensor_tensor(out=slot_dst[:], in0=pair_no[:, NUMBER], scalar=-1.0,
                                     in1=pair_no[:, OUTSIDE], op0=ALU.add,
                                     op1=ALU.add).then_inc(slots_ready, 1)
            then(dve.scalar_tensor_tensor(out=pair_no[:, ROW], in0=pair_no[:, NUMBER], scalar=-1.0,
                                          in1=pair_no[:, SECOND], op0=ALU.add, op1=ALU.add))
            dve.tensor_scalar(slot_src[:], pair_no[:, ROW], 0.0, None, ALU.max).then_inc(slots_ready, 1)
            dve.wait_ge(odds_ready, 1)
            then(dve.tensor_scalar(odds[:, 2], odds[:, 1], 1.0, None, ALU.add))
            then(dve.reciprocal(tok_w[:, 0, :], odds[:, 2]))
            then(dve.tensor_tensor(tok_w[:, 1, :], odds[:, 1], tok_w[:, 0, :], ALU.mult))

            def rows_low(n, s, k):
                d = s % 2
                dve.wait_ge(rowT_hi_ready, n + 1)
                dve.tensor_tensor(rowT_lo[:, d], bank[2 + d][:, 0:KH * P].rearrange("p (k n) -> p k n", k=KH),
                                  rowT_hi[:, d].bitcast(F32), ALU.subtract).then_inc(rowT_lo_ready, 1)

            def step_b(n, s, k):
                if (last := earlier(n, s, k, 2, UNROLL)) is not None:
                    act_low(*last)
                if (after := later(n, s, k, UNROLL, NB)) is not None:
                    rows_low(*after)
                if (last := earlier(n, s, k, 1, UNROLL)) is not None:
                    activated(*last)
                clip(n, s, k)

            def clip(n, s, k):
                d = s % 2
                dve.wait_ge(gu_psum, n + 1)
                dve.tensor_scalar(gate[:, d], bank[d][:, 0:I], LIMIT, 0.5, ALU.min,
                                  ALU.mult).then_inc(gate_ready, 1)
                dve.tensor_scalar(up[:, d], bank[d][:, I:GU], LIMIT + 1.0, 1.0 - LIMIT, ALU.min,
                                  ALU.max).then_inc(up_ready, 1)
                dve.wait_ge(up_ready, n + 1)
                dve.tensor_tensor(glu[:, d], gate[:, d], up[:, d], ALU.mult).then_inc(glu_ready, 1)

            def activated(n, s, k):
                d = s % 2
                dve.wait_ge(tanh_ready, n + 1)
                dve.wait_ge(glu_ready, n + 1)
                dve.scalar_tensor_tensor(out=act[:, d], in0=tanh[:, d], scalar=1.0, in1=glu[:, d],
                                         op0=ALU.add, op1=ALU.mult).then_inc(act_ready, 1)

            def act_low(n, s, k):
                d = s % 2
                dve.wait_ge(actT_hi_ready, n + 1)
                dve.tensor_tensor(actT_lo[:, d], bank[4 + d][:, 0:KI * P].rearrange("p (k n) -> p k n", k=KI),
                                  actT_hi[:, d].bitcast(F32), ALU.subtract).then_inc(actT_lo_ready, 1)

            rows_low(0, 0, 0)
            K = steps_peeled(dve, NB, UNROLL, step_b)
            act_low(NB - 2, UNROLL - 2, K)
            activated(NB - 1, UNROLL - 1, K)
            act_low(NB - 1, UNROLL - 1, K)

            dve.wait_ge(w1_split, 1)
            dve.tensor_tensor(w1_lo[:], w1_sb[:], w1_hi[:].bitcast(F32), ALU.subtract).then_inc(w1_split, 1)

            def mix_of(n, s, k):
                if not (isinstance(n, int) and n < 2):
                    dve.wait_ge(mixed_kept[s], 16 * k)
                    dve.wait_ge(X_lo_ready, n - 1)
                for c in range(2):
                    dve.wait_ge(y_loaded[c][s], 16 * (k + 1))
                    for t in range(TB):
                        last_sum = X[:, ds(n * TB + t), 0:H].rearrange("p t h -> p (t h)") if c == 0 else mix[:, s, t, :]
                        op = dve.scalar_tensor_tensor(out=mix[:, s, t, :], in0=picks[:, s, c, t, :],
                                                      scalar=tok_w[:, c, ds(n * TB + t)], in1=last_sum,
                                                      op0=ALU.mult, op1=ALU.add)
                    if c == 0:
                        op.then_inc(mix_step, 1)
                        dve.wait_ge(mix_step, n + 1)
                op.then_inc(mixed, 1)
                if (last := earlier(n, s, k, 1, 2)) is not None:
                    xT_low(*last)

            def xT_low(n, s, k):
                for half in range(KH):
                    dve.wait_ge(xT_hi_ready, 2 * n + half + 1)
                    dve.tensor_tensor(xT_lo[:, s, half], bank[2 * s + half][:],
                                      xT_hi[:, s, half].bitcast(F32), ALU.subtract).then_inc(xT_lo_ready, 1)

            steps(dve, B, 2, mix_of)
            xT_low(B - 1, 1, B // 2 - 1)

            tdone = [0]

            def table(instruction):
                tdone[0] += 1
                instruction.then_inc(table_step, 1)
                dve.wait_ge(table_step, tdone[0])

            dve.wait_ge(c_loaded, 16 * C_DMAS)
            dve.wait_ge(tables, 7)
            table(dve.reciprocal(scales[:, 3:5], scales[:, 0:2]))
            table(dve.tensor_scalar(k_scaled[:], k_raw[:], scales[:, 4:5], None, ALU.mult))
            table(dve.tensor_scalar(k_grid[:].bitcast(I32), k_scaled[:].bitcast(I32), EXPONENT_BITS, None,
                                    ALU.bitwise_and))
            table(dve.tensor_scalar(k_grid[:], k_grid[:], FP8_LEAST_NORMAL, FP8_GRID, ALU.max, ALU.mult))
            table(dve.tensor_tensor(k_scaled[:], k_scaled[:], k_grid[:], ALU.add))
            table(dve.tensor_tensor(k_quant[:], k_scaled[:], k_grid[:], ALU.subtract))
            table(dve.tensor_tensor(scales[:, 2:3], scales[:, 0:1], scales[:, 1:2], ALU.mult))
            table(dve.tensor_copy(counts[:, 0, :], counts_i[:]))
            table(dve.tensor_scalar(counts[:, 1, :], counts[:, 0, :], -1.0, float(S + 1), ALU.mult, ALU.add))
            dve.memset(counts[:, 2, :], float(S - 1))
            table(dve.tensor_copy(kind_row[:, 0, :], kind_row_i[:, 0, :]))
            table(dve.reciprocal(counts[:], counts[:]))
            dve.tensor_scalar(kind_row[:, 1, :], kind_row[:, 0, :], 0.0, -2.0, ALU.is_equal, ALU.mult)
            table(dve.tensor_scalar(kind_row[:, 2, :], kind_row[:, 0, :], 1.0, None, ALU.is_equal))
            table(dve.tensor_tensor(kind_row[:, 1, :], kind_row[:, 1, :], kind_row[:, 2, :], ALU.subtract))
            table(dve.tensor_scalar(kind_row_i[:, 1, :], kind_row[:, 1, :], 2.0, None, ALU.add))
            table(dve.tensor_copy(kind_of[:, 0:1], kind_i[:]))
            dve.tensor_scalar(kind_of[:, 1:2], kind_of[:, 0:1], 0.0, NEG, ALU.not_equal, ALU.mult)
            dve.tensor_scalar(kind_of[:, 2:3], kind_of[:, 0:1], 1.0, NEG, ALU.not_equal, ALU.mult)
            dve.tensor_scalar(kind_of[:, 4:5], kind_of[:, 0:1], 1.0, None, ALU.is_equal)
            table(dve.tensor_scalar(kind_of[:, 5:6], kind_of[:, 0:1], 0.0, None, ALU.is_equal))
            table(dve.tensor_tensor(kind_of[:, 4:5], kind_of[:, 4:5], kind_of[:, 5:6], ALU.add))
            table(dve.tensor_scalar(kind_of[:, 3:4], kind_of[:, 4:5], NEG, None, ALU.mult))

            mdone = [0]

            def stat(instruction):
                mdone[0] += 1
                instruction.then_inc(max_step, 1)
                dve.wait_ge(max_step, mdone[0])

            dve.wait_ge(scores_loaded, 16)
            LOWEST = -3.0e38
            stat(dve.tensor_tensor_scan(from_left[:], scores[:], scores[:], LOWEST, ALU.max, ALU.max))
            stat(dve.tensor_tensor_scan(from_right[:, ::-1], scores[:, ::-1], scores[:, ::-1], LOWEST,
                                        ALU.max, ALU.max))
            dve.tensor_tensor(around[:, 1:S - 1], from_left[:, 0:S - 2], from_right[:, 2:S], ALU.max)
            dve.tensor_copy(around[:, 0:1], from_right[:, 1:2])
            dve.tensor_copy(around[:, S - 1:S], from_left[:, S - 2:S - 1])
            stat(dve.tensor_scalar(row_max[:], from_left[:], kind_of[:, 1:2], None, ALU.add))
            stat(dve.scalar_tensor_tensor(out=row_max[:], in0=from_right[:], scalar=kind_of[:, 2:3],
                                          in1=row_max[:], op0=ALU.add, op1=ALU.max))
            stat(dve.scalar_tensor_tensor(out=row_max[:], in0=around[:], scalar=kind_of[:, 3:4],
                                          in1=row_max[:], op0=ALU.add, op1=ALU.max))
            dve.tensor_scalar(row_max[:], row_max[:], -1.0, None, ALU.mult).then_inc(max_ready, 1)

            def exponent(n, s, k, kind, l):
                lo = S - P - P * l
                wait_count(dve, probs_ready, TB * n + l - 1)
                dve.tensor_tensor(expo[:, l % 2], neg_max[:, s, :],
                                  masks[:, ds(kind), lo:lo + S].rearrange("p m s -> p (m s)"),
                                  ALU.add).then_inc(expo_ready, 1)

            def probs_low(n, s, l):
                dve.wait_ge(probs_ready, TB * n + l + 1)
                dve.tensor_tensor(probs_lo[:, s, l], probs[:, l % 2], probs_hi[:, s, l].bitcast(F32),
                                  ALU.subtract).then_inc(probs_lo_ready, 1)

            def scale_up(n, s, k):
                dve.wait_ge(pooled_ready, TB * (n + 1))
                wait_count(dve, quant_ready, n)
                dve.tensor_scalar(scaled[:], pooled[:], scales[:, 3:4], None,
                                  ALU.mult).then_inc(scaled_ready, 1)

            def exponent_bits(n, s, k):
                dve.wait_ge(scaled_ready, n + 1)
                dve.tensor_scalar(grid[:].bitcast(I32), scaled[:].bitcast(I32), EXPONENT_BITS, None,
                                  ALU.bitwise_and).then_inc(bits_ready, 1)

            def rounding(n, s, k):
                dve.wait_ge(bits_ready, n + 1)
                dve.tensor_scalar(grid[:], grid[:], FP8_LEAST_NORMAL, FP8_GRID, ALU.max,
                                  ALU.mult).then_inc(grid_ready, 1)

            def step_c(n, s, k, after):
                between = [[], [], [], []]
                if (last := earlier(n, s, k, 1, 2)) is not None:
                    between[0] = [(scale_up, last)]
                    between[1] = [(exponent_bits, last)]
                    between[2] = [(rounding, last)]
                if after is not None:
                    kind = dve.value_load(kind_row_i[0:1, 1, ds(after[0])], min_val=0, max_val=2)
                    dve.wait_ge(max_loaded[after[1]], 16 * (after[2] + 1))
                    exponent(*after, kind, 0)
                for l in range(TB):
                    if after is not None and l + 1 < TB:
                        exponent(*after, kind, l + 1)
                    for what, batch in between[l]:
                        what(*batch)
                    if after is not None:
                        probs_low(after[0], after[1], l)
                pooled_rows(n, s, k)
                if (last := earlier(n, s, k, 3, 2)) is not None:
                    add_bias(*last)

            def pooled_rows(n, s, k):
                kind = dve.value_load(kind_row_i[0:1, 1, ds(n)], min_val=0, max_val=2)
                for j in range(TB):
                    dve.wait_ge(pool_psum, TB * n + j + 1)
                    op = dve.reciprocal(norm[:, j:j + 1], bank[j][:, H:H + 1])
                op.then_inc(norm_ready, 1)
                dve.wait_ge(norm_ready, n + 1)
                for j in range(TB):
                    dve.tensor_scalar(pooled[:, j, :], bank[j][:, 0:H], norm[:, j:j + 1],
                                      counts[:, ds(kind), j], ALU.mult, ALU.mult).then_inc(pooled_ready, 1)

            def add_bias(n, s, k):
                dve.wait_ge(ffn_ready, 2 * n + 2)
                wait_count(dve, result_ready, n)
                dve.tensor_tensor(ffn_sum[:], ffn[:, s], bias_f[:].unsqueeze(1).broadcast_to([P, TB, F]),
                                  ALU.add).then_inc(ffn_sum_ready, 1)

            dve.wait_ge(X_lo_ready, B)
            kind = dve.value_load(kind_row_i[0:1, 1, ds(0)], min_val=0, max_val=2)
            dve.wait_ge(max_loaded[0], 16)
            exponent(0, 0, 0, kind, 0)
            for l in range(TB):
                if l + 1 < TB:
                    exponent(0, 0, 0, kind, l + 1)
                probs_low(0, 0, l)
            K = steps_peeled(dve, B, 2, lambda n, s, k: step_c(n, s, k, later(n, s, k, 2, B)))
            for what in (scale_up, exponent_bits, rounding):
                what(B - 1, 1, K)
            for n in range(B - 3, B):
                add_bias(n, n % 2, K)


_INS = ["x", "condB_zX", "condB_zY", "condB_zR", "itok_B_0_2", "L0_ffn_router_weight", "L0_ffn_gate_up_proj",
        "L0_ffn_gate_up_proj_bias", "L0_ffn_down_proj", "L0_ffn_down_proj_bias", "L1_cond_W1", "L1_cond_b1",
        "L1_cond_v", "L1_ffn_kernel", "L1_ffn_input_scale", "L1_ffn_kernel_scale", "L1_ffn_bias"]


def kernel(**inputs):
    import numpy as np
    import concourse.bacc as bacc
    from concourse.bass_utils import run_bass_kernel_spmd

    nc = bacc.Bacc("TRN2", target_bir_lowering=False, num_devices=1)
    arrays, args = {}, []
    for name in _INS:
        a = np.ascontiguousarray(inputs[name])
        arrays[f"in_{name}"] = a
        args.append(nc.dram_tensor(f"in_{name}", a.shape, mybir.dt.from_np(a.dtype), kind="ExternalInput").ap())
    args.append(nc.dram_tensor("out_0", inputs["x"].shape, F32, kind="ExternalOutput").ap())
    adaln_ffn_kernel(nc, *args)
    r = run_bass_kernel_spmd(nc, [arrays], core_ids=[0])
    return r.results[0]["out_0"]
```
